# Optimizing a Trainium2 kernel written in Bass

```python
import numpy as np
import jax
import jax.numpy as jnp

def _softmax(x, axis=-1):
    return jax.nn.softmax(x, axis=axis)

def _gelu(x):
    return jax.nn.gelu(x, approximate=True)

def _silu(x):
    return jax.nn.silu(x)

def _sigmoid(x):
    return jax.nn.sigmoid(x)

def _layernorm(x, axis=-1, eps=1e-05):
    m = jnp.mean(x, axis=axis, keepdims=True)
    v = jnp.var(x, axis=axis, keepdims=True)
    return (x - m) / jnp.sqrt(v + eps)

def _scatter_add(tgt, idx, src, axis=0):
    return tgt.at[idx].add(src)

def _segment_sum(src, seg, n):
    return jax.ops.segment_sum(src, seg, n)
kernel_name = 'mk_gnn_ffn_d1_gnn_r8_43dfc2'

def setup_inputs(seed: int=0):
    np.random.seed(seed)
    _w = jnp.asarray

    def _rec_inputs():
        import jax
        import jax.numpy as jnp
        _gk = jax.random.key(seed)
        x = -0.0002117 + 1 * jax.random.normal(jax.random.fold_in(_gk, 1), (12500, 256), jnp.float32)
        _s = jax.random.randint(jax.random.fold_in(_gk, 2), (100000,), 0, 12500, jnp.int32)
        _d = jax.random.randint(jax.random.fold_in(_gk, 3), (100000,), 0, 12500, jnp.int32)
        _loop = jnp.arange(12500, dtype=jnp.int32)
        src = jnp.concatenate([_s, _d, _loop])
        dst = jnp.concatenate([_d, _s, _loop])
        _o = jnp.argsort(dst, stable=True)
        src = src[_o]
        dst = dst[_o]
        edge_weight = jax.random.uniform(jax.random.fold_in(_gk, 12), (212500,), jnp.float32, 0.0, 1)
        return (x, src, dst, edge_weight)
    x, src, dst, edge_weight = _rec_inputs()

    def _L0_gnn_setup():
        import jax, jax.numpy as jnp
        import numpy as np
        N_NODES = 12500
        N_EDGES = 400000
        IN_F = 256
        OUT_F = 256
        key = jax.random.key(seed)
        k1, k2, k3, k4, k5, k6 = jax.random.split(key, 6)
        H = jax.random.normal(k1, (N_NODES, IN_F), dtype=jnp.float32)
        row = jax.random.randint(k2, (N_EDGES,), 0, N_NODES)
        col = jax.random.randint(k3, (N_EDGES,), 0, N_NODES)
        edge_index = jnp.stack([row, col], axis=0)
        edge_vals = jax.random.uniform(k4, (N_EDGES,), dtype=jnp.float32)
        stdv = 1.0 / np.sqrt(OUT_F)
        W = jax.random.uniform(k5, (IN_F, OUT_F), dtype=jnp.float32, minval=-stdv, maxval=stdv)
        b = jax.random.uniform(k6, (OUT_F,), dtype=jnp.float32, minval=-stdv, maxval=stdv)
        return {'H': H, 'edge_index': edge_index, 'edge_vals': edge_vals, 'W': W, 'b': b}
    _L0_gnn_all = _L0_gnn_setup()
    _L0_gnn_in = {k: v for k, v in _L0_gnn_all.items() if k in ('W', 'b')}
    del _L0_gnn_all

    def _L0_ffn_setup():
        import jax, jax.numpy as jnp
        import numpy as np
        E = 8
        K = 2
        D = 256
        H = 512
        DOUT = 256
        EPS = 1e-05
        key = jax.random.key(seed)
        ks = jax.random.split(key, 9)
        s = 0.02
        return {'x': jax.random.normal(ks[0], (4, 1024, D), jnp.float32), 'gamma': 1.0 + 0.05 * jax.random.normal(ks[1], (D,), jnp.float32), 'beta': 0.05 * jax.random.normal(ks[2], (D,), jnp.float32), 'Wr': 0.01 * jax.random.normal(ks[3], (D, E), jnp.float32), 'br': jnp.zeros((E,), jnp.float32), 'W1': s * jax.random.normal(ks[4], (E, D, H), jnp.float32), 'b1': s * jax.random.normal(ks[5], (E, H), jnp.float32), 'W2': s * jax.random.normal(ks[6], (E, H, DOUT), jnp.float32), 'b2': s * jax.random.normal(ks[7], (E, DOUT), jnp.float32)}
    _L0_ffn_all = _L0_ffn_setup()
    _L0_ffn_in = {k: v for k, v in _L0_ffn_all.items() if k in ('gamma', 'beta', 'Wr', 'br', 'W1', 'b1', 'W2', 'b2')}
    del _L0_ffn_all
    return {'x': x, 'src': src, 'dst': dst, 'edge_weight': edge_weight, 'L0_gnn_W': _L0_gnn_in['W'], 'L0_gnn_b': _L0_gnn_in['b'], 'L0_ffn_gamma': _L0_ffn_in['gamma'], 'L0_ffn_beta': _L0_ffn_in['beta'], 'L0_ffn_Wr': _L0_ffn_in['Wr'], 'L0_ffn_br': _L0_ffn_in['br'], 'L0_ffn_W1': _L0_ffn_in['W1'], 'L0_ffn_b1': _L0_ffn_in['b1'], 'L0_ffn_W2': _L0_ffn_in['W2'], 'L0_ffn_b2': _L0_ffn_in['b2']}

def reference(x, src, dst, edge_weight, L0_gnn_W, L0_gnn_b, L0_ffn_gamma, L0_ffn_beta, L0_ffn_Wr, L0_ffn_br, L0_ffn_W1, L0_ffn_b1, L0_ffn_W2, L0_ffn_b2):
    import jax
    import jax.numpy as jnp

    def _L0_gnn_ref(H, edge_index, edge_vals, W, b):
        import jax, jax.numpy as jnp
        import numpy as np
        N_NODES = 12500
        N_EDGES = 400000
        IN_F = 256
        OUT_F = 256
        HW = H @ W
        row, col = (edge_index[0], edge_index[1])
        msgs = edge_vals[:, None] * HW[col]
        AHW = jax.ops.segment_sum(msgs, row, num_segments=N_NODES)
        return AHW + b

    def _L0_ffn_ref(x, gamma, beta, Wr, br, W1, b1, W2, b2):
        import jax, jax.numpy as jnp
        import numpy as np
        E = 8
        K = 2
        D = 256
        H = 512
        DOUT = 256
        EPS = 1e-05
        mu = jnp.mean(x, axis=-1, keepdims=True)
        var = jnp.mean(jnp.square(x - mu), axis=-1, keepdims=True)
        xn = (x - mu) * jax.lax.rsqrt(var + EPS) * gamma + beta
        logits = jnp.einsum('bsd,de->bse', xn, Wr) + br
        top_vals, top_idx = jax.lax.top_k(logits, K)
        w = jax.nn.softmax(top_vals, axis=-1)
        w_full = jnp.einsum('bsk,bske->bse', w, jax.nn.one_hot(top_idx, E, dtype=w.dtype))
        y = jnp.zeros(x.shape[:-1] + (DOUT,), x.dtype)
        for e in range(E):
            h = jax.nn.gelu(jnp.einsum('bsd,dh->bsh', xn, W1[e]) + b1[e], approximate=False)
            y_e = jnp.einsum('bsh,hd->bsd', h, W2[e]) + b2[e]
            y = y + y_e * w_full[..., e, None]
        return y
    edge_index = jnp.stack([src, dst])
    x = x + _L0_gnn_ref(_layernorm(x, axis=-1), edge_index, edge_weight, L0_gnn_W, L0_gnn_b)
    x = x + _L0_ffn_ref(_layernorm(x, axis=-1)[None], L0_ffn_gamma, L0_ffn_beta, L0_ffn_Wr, L0_ffn_br, L0_ffn_W1, L0_ffn_b1, L0_ffn_W2, L0_ffn_b2)[0]
    return x

_drawn_inputs = setup_inputs


def setup_inputs(seed=0):
    import zlib

    import numpy as np

    out = dict(_drawn_inputs(seed))
    spreads = {'L0_ffn_br': (0.0, 0.1)}
    factors = {'L0_ffn_gamma': 8.0, 'L0_ffn_beta': 8.0, 'L0_ffn_b1': 8.0, 'L0_ffn_b2': 7.197}
    for name, (base, spread) in spreads.items():
        noise = np.random.default_rng([zlib.crc32(name.encode()), seed]).standard_normal(out[name].shape)
        drawn = base * np.exp(spread * noise) if base else spread * noise
        out[name] = jnp.asarray(drawn.astype(out[name].dtype))
    for name, factor in factors.items():
        out[name] = (out[name] * factor).astype(out[name].dtype)
    return out
```

```python
import concourse.bass as bass
from concourse import mybir
from contextlib import ExitStack

f32 = mybir.dt.float32
bf16 = mybir.dt.bfloat16
i32 = mybir.dt.int32
ALU = mybir.AluOpType
ACT = mybir.ActivationFunctionType
AX = mybir.AxisListType


class Steps:

    def __init__(self, engine, semaphore):
        self.engine, self.semaphore = engine, semaphore
        self.before, self.base, self.n = 0, 0, 0

    def __call__(self, instruction, held=None):
        self.n += 1
        instruction.then_inc(self.semaphore, 1)
        self.engine.wait_ge(self.semaphore, self.base + self.n)
        if held is not None:
            self.engine.sem_inc(held, 1)

    def enter(self, i, first, per_round):
        self.before, self.base, self.n, self.per_round = self.before + self.n, 0, 0, per_round
        self.base = (i - first) * per_round + self.before

    def leave(self, rounds):
        assert self.n == self.per_round, (self.n, self.per_round)
        self.before, self.base, self.n = self.before + rounds * self.per_round, 0, 0
        self.base = self.before
        self.before = self.before

    def straight(self):
        self.base = self.before


def ceil_div(a, b):
    return -(-a // b)


def gnn_moe(nc, x, src, dst, edge_weight, gnn_W, gnn_b, gamma, beta, Wr, br, W1, b1_cols, W2, b2, out):
    P = 128
    N, D = x.shape
    E_EDGES = src.shape[0]
    NE, _, H = W1.shape
    KD, KH = D // P, H // P
    EPS = 1e-5

    TILES = ceil_div(N, P)
    LAST = N - (TILES - 1) * P
    R0 = 125
    T0 = 4
    ROUNDS0 = N // (R0 * T0)
    COLS = E_EDGES // P
    TAIL = E_EDGES - COLS * P
    BC = 20
    PAIRS_A = ceil_div(COLS + 1, 2 * BC)
    EC = PAIRS_A * 2 * BC
    assert COLS == EC - 2 * BC + BC and 0 < TAIL < P
    NOBUCKET = 127
    GC = 16
    PAIRS_B = ceil_div((E_EDGES + TILES * (P - 1)) // P, 2 * GC)
    CH = PAIRS_B * 2 * GC
    F = 3
    GT = 256
    GROUPS = (2 * N + NE * (GT - 1)) // GT
    PAIRS_D = ceil_div(GROUPS, 2)
    GROUPS = 2 * PAIRS_D
    SLOTS = GROUPS * GT
    TG = 7
    PAIRS_E = TILES // (2 * TG)
    assert PAIRS_E * 2 * TG == TILES
    KT = 2 * TILES

    ctx = ExitStack()
    with ctx:
        def sb(name, shape, dt=f32):
            return ctx.enter_context(nc.sbuf_tensor(name, shape, dt))

        def sem(name):
            return ctx.enter_context(nc.semaphore(name))

        features = nc.dram_tensor("features", [N + 1, D], f32, kind="Internal").ap()
        records = nc.dram_tensor("records", [P * CH, F], f32, kind="Internal").ap()
        tokens = nc.dram_tensor("tokens", [TILES * P, D], f32, kind="Internal").ap()
        expert_in = nc.dram_tensor("expert_in", [SLOTS, D], f32, kind="Internal").ap()
        expert_out = nc.dram_tensor("expert_out", [SLOTS, D], f32, kind="Internal").ap()

        acc = sb("acc", [P, TILES, D])
        ident = sb("ident", [P, P])
        lower = sb("lower", [P, P])
        ones = sb("ones", [P, P])
        iota_row = sb("iota_row", [P, P])
        iota_bf = sb("iota_bf", [P, P], bf16)
        zeros = sb("zeros", [P, D])
        Wg = sb("Wg", [P, KD, D])
        Wr_sb = sb("Wr_sb", [P, KD, NE])
        rows = sb("rows", [P, 3, D])
        br_row = sb("br_row", [P, NE])
        tile_pack = sb("tile_pack", [1, CH // 4], i32)
        group_ids = sb("group_ids", [1, GROUPS], i32)
        logits = sb("logits", [P, TILES, NE])
        slot = sb("slot", [P, 2, TILES], i32)
        gate = sb("gate", [P, 2, TILES])
        small = sb("small", [P, 64])
        eps = sb("eps", [P, 1])

        U = sb("U", [P, 18000])
        V = sb("V", [P, 4200])
        ps = ctx.enter_context(nc.psum_tensor("ps", [P, 8, 512], f32))

        def carve(region, parts):
            at, views = 0, []
            for shape, dt in parts:
                words = ceil_div(int(mybir.dt.size(dt)) * _prod(shape), 4)
                v = region[:, at:at + words]
                if dt != f32:
                    v = v.bitcast(dt)
                v = v[:, 0:_prod(shape)]
                if len(shape) == 2:
                    v = v.rearrange("p (a b) -> p a b", a=shape[0])
                if len(shape) == 3:
                    v = v.rearrange("p (a b c) -> p a b c", a=shape[0], b=shape[1])
                views.append(v)
                at += words
            assert at <= region.shape[1], at
            return views

        xin, xn0, xT0, hw_sb = carve(V, [((T0, D), f32), ((T0, D), f32), ((T0 * KD, R0), f32), ((T0, D), f32)])
        xin, xn0, hw_sb = xin[0:R0, :, :], xn0[0:R0, :, :], hw_sb[0:R0, :, :]
        (src_raw, dst_raw, w_raw, fields, hi, onehot, reset, cum, prod) = carve(U, [
            ((COLS + 1,), i32), ((COLS + 1,), i32), ((COLS + 1,), f32), ((EC, F), f32), ((EC,), bf16),
            ((TILES, BC + 1), f32), ((TILES * (BC + 1),), bf16), ((TILES, BC + 1), f32), ((TILES, BC), f32)])
        chunk_ge = prod.rearrange("p a b -> p (a b)").bitcast(bf16)[:, 0:CH]
        tile_ids = U[0:1, 0:CH].bitcast(i32)
        tile_part = U[0:1, CH:CH + CH // 4].bitcast(i32)
        hist = sb("hist", [P, TILES])
        counts = sb("counts", [P, TILES])
        counts_i = sb("counts_i", [P, TILES], i32)
        chunk_end = sb("chunk_end", [P, TILES])
        chunk_end_col = sb("chunk_end_col", [P, 1])
        iota_chunk = onehot.rearrange("p a b -> p (a b)")[:, 0:CH]
        rank = sb("rank", [P, BC])
        rank_i = sb("rank_i", [P, BC], i32)
        rank_lo = sb("rank_lo", [P, BC], i32)
        rank_hi = sb("rank_hi", [P, BC], i32)
        addr = [sb(f"addr{s}", [P, BC], i32) for s in range(2)]
        rec = [sb(f"rec{s}", [P, BC, F]) for s in range(2)]
        pad_rec = sb("pad_rec", [P, 1, F])
        ones_bf = sb("ones_bf", [P, 1], bf16)
        real_row = sb("real_row", [P, 1])
        m1, m2, pick = sb("m1", [P, TILES]), sb("m2", [P, TILES]), sb("pick", [P, TILES])
        falling = sb("falling", [P, NE])
        (sorted_rec, gathered, onehot_w) = carve(U, [((CH, F), f32), ((2 * GC, D), f32), ((2 * GC, P), f32)])
        gather_idx = [sb(f"gather_idx{s}", [P, GC], i32) for s in range(2)]
        edge_lw = [sb(f"edge_lw{s}", [P, GC, 2]) for s in range(2)]
        (t_norm, t_out, t_T) = carve(U, [((TG, D), f32), ((2 * TG, D), f32), ((2 * KD, P), f32)])
        (eq, score, oh12, first2, rdata, rreset, rcum, rprod, rlog) = carve(U, [
            ((TILES, NE), f32), ((TILES, NE), f32), ((KT, NE), f32), ((2, TILES), f32),
            ((NE, KT + 1), f32), ((NE * (KT + 1),), bf16), ((NE, KT + 1), f32), ((NE, KT), f32), ((TILES, NE), f32)])
        (W1g, W2g, b2g, b1g, xs, xT, hT, ysb) = carve(U, [
            ((2 * KD, H), f32), ((2 * KH, D), f32), ((2, D), f32), ((2, KH), f32),
            ((4, D), f32), ((2 * KD, GT), f32), ((2 * KH, GT), f32), ((4, D), f32)])
        (tok_ring,) = carve(U, [((2 * TG, D), f32)])
        (y_ring, out_ring) = carve(U, [((4 * TG, D), f32), ((2 * TG, D), f32)])
        slot_st = [sb(f"slot_st{s}", [P, 2, TG], i32) for s in range(2)]

        gnn_b_row, gamma_row, beta_row = rows[:, 0, :], rows[:, 1, :], rows[:, 2, :]

        s_const_ld = sem("s_const_ld")
        s_edge_ld = sem("s_edge_ld")
        s_acc_ld = sem("s_acc_ld")
        s_pool_const = sem("s_pool_const")
        s_zero = sem("s_zero")
        s_dve = sem("s_dve")
        s_hist = sem("s_hist")
        s_prefix = sem("s_prefix")
        s_ends = sem("s_ends")
        s_ends_T = sem("s_ends_T")
        s_iota = sem("s_iota")
        s_ge = sem("s_ge")
        s_ids = sem("s_ids")
        s_padded = sem("s_padded")
        s_addr = sem("s_addr")
        s_scattered = [sem(f"s_scattered{s}") for s in range(2)]
        s_xin = sem("s_xin")
        s_xn0 = sem("s_xn0")
        s_var0 = sem("s_var0")
        s_std0 = sem("s_std0")
        s_xT0_ps = sem("s_xT0_ps")
        s_xT0 = sem("s_xT0")
        s_hw_ps = sem("s_hw_ps")
        s_hw = sem("s_hw")
        s_hw_st = sem("s_hw_st")
        s_rec_ld = sem("s_rec_ld")
        s_idx = sem("s_idx")
        s_gathered = [sem(f"s_gathered{s}") for s in range(2)]
        s_onehot = sem("s_onehot")
        s_agg = sem("s_agg")
        s_added = sem("s_added")
        s_var = sem("s_var")
        s_std = sem("s_std")
        s_tok = sem("s_tok")
        s_tok_T_ps = sem("s_tok_T_ps")
        s_tok_T = sem("s_tok_T")
        s_logit_ps = sem("s_logit_ps")
        s_tok_st = [sem(f"s_tok_st{s}") for s in range(2)]
        s_rhist = sem("s_rhist")
        s_rprefix = sem("s_rprefix")
        s_slots = sem("s_slots")
        s_logit = sem("s_logit")
        s_exp = sem("s_exp")
        s_gap = sem("s_gap")
        s_tok_ld = [sem(f"s_tok_ld{s}") for s in range(2)]
        s_slot_st = sem("s_slot_st")
        s_sent = [sem(f"s_sent{s}") for s in range(2)]
        s_exp_zero = sem("s_exp_zero")
        s_grp_ld = [sem(f"s_grp_ld{s}") for s in range(2)]
        s_xT_ps = sem("s_xT_ps")
        s_xT = sem("s_xT")
        s_h_ps = sem("s_h_ps")
        s_h = sem("s_h")
        s_y_ps = sem("s_y_ps")
        s_y = sem("s_y")
        s_y_st = [sem(f"s_y_st{s}") for s in range(2)]
        s_slot_st2 = sem("s_slot_st2")
        s_fetched = [sem(f"s_fetched{s}") for s in range(2)]
        s_out = sem("s_out")
        s_out_st = [sem(f"s_out_st{s}") for s in range(2)]

        s_held = sem("s_held")

        def hold(engine, semaphore, value):
            engine.wait_ge(semaphore, value)
            engine.sem_inc(s_held, 1)

        block = ctx.enter_context(nc.Block())

        x_rounds = x.rearrange("(t p) d -> p t d", p=R0)
        feat_rounds = features[0:N, :].rearrange("(t p) d -> p t d", p=R0)
        rec_rows = records.rearrange("(p c) f -> p (c f)", p=P)
        tok_tiles = tokens.rearrange("(t p) d -> p t d", p=P)
        in_groups = expert_in.rearrange("(g p) d -> p g d", p=P)
        out_groups = expert_out.rearrange("(g p) d -> p g d", p=P)
        out_tiles = out[0:(TILES - 1) * P, :].rearrange("(t p) d -> p t d", p=P)
        W1_e = W1.rearrange("e (k p) h -> p (e k) h", p=P)
        W2_e = W2.rearrange("e (k p) d -> p (e k) d", p=P)

        @block.sync
        def _(sp):
            src_cols = src[0:COLS * P].rearrange("(p c) -> p c", p=P)
            dst_cols = dst[0:COLS * P].rearrange("(p c) -> p c", p=P)
            w_cols = edge_weight[0:COLS * P].rearrange("(p c) -> p c", p=P)
            sp.wait_ge(s_zero, 1)
            sp.dma_start(src_raw[:, 0:COLS], src_cols).then_inc(s_edge_ld, 16)
            sp.dma_start(src_raw[0:TAIL, COLS:COLS + 1],
                         src[COLS * P:E_EDGES].rearrange("(p c) -> p c", c=1)).then_inc(s_edge_ld, 16)
            sp.dma_start(dst_raw[:, 0:COLS], dst_cols).then_inc(s_edge_ld, 16)
            sp.dma_start(dst_raw[0:TAIL, COLS:COLS + 1],
                         dst[COLS * P:E_EDGES].rearrange("(p c) -> p c", c=1)).then_inc(s_edge_ld, 16)
            sp.dma_start(w_raw[:, 0:COLS], w_cols).then_inc(s_edge_ld, 16)
            sp.dma_start(w_raw[0:TAIL, COLS:COLS + 1],
                         edge_weight[COLS * P:E_EDGES].rearrange("(p c) -> p c", c=1)).then_inc(s_edge_ld, 16)
            reps = CH // 4
            for q in range(4):
                sp.dma_start(records.rearrange("(p c) f -> p c f", p=P)[:, q * reps:(q + 1) * reps, :],
                             pad_rec[:, 0:1, :].broadcast_to([P, reps, F])).then_inc(s_padded, 16)
            sp.dma_start(features[N:N + 1, :], zeros[0:1, :]).then_inc(s_padded, 16)
            sp.dma_start(Wg[:, :, :], gnn_W.rearrange("(k p) n -> p k n", p=P)).then_inc(s_const_ld, 16)
            sp.dma_start(Wr_sb[:, :, :], Wr.rearrange("(k p) n -> p k n", p=P)).then_inc(s_const_ld, 16)
            sp.dma_start(rows[:, 0, :], gnn_b.partition_broadcast(P)).then_inc(s_const_ld, 16)
            sp.dma_start(rows[:, 1, :], gamma.partition_broadcast(P)).then_inc(s_const_ld, 16)
            sp.dma_start(rows[:, 2, :], beta.partition_broadcast(P)).then_inc(s_const_ld, 16)
            sp.dma_start(br_row[:, :], br.partition_broadcast(P)).then_inc(s_const_ld, 16)

            def load_round0(i, first):
                if not first:
                    sp.wait_ge(s_xn0, i)
                sp.dma_start(xin[:, :, :], x_rounds[:, bass.ds(i * T0, T0), :]).then_inc(s_xin, 16)

            load_round0(0, True)
            with sp.Fori(1, ROUNDS0) as i:
                load_round0(i, False)

            TQ = (TILES - 1)
            sp.wait_ge(s_zero, 2)
            cuts = [0, 25, 50, 75, TQ]
            for a, b in zip(cuts, cuts[1:]):
                sp.dma_start(acc[:, a:b, :], x[a * P:b * P, :].rearrange("(t p) d -> p t d", p=P)).then_inc(s_acc_ld, 16)
            sp.dma_start(acc[0:LAST, TILES - 1, :], x[TQ * P:N, :]).then_inc(s_acc_ld, 16)
            ZG = 4
            with sp.Fori(0, GROUPS * 2 // ZG) as i:
                sp.dma_start(in_groups[:, bass.ds(i * ZG, ZG), :],
                             zeros[:, None, :].broadcast_to([P, ZG, D])).then_inc(s_exp_zero, 16)

            for s in range(2):
                sp.wait_ge(s_scattered[s], 16 * (BC * PAIRS_A if s == 0 else BC * (PAIRS_A - 1) + 1))
            SR = CH * F // 4
            flat = sorted_rec.rearrange("p c f -> p (c f)")
            sp.wait_ge(s_addr, 2 * PAIRS_A)
            for q in range(4):
                sp.dma_start(flat[:, q * SR:(q + 1) * SR], rec_rows[:, q * SR:(q + 1) * SR]).then_inc(s_rec_ld, 16)

            with sp.Fori(0, PAIRS_E) as i:
                for s in range(2):
                    sp.wait_ge(s_tok, i * 2 + s + 1)
                    sp.dma_start(tok_tiles[:, bass.ds((i * 2 + s) * TG, TG), :],
                                 t_out[:, s * TG:(s + 1) * TG, :]).then_inc(s_tok_st[s], 16)

            for s in range(2):
                sp.wait_ge(s_tok_st[s], 16 * PAIRS_E)
            sp.wait_ge(s_slots, 1)

            def load_tokens(i, s, first):
                if not first:
                    sp.wait_ge(s_sent[s], i * (2 * TG * 16))
                sp.dma_start(tok_ring[:, s * TG:(s + 1) * TG, :],
                             tok_tiles[:, bass.ds((i * 2 + s) * TG, TG), :]).then_inc(s_tok_ld[s], 16)
            for s in range(2):
                load_tokens(0, s, True)
            with sp.Fori(1, PAIRS_E) as i:
                for s in range(2):
                    load_tokens(i, s, False)
            for s in range(2):
                sp.wait_ge(s_sent[s], PAIRS_E * 2 * TG * 16)

            def load_group(i, s, first):
                e = sp.value_load(group_ids[0:1, bass.ds(i * 2 + s, 1)], min_val=0, max_val=NE - 1)
                if not first:
                    sp.wait_ge(s_y_ps, 2 * i + s - 1)
                    sp.wait_ge(s_y, 2 * i + s - 1)
                sp.dma_start(xs[:, 2 * s:2 * s + 2, :], in_groups[:, bass.ds((i * 2 + s) * 2, 2), :]).then_inc(s_grp_ld[s], 16)
                sp.dma_start(W1g[:, KD * s:KD * s + KD, :], W1_e[:, bass.ds(e * KD, KD), :]).then_inc(s_grp_ld[s], 16)
                sp.dma_start(b1g[:, s, :], b1_cols[bass.ds(e, 1), :, :].rearrange("a p k -> p (a k)")).then_inc(s_grp_ld[s], 16)
                sp.dma_start(W2g[:, KH * s:KH * s + KH, :], W2_e[:, bass.ds(e * KH, KH), :]).then_inc(s_grp_ld[s], 16)
                sp.dma_start(b2g[:, s:s + 1, :], b2[bass.ds(e, 1), :].partition_broadcast(P)).then_inc(s_grp_ld[s], 16)
            for s in range(2):
                load_group(0, s, True)
            with sp.Fori(1, PAIRS_D) as i:
                for s in range(2):
                    load_group(i, s, False)

            def store_out(i, s):
                sp.wait_ge(s_out, i * 2 + s + 1)
                sp.dma_start(out_tiles[:, bass.ds((i * 2 + s) * TG, TG), :],
                             out_ring[:, s * TG:(s + 1) * TG, :]).then_inc(s_out_st[s], 16)
            with sp.Fori(0, PAIRS_E - 1) as i:
                for s in range(2):
                    store_out(i, s)
            store_out(PAIRS_E - 1, 0)
            sp.wait_ge(s_out, 2 * PAIRS_E)
            at = (2 * PAIRS_E - 1) * TG
            sp.dma_start(out_tiles[:, at:TILES - 1, :], out_ring[:, TG:2 * TG - 1, :]).then_inc(s_out_st[1], 16)
            sp.dma_start(out[(TILES - 1) * P:N, :], out_ring[0:LAST, 2 * TG - 1, :]).then_inc(s_out_st[1], 16)
            sp.wait_ge(s_out_st[0], 16 * PAIRS_E)
            sp.wait_ge(s_out_st[1], 16 * PAIRS_E + 16)

        @block.gpsimd
        def _(pool):
            nc.gpsimd.memset(ident[:, :], 0.0).then_inc(s_pool_const, 1)
            nc.gpsimd.memset(ones[:, :], 1.0).then_inc(s_pool_const, 1)
            nc.gpsimd.memset(ones_bf[:, :], 1.0)
            nc.gpsimd.iota(iota_row[:, :], pattern=[[1, P]], base=0, channel_multiplier=0,
                           allow_small_or_imprecise_dtypes=True).then_inc(s_pool_const, 1)
            pool.wait_ge(s_pool_const, 3)
            nc.gpsimd.affine_select(out=ident[:, :], in_=ident[:, :], compare_op=ALU.not_equal, fill=1.0,
                                    base=0, pattern=[[-1, P]], channel_multiplier=1).then_inc(s_pool_const, 1)
            nc.gpsimd.affine_select(out=real_row[:, :], in_=ones[:, 0:1], compare_op=ALU.is_gt, fill=0.0,
                                    base=LAST, pattern=[[0, 1]], channel_multiplier=-1)
            nc.gpsimd.affine_select(out=lower[:, :], in_=ones[:, :], compare_op=ALU.is_gt, fill=0.0,
                                    base=0, pattern=[[1, P]], channel_multiplier=-1).then_inc(s_pool_const, 1)

            pool.wait_ge(s_hist, 1)
            nc.gpsimd.iota(iota_chunk, pattern=[[1, CH]], base=0, channel_multiplier=0,
                           allow_small_or_imprecise_dtypes=True).then_inc(s_iota, 1)

            pool.wait_ge(s_padded, 16 * 5)

            def scatter_block(k, s, columns):
                hold(pool, s_addr, k + 1)
                for c in range(columns):
                    parts = P if columns == BC else TAIL
                    nc.gpsimd.indirect_dma_start(
                        out=records[:, :], out_offset=bass.IndirectOffsetOnAxis(ap=addr[s][0:parts, c:c + 1], axis=0),
                        in_=rec[s][0:parts, c, :], in_offset=None, compute_op=ALU.bypass).then_inc(s_scattered[s], 16)
            with pool.Fori(0, PAIRS_A - 1) as i:
                for s in range(2):
                    scatter_block(i * 2 + s, s, BC)
            scatter_block(2 * PAIRS_A - 2, 0, BC)
            scatter_block(2 * PAIRS_A - 1, 1, 1)

            pool.wait_ge(s_hw_st, 16 * ROUNDS0)
            pool.wait_ge(s_padded, 16 * 5)

            def gather_group(i, s, first):
                if not first:
                    pool.wait_ge(s_agg, (i * 2 + s - 1) * (GC // 4))
                hold(pool, s_idx, i * 2 + s + 1)
                for c in range(GC):
                    nc.gpsimd.indirect_dma_start(
                        out=gathered[:, s * GC + c, :], out_offset=None, in_=features[:, :],
                        in_offset=bass.IndirectOffsetOnAxis(ap=gather_idx[s][:, c:c + 1], axis=0),
                        compute_op=ALU.bypass).then_inc(s_gathered[s], 16)
            for s in range(2):
                gather_group(0, s, True)
            with pool.Fori(1, PAIRS_B) as i:
                for s in range(2):
                    gather_group(i, s, False)

            pool.wait_ge(s_exp_zero, 16 * (GROUPS * 2 // 4))

            def send_group(i, s, last):
                pool.wait_ge(s_slot_st, i * 2 + s + 1)
                hold(pool, s_tok_ld[s], i * 16 + 16)
                for t in range(TG):
                    parts = LAST if last and t == TG - 1 else P
                    for k in range(2):
                        nc.gpsimd.indirect_dma_start(
                            out=expert_in[:, :],
                            out_offset=bass.IndirectOffsetOnAxis(ap=slot_st[s][0:parts, k, t:t + 1], axis=0),
                            in_=tok_ring[0:parts, s * TG + t, :], in_offset=None,
                            compute_op=ALU.bypass).then_inc(s_sent[s], 16)
            with pool.Fori(0, PAIRS_E - 1) as i:
                for s in range(2):
                    send_group(i, s, False)
            send_group(PAIRS_E - 1, 0, False)
            send_group(PAIRS_E - 1, 1, True)

            for s in range(2):
                pool.wait_ge(s_y_st[s], 16 * PAIRS_D)

            def fetch_group(i, s, first, last):
                if not first:
                    pool.wait_ge(s_out, i * 2 + s - 1)
                hold(pool, s_slot_st2, i * 2 + s + 1)
                for t in range(TG):
                    parts = LAST if last and t == TG - 1 else P
                    for k in range(2):
                        nc.gpsimd.indirect_dma_start(
                            out=y_ring[0:parts, s * 2 * TG + 2 * t + k, :], out_offset=None, in_=expert_out[:, :],
                            in_offset=bass.IndirectOffsetOnAxis(ap=slot_st[s][0:parts, k, t:t + 1], axis=0),
                            compute_op=ALU.bypass).then_inc(s_fetched[s], 16)
            fetch_group(0, 0, True, False)
            fetch_group(0, 1, True, False)
            with pool.Fori(1, PAIRS_E - 1) as i:
                for s in range(2):
                    fetch_group(i, s, False, False)
            fetch_group(PAIRS_E - 1, 0, False, False)
            fetch_group(PAIRS_E - 1, 1, False, True)

        @block.vector
        def _(dve):
            v = nc.vector
            step = Steps(dve, s_dve)
            v.memset(src_raw[:, COLS:COLS + 1], NOBUCKET * P)
            v.memset(dst_raw[:, COLS:COLS + 1], 0)
            v.memset(zeros[:, :], 0.0)
            v.memset(eps[:, :], EPS)
            v.memset(pad_rec[:, 0, 0:1], float(N))
            v.memset(pad_rec[:, 0, 1:3], 0.0)
            v.memset(w_raw[:, COLS:COLS + 1], 0.0).then_inc(s_zero, 1)
            v.memset(acc[:, TILES - 1, :], 0.0).then_inc(s_zero, 1)
            v.memset(reset[:, :], 1.0)
            step(v.memset(hi[:, COLS:EC], float(NOBUCKET)))
            step(v.memset(reset.rearrange("p (b c) -> p b c", c=BC + 1)[:, :, 0:1], 0.0))
            step(v.memset(fields[:, COLS:EC, :], 0.0))

            dve.wait_ge(s_edge_ld, 16 * 6)
            src_hi = cum.rearrange("p a b -> p (a b)").bitcast(i32)[:, 0:COLS + 1]
            src_lo = onehot.rearrange("p a b -> p (a b)").bitcast(i32)[:, 0:COLS + 1]
            v.tensor_single_scalar(src_hi, src_raw[:, :], 7, ALU.arith_shift_right)
            step(v.tensor_single_scalar(src_lo, src_raw[:, :], P - 1, ALU.bitwise_and))
            v.tensor_copy(hi[:, 0:COLS + 1], src_hi)
            v.tensor_copy(fields[:, 0:COLS + 1, 0], dst_raw[:, :])
            v.tensor_copy(fields[:, 0:COLS + 1, 1], src_lo)
            step(v.tensor_copy(fields[:, 0:COLS + 1, 2], w_raw[:, :]))
            dve.wait_ge(s_pool_const, 5)
            step(v.tensor_copy(iota_bf[:, :], iota_row[:, :]))

            HB = 14
            junk = w_raw.bitcast(bf16)[:, 0:EC]
            with dve.Fori(0, TILES // HB) as i:
                step.enter(i, 0, HB)
                for j in range(HB):
                    step(v.tensor_scalar(junk, hi[:, :], iota_row[:, bass.ds(i * HB + j, 1)], 0.0,
                                         ALU.is_equal, ALU.add, accum_out=hist[:, bass.ds(i * HB + j, 1)]))
            step.leave(TILES // HB)
            dve.sem_inc(s_hist, 1)

            dve.wait_ge(s_prefix, 1)
            step(v.tensor_scalar(counts_i[:, :], ps[:, 5, 0:TILES], float(P - 1), None, ALU.add))
            step(v.tensor_single_scalar(counts_i[:, :], counts_i[:, :], 7, ALU.arith_shift_right))
            step(v.tensor_copy(counts[:, :], counts_i[:, :]))
            step(v.tensor_tensor_scan(chunk_end[:, :], ones[:, 0:TILES], counts[:, :], 0.0, ALU.mult, ALU.add))
            dve.sem_inc(s_ends, 1)
            step(v.tensor_tensor(counts[:, :], chunk_end[:, :], counts[:, :], ALU.subtract))
            step(v.tensor_scalar(counts[:, :], counts[:, :], float(P), -1.0, ALU.mult, ALU.add))
            step(v.tensor_tensor(cum[:, :, BC], ps[:, 4, 0:TILES], counts[:, :], ALU.add))

            dve.wait_ge(s_ends_T, 1)
            step(v.tensor_copy(chunk_end_col[0:TILES, :], ps[0:TILES, 6, 0:1]))
            dve.wait_ge(s_iota, 1)
            v.tensor_scalar(chunk_ge[0:TILES, :], iota_chunk[0:TILES, :], chunk_end_col[0:TILES, 0:1], None,
                            ALU.is_ge).then_inc(s_ge, 1)
            dve.wait_ge(s_ids, 1)
            CQ = CH // 4
            step(v.tensor_scalar(tile_ids[0:1, :].rearrange("p (q c) -> p q c", q=4), ps[0:1, 4:8, 0:CQ],
                                 float(TILES - 1), None, ALU.min))
            packed = tile_ids[0:1, :].rearrange("p (g c) -> p g c", c=4)
            step(v.tensor_copy(tile_pack[0:1, :], packed[:, :, 0]))
            for j in range(1, 4):
                step(v.tensor_single_scalar(tile_part[0:1, :], packed[:, :, j], 7 * j, ALU.logical_shift_left))
                step(v.tensor_tensor(tile_pack[0:1, :], tile_pack[0:1, :], tile_part[0:1, :], ALU.bitwise_or))

            def rank_block(i, s, first):
                k = i * 2 + s
                step(v.tensor_tensor(onehot[:, :, 1:BC + 1],
                                     hi[:, None, bass.ds(k * BC, BC)].broadcast_to([P, TILES, BC]),
                                     iota_bf[:, 0:TILES, None].broadcast_to([P, TILES, BC]), ALU.is_equal))
                step(v.tensor_copy(onehot[:, :, 0], cum[:, :, BC]))
                step(v.tensor_tensor_scan(cum.rearrange("p b c -> p (b c)"), reset[:, :],
                                          onehot.rearrange("p b c -> p (b c)"), 0.0, ALU.mult, ALU.add))
                step(v.tensor_tensor(prod[:, :, :], cum[:, :, 1:BC + 1], onehot[:, :, 1:BC + 1], ALU.mult))
                step(v.tensor_reduce(rank[:, :], prod.rearrange("p b c -> p c b"), AX.X, ALU.add))
                step(v.tensor_copy(rank_i[:, :], rank[:, :]))
                v.tensor_single_scalar(rank_lo[:, :], rank_i[:, :], P - 1, ALU.bitwise_and)
                step(v.tensor_single_scalar(rank_hi[:, :], rank_i[:, :], 7, ALU.arith_shift_right))
                if not first:
                    dve.wait_ge(s_scattered[s], i * (16 * BC))
                step(v.tensor_copy(rec[s][:, :, :], fields[:, bass.ds(k * BC, BC), :]))
                v.scalar_tensor_tensor(addr[s][:, :], rank_lo[:, :], float(CH), rank_hi[:, :],
                                       ALU.mult, ALU.add).then_inc(s_addr, 1)

            SA = 8

            SN = 4

            def norm0(i, first):
                dve.wait_ge(s_xin, i * 16 + 16)
                if not first:
                    dve.wait_ge(s_xT0_ps, i)
                st, mv, rs = small[0:R0, 0:24], small[0:R0, 24:32], small[0:R0, 32:36]
                dve.sem_inc(s_held, 1)
                for t in range(T0):
                    last = v.bn_stats(st[:, 6 * t:6 * t + 6], xin[:, t, :])
                step(last, s_held)
                for t in range(T0):
                    last = v.bn_aggr(mv[:, 2 * t:2 * t + 2], st[:, 6 * t:6 * t + 6])
                step(last)
                dve.sem_inc(s_var0, 1)
                dve.wait_ge(s_std0, i + 1)
                step(v.reciprocal(rs, rs))
                for t in range(T0):
                    last = v.tensor_scalar(xn0[:, t, :], xin[:, t, :], mv[:, 2 * t:2 * t + 1], rs[:, t:t + 1],
                                           ALU.subtract, ALU.mult)
                step(last)
                dve.sem_inc(s_xn0, 1)

            step(v.memset(small[:, :], 0.0))
            rank_block(0, 0, True)
            rank_block(0, 1, True)
            norm0(0, True)
            with dve.Fori(1, ROUNDS0) as i:
                step.enter(i, 1, 2 * SA + SN)
                rank_block(i, 0, False)
                rank_block(i, 1, False)
                norm0(i, False)
            step.leave(ROUNDS0 - 1)
            with dve.Fori(ROUNDS0, PAIRS_A) as i:
                step.enter(i, ROUNDS0, 2 * SA)
                rank_block(i, 0, False)
                rank_block(i, 1, False)
            step.leave(PAIRS_A - ROUNDS0)

            dve.wait_ge(s_acc_ld, 16 * 5)
            dve.wait_ge(s_rec_ld, 16 * 4)

            def sum_group(i, s, first):
                g = i * 2 + s
                dve.wait_ge(s_idx, g + 1)
                if not first:
                    dve.wait_ge(s_agg, (g - 1) * (GC // 4))
                for c in range(GC):
                    last = v.tensor_scalar(onehot_w[:, s * GC + c, :], iota_row[:, :], edge_lw[s][:, c, 0:1],
                                           edge_lw[s][:, c, 1:2], ALU.is_equal, ALU.mult)
                last.then_inc(s_onehot, 1)
                for q in range(GC // 4):
                    pk = dve.value_load(tile_pack[0:1, bass.ds(g * (GC // 4) + q, 1)], min_val=0, max_val=(1 << 28) - 1)
                    dve.wait_ge(s_agg, g * (GC // 4) + q + 1)
                    for c in range(4):
                        t = nc.s_assert_within(dve.snap((pk >> (7 * c)) & 127), 0, TILES - 1, 
                                               skip_runtime_bounds_check_because="a tile's number, cut at the last tile")
                        bank, half = 2 * q + c // 2, 256 * (c % 2)
                        ins = v.tensor_tensor(acc[:, bass.ds(t, 1), :], acc[:, bass.ds(t, 1), :],
                                              ps[:, bank:bank + 1, half:half + D], ALU.add)
                        step(ins)
                    dve.sem_inc(s_added, 1)
            sum_group(0, 0, True)
            sum_group(0, 1, True)
            with dve.Fori(1, PAIRS_B) as i:
                step.enter(i, 1, 2 * GC)
                sum_group(i, 0, False)
                sum_group(i, 1, False)
            step.leave(PAIRS_B - 1)

            def norm_group(i, s, first):
                g = i * 2 + s
                a, n, o = acc[:, bass.ds(g * TG, TG), :], t_norm, t_out[:, s * TG:(s + 1) * TG, :]
                st, mv, rs = small[:, 0:6 * TG], small[:, 6 * TG:8 * TG], small[:, 8 * TG:9 * TG]
                step(v.tensor_tensor(a, a, rows[:, 0:1, :].broadcast_to([P, TG, D]), ALU.add), s_held)
                for r in range(2):
                    def tile(t):
                        return n[:, t, :] if r else acc[:, bass.ds(g * TG + t, 1), :].rearrange("p a d -> p (a d)")
                    for t in range(TG):
                        last = v.bn_stats(st[:, 6 * t:6 * t + 6], tile(t))
                    step(last, s_held)
                    for t in range(TG):
                        last = v.bn_aggr(mv[:, 2 * t:2 * t + 2], st[:, 6 * t:6 * t + 6])
                    last.then_inc(s_var, 1)
                    dve.wait_ge(s_std, g * 2 + r + 1)
                    step(v.reciprocal(rs, rs))
                    for t in range(TG):
                        last = v.tensor_scalar(n[:, t, :], tile(t), mv[:, 2 * t:2 * t + 1], rs[:, t:t + 1],
                                               ALU.subtract, ALU.mult)
                    step(last, s_held)
                step(v.tensor_tensor(n, n, rows[:, 1:2, :].broadcast_to([P, TG, D]), ALU.mult))
                if not first:
                    dve.wait_ge(s_tok_T_ps, (g - 1) * TG)
                    dve.wait_ge(s_tok_st[s], i * 16)
                v.tensor_tensor(o, n, rows[:, 2:3, :].broadcast_to([P, TG, D]), ALU.add).then_inc(s_tok, 1)

            def add_br(g):
                for t in range(TG):
                    tt = g * TG + t
                    dve.wait_ge(s_logit_ps, tt + 1)
                    v.tensor_tensor(logits[:, bass.ds(tt, 1), :], ps[:, 2 + t % 2:3 + t % 2, 0:NE], br_row[:, None, :],
                                    ALU.add).then_inc(s_logit, 1)
            SC = 8
            norm_group(0, 0, True)
            add_br(0)
            norm_group(0, 1, True)
            add_br(1)
            with dve.Fori(1, PAIRS_E) as i:
                step.enter(i, 1, 2 * SC)
                norm_group(i, 0, False)
                add_br(i * 2)
                norm_group(i, 1, False)
                add_br(i * 2 + 1)
            step.leave(PAIRS_E - 1)

            dve.wait_ge(s_logit, TILES)
            for s in range(2):
                dve.wait_ge(s_tok_st[s], 16 * PAIRS_E)
            L = logits[:, :, :]

            def wide(a):
                return a[:, :, None].broadcast_to([P, TILES, NE])
            step(v.tensor_scalar(falling[:, :], iota_row[:, 0:NE], -1.0, float(NE), ALU.mult, ALU.add))
            fall = falling[:, None, :].broadcast_to([P, TILES, NE])
            cur = L
            for k, m in enumerate((m1, m2)):
                oh = oh12[:, k * TILES:(k + 1) * TILES, :]
                step(v.tensor_reduce(m[:, :], cur, AX.X, ALU.max))
                step(v.tensor_tensor(eq[:, :, :], cur, wide(m), ALU.is_equal))
                step(v.tensor_tensor(score[:, :, :], eq[:, :, :], fall, ALU.mult))
                step(v.tensor_reduce(pick[:, :], score[:, :, :], AX.X, ALU.max))
                step(v.tensor_tensor(oh, fall, wide(pick), ALU.is_equal))
                if k == 0:
                    step(v.scalar_tensor_tensor(rlog[:, :, :].rearrange("p a b -> p (a b)"),
                                                oh.rearrange("p a b -> p (a b)"), -3.0e38,
                                                L.rearrange("p a b -> p (a b)"), ALU.mult, ALU.add))
                    cur = rlog[:, :, :]
            v.tensor_tensor(pick[:, :], m2[:, :], m1[:, :], ALU.subtract).then_inc(s_gap, 1)
            for k in range(2):
                oh = oh12[:, (k + 1) * TILES - 1, :]
                step(v.tensor_scalar(oh, oh, real_row[:, 0:1], None, ALU.mult))
            dve.wait_ge(s_exp, 1)
            step(v.tensor_scalar(m1[:, :], m2[:, :], 1.0, None, ALU.add))
            step(v.reciprocal(gate[:, 0, :], m1[:, :]))
            step(v.tensor_tensor(gate[:, 1, :], m2[:, :], gate[:, 0, :], ALU.mult))

            step(v.tensor_copy(rdata[:, :, 1:KT + 1], oh12[:, :, :].rearrange("p t e -> p e t")))
            step(v.memset(rreset[:, :], 1.0))
            step(v.memset(rreset.rearrange("p (e t) -> p e t", e=NE)[:, :, 0:1], 0.0))
            rh = small[:, 0:NE]
            step(v.tensor_reduce(rh, rdata[:, :, 1:KT + 1], AX.X, ALU.add))
            dve.sem_inc(s_rhist, 1)
            dve.wait_ge(s_rprefix, 1)
            rc, rci, rend = small[:, 8:16], counts_i[:, 0:NE], small[:, 16:24]
            step(v.tensor_scalar(rci, ps[:, 5, 0:NE], float(GT - 1), None, ALU.add))
            step(v.tensor_single_scalar(rci, rci, 8, ALU.arith_shift_right))
            step(v.tensor_copy(rc, rci))
            step(v.tensor_tensor_scan(rend, ones[:, 0:NE], rc, 0.0, ALU.mult, ALU.add))
            step(v.tensor_tensor(rc, rend, rc, ALU.subtract))
            step(v.tensor_scalar(rc, rc, float(GT), -1.0, ALU.mult, ALU.add))
            step(v.tensor_tensor(rdata[:, :, 0], ps[:, 4, 0:NE], rc, ALU.add))
            step(v.tensor_tensor_scan(rcum.rearrange("p e t -> p (e t)"), rreset[:, :],
                                      rdata.rearrange("p e t -> p (e t)"), 0.0, ALU.mult, ALU.add))
            step(v.tensor_tensor(rprod[:, :, :], rcum[:, :, 1:KT + 1], rdata[:, :, 1:KT + 1], ALU.mult))
            flat_slot = slot[:, :, :].rearrange("p k t -> p (k t)")
            rank_f = eq.rearrange("p a b -> p (a b)")[:, 0:KT]
            step(v.tensor_reduce(rank_f, rprod.rearrange("p e t -> p t e"), AX.X, ALU.add))
            step(v.tensor_copy(flat_slot, rank_f))
            ge = rcum.rearrange("p e t -> p (e t)")[0:1, 0:NE * GROUPS].rearrange("p (e g) -> p e g", e=NE)
            gf = score.rearrange("p a b -> p (a b)")[0:1, 0:GROUPS]
            step(v.tensor_tensor(ge, iota_row[0:1, None, 0:GROUPS].broadcast_to([1, NE, GROUPS]),
                                 rend[0:1, :, None].broadcast_to([1, NE, GROUPS]), ALU.is_ge))
            step(v.tensor_reduce(gf, ge.rearrange("p e g -> p g e"), AX.X, ALU.add))
            step(v.tensor_scalar(group_ids[0:1, :], gf, float(NE - 1), None, ALU.min))
            dve.sem_inc(s_slots, 1)

            def move_xT(g, s, first):
                dve.wait_ge(s_xT_ps, g + 1)
                if not first:
                    dve.wait_ge(s_h_ps, (g - 1) * KH)
                v.tensor_copy(xT[:, KD * s:KD * s + KD, :], ps[:, s, :].rearrange("p (k t) -> p k t", k=KD)).then_inc(s_xT, 1)

            def add_b2(g, s, i, first):
                dve.wait_ge(s_y_ps, g + 1)
                if not first:
                    dve.wait_ge(s_y_st[s], i * 16)
                v.tensor_tensor(ysb[:, 2 * s:2 * s + 2, :], ps[:, 6 + s, :].rearrange("p (j d) -> p j d", j=2),
                                b2g[:, s:s + 1, :].broadcast_to([P, 2, D]), ALU.add).then_inc(s_y, 1)

            move_xT(0, 0, True)
            move_xT(1, 1, True)
            add_b2(0, 0, 0, True)
            move_xT(2, 0, False)
            add_b2(1, 1, 0, True)
            move_xT(3, 1, False)
            add_b2(2, 0, 1, False)
            with dve.Fori(2, PAIRS_D) as i:
                move_xT(i * 2, 0, False)
                add_b2(i * 2 - 1, 1, i - 1, False)
                move_xT(i * 2 + 1, 1, False)
                add_b2(i * 2, 0, i, False)
            add_b2(GROUPS - 1, 1, PAIRS_D - 1, False)

            def combine(i, s, first, last):
                g = i * 2 + s
                dve.wait_ge(s_fetched[s], i * (2 * TG * 16) + 2 * TG * 16)
                if not first:
                    dve.wait_ge(s_out_st[s], i * 16)
                for k in range(2):
                    for t in range(TG):
                        rows_ = LAST if last and t == TG - 1 else P
                        tt = g * TG + t
                        o = out_ring[0:rows_, s * TG + t, :]
                        prev = acc[0:rows_, bass.ds(tt, 1), :].rearrange("p a d -> p (a d)") if k == 0 else o
                        ins = v.scalar_tensor_tensor(o, y_ring[0:rows_, s * 2 * TG + 2 * t + k, :],
                                                     gate[0:rows_, k, bass.ds(tt, 1)], prev, ALU.mult, ALU.add)
                    if k == 0:
                        step(ins)
                ins.then_inc(s_out, 1)
            combine(0, 0, True, False)
            combine(0, 1, True, False)
            with dve.Fori(1, PAIRS_E - 1) as i:
                step.enter(i, 1, 2)
                combine(i, 0, False, False)
                combine(i, 1, False, False)
            step.leave(PAIRS_E - 2)
            combine(PAIRS_E - 1, 0, False, False)
            combine(PAIRS_E - 1, 1, False, True)

        @block.scalar
        def _(act):
            a = nc.scalar

            act.wait_ge(s_zero, 1)
            def round0(i, first):
                act.wait_ge(s_var0, i + 1)
                a.activation(small[0:R0, 32:36], small[0:R0, 25:32:2], ACT.Sqrt, bias=eps[0:R0, :]).then_inc(s_std0, 1)
                act.wait_ge(s_xT0_ps, i + 1)
                a.activation(xT0[:, :, :].rearrange("p a b -> p (a b)").rearrange("p (q c) -> p q c", q=2),
                             ps[:, 0:2, 0:T0 * KD * R0 // 2], ACT.Copy).then_inc(s_xT0, 1)
                act.wait_ge(s_hw_ps, i + 1)
                if not first:
                    act.wait_ge(s_hw_st, i * 16)
                a.activation(hw_sb.rearrange("p t d -> p (t d)").rearrange("p (q c) -> p q c", q=2),
                             ps[0:R0, 2:4, :], ACT.Copy).then_inc(s_hw, 1)
                act.wait_ge(s_hw, i + 1)
                act.dma_start(feat_rounds[:, bass.ds(i * T0, T0), :], hw_sb).then_inc(s_hw_st, 16)
            round0(0, True)
            with act.Fori(1, ROUNDS0) as i:
                round0(i, False)

            act.wait_ge(s_rec_ld, 16 * 4)

            def stage(i, s, first):
                g = i * 2 + s
                if not first:
                    act.wait_ge(s_gathered[s], i * (GC * 16))
                    act.wait_ge(s_onehot, g - 1)
                a.activation(edge_lw[s][:, :, :], sorted_rec[:, bass.ds(g * GC, GC), 1:3], ACT.Copy)
                a.activation(gather_idx[s][:, :], sorted_rec[:, bass.ds(g * GC, GC), 0], ACT.Copy).then_inc(s_idx, 1)
            stage(0, 0, True)
            stage(0, 1, True)
            with act.Fori(1, PAIRS_B) as i:
                stage(i, 0, False)
                stage(i, 1, False)

            def tok_group(g, first):
                for r in range(2):
                    act.wait_ge(s_var, g * 2 + r + 1)
                    a.activation(small[:, 8 * TG:9 * TG], small[:, 6 * TG + 1:8 * TG:2], ACT.Sqrt,
                                 bias=eps[:, :]).then_inc(s_std, 1)
                for t in range(TG):
                    tt = g * TG + t
                    act.wait_ge(s_tok_T_ps, tt + 1)
                    if not (first and t < 1):
                        act.wait_ge(s_logit_ps, tt)
                    h = t % 2
                    a.activation(t_T[:, KD * h:KD * h + KD, :], ps[:, h, 0:KD * P].rearrange("p (k t) -> p k t", k=KD),
                                 ACT.Copy).then_inc(s_tok_T, 1)
            tok_group(0, True)
            with act.Fori(1, 2 * PAIRS_E) as g:
                tok_group(g, False)

            act.wait_ge(s_gap, 1)
            a.activation(m2[:, :], pick[:, :], ACT.Exp).then_inc(s_exp, 1)

            def stage_slots(semaphore, i, s, first, used):
                if not first:
                    act.wait_ge(used[s], i * (2 * TG * 16))
                a.activation(slot_st[s][:, :, :], slot[:, :, bass.ds((i * 2 + s) * TG, TG)], ACT.Copy).then_inc(semaphore, 1)
            act.wait_ge(s_slots, 1)
            for s in range(2):
                stage_slots(s_slot_st, 0, s, True, s_sent)
            with act.Fori(1, PAIRS_E) as i:
                for s in range(2):
                    stage_slots(s_slot_st, i, s, False, s_sent)

            def gelu(i, s, first):
                g = i * 2 + s
                for h in range(KH):
                    if h % 2 == 0:
                        act.wait_ge(s_h_ps, g * KH + h + 2)
                    if not first and h == 0:
                        act.wait_ge(s_y_ps, g - 1)
                    a.activation(hT[:, KH * s + h, :], ps[:, 2 + 2 * s + h // 2, GT * (h % 2):GT * (h % 2) + GT],
                                 ACT.Gelu, bias=b1g[:, s, h:h + 1]).then_inc(s_h, 1)

            def store_y(i, s):
                g = i * 2 + s
                act.wait_ge(s_y, g + 1)
                act.dma_start(out_groups[:, bass.ds(g * 2, 2), :], ysb[:, 2 * s:2 * s + 2, :]).then_inc(s_y_st[s], 16)
            gelu(0, 0, True)
            gelu(0, 1, True)
            store_y(0, 0)
            with act.Fori(1, PAIRS_D) as i:
                gelu(i, 0, False)
                store_y(i - 1, 1)
                gelu(i, 1, False)
                store_y(i, 0)
            store_y(PAIRS_D - 1, 1)

            for s in range(2):
                act.wait_ge(s_sent[s], PAIRS_E * 2 * TG * 16)
                stage_slots(s_slot_st2, 0, s, True, s_fetched)
            with act.Fori(1, PAIRS_E) as i:
                for s in range(2):
                    stage_slots(s_slot_st2, i, s, False, s_fetched)

        @block.tensor
        def _(pe):
            mm = nc.tensor.matmul

            def T(out_, in_, n):
                return nc.tensor.transpose(out_, in_, ident[0:n, 0:n])

            pe.wait_ge(s_pool_const, 5)
            pe.wait_ge(s_hist, 1)
            mm(ps[:, 4, 0:TILES], lower[:, :], hist[:, :], start=True, stop=True)
            mm(ps[:, 5, 0:TILES], ones[:, :], hist[:, :], start=True, stop=True).then_inc(s_prefix, 1)
            pe.wait_ge(s_ends, 1)
            T(ps[0:TILES, 6, 0:P], chunk_end[:, :], P).then_inc(s_ends_T, 1)
            pe.wait_ge(s_ge, 1)
            CQ = CH // 4
            for q in range(4):
                last = mm(ps[0:1, 4 + q, 0:CQ], ones_bf[0:TILES, 0:1], chunk_ge[0:TILES, q * CQ:(q + 1) * CQ],
                          start=True, stop=True)
            last.then_inc(s_ids, 1)

            pe.wait_ge(s_const_ld, 16 * 6)

            def round0(i, first):
                pe.wait_ge(s_xn0, i + 1)
                for t in range(T0):
                    for k in range(KD):
                        j = t * KD + k
                        last = T(ps[:, j // 4, R0 * (j % 4):R0 * (j % 4) + R0], xn0[:, t, k * P:(k + 1) * P], R0)
                last.then_inc(s_xT0_ps, 1)
                pe.wait_ge(s_xT0, i + 1)
                if not first:
                    pe.wait_ge(s_hw, i)
                for t in range(T0):
                    for k in range(KD):
                        last = mm(ps[0:R0, 2 + t // 2, D * (t % 2):D * (t % 2) + D], xT0[:, t * KD + k, :],
                                  Wg[:, k, :], start=(k == 0), stop=(k == KD - 1))
                last.then_inc(s_hw_ps, 1)
            round0(0, True)
            with pe.Fori(1, ROUNDS0) as i:
                round0(i, False)

            def agg_group(i, s, first):
                g = i * 2 + s
                pe.wait_ge(s_gathered[s], i * (GC * 16) + GC * 16)
                pe.wait_ge(s_onehot, g + 1)
                for q in range(GC // 4):
                    if not first:
                        pe.wait_ge(s_added, (g - 1) * (GC // 4) + q + 1)
                    for c in range(4):
                        n = s * GC + 4 * q + c
                        bank, half = 2 * q + c // 2, 256 * (c % 2)
                        last = mm(ps[:, bank, half:half + D], onehot_w[:, n, :], gathered[:, n, :], start=True, stop=True)
                    last.then_inc(s_agg, 1)
            pe.wait_ge(s_hw, ROUNDS0)
            agg_group(0, 0, True)
            agg_group(0, 1, False)
            with pe.Fori(1, PAIRS_B) as i:
                agg_group(i, 0, False)
                agg_group(i, 1, False)

            pe.wait_ge(s_added, PAIRS_B * 2 * (GC // 4))

            def router(g, s, first):
                pe.wait_ge(s_tok, g + 1)
                for t in range(TG):
                    tt, h = g * TG + t, t % 2
                    if not (first and t < 1):
                        pe.wait_ge(s_tok_T, tt)
                    for k in range(KD):
                        last = T(ps[:, h, k * P:(k + 1) * P], t_out[:, s * TG + t, k * P:(k + 1) * P], P)
                    last.then_inc(s_tok_T_ps, 1)
                    pe.wait_ge(s_tok_T, tt + 1)
                    if not (first and t < 1):
                        pe.wait_ge(s_logit, tt)
                    for k in range(KD):
                        last = mm(ps[:, 2 + h, 0:NE], t_T[:, KD * h + k, :], Wr_sb[:, k, :], start=(k == 0), stop=(k == KD - 1))
                    last.then_inc(s_logit_ps, 1)
            router(0, 0, True)
            router(1, 1, False)
            with pe.Fori(1, PAIRS_E) as i:
                router(i * 2, 0, False)
                router(i * 2 + 1, 1, False)

            pe.wait_ge(s_rhist, 1)
            mm(ps[:, 4, 0:NE], lower[:, :], small[:, 0:NE], start=True, stop=True)
            mm(ps[:, 5, 0:NE], ones[:, :], small[:, 0:NE], start=True, stop=True).then_inc(s_rprefix, 1)
            pe.wait_ge(s_slots, 1)

            def expert_T(i, s, first):
                pe.wait_ge(s_grp_ld[s], i * 80 + 80)
                for j in range(2):
                    for k in range(KD):
                        last = T(ps[:, s, k * GT + j * P:k * GT + (j + 1) * P], xs[:, 2 * s + j, k * P:(k + 1) * P], P)
                last.then_inc(s_xT_ps, 1)

            def expert_up(i, s, first):
                g = i * 2 + s
                pe.wait_ge(s_xT, g + 1)
                if not first:
                    pe.wait_ge(s_h, (g - 1) * KH)
                for h in range(KH):
                    for k in range(KD):
                        last = mm(ps[:, 2 + 2 * s + h // 2, GT * (h % 2):GT * (h % 2) + GT],
                                  W1g[:, KD * s + k, h * P:(h + 1) * P], xT[:, KD * s + k, :],
                                  start=(k == 0), stop=(k == KD - 1))
                    last.then_inc(s_h_ps, 1)

            def expert_down(i, s, first):
                g = i * 2 + s
                pe.wait_ge(s_h, g * KH + KH)
                if not first:
                    pe.wait_ge(s_y, g - 1)
                for j in range(2):
                    for h in range(KH):
                        last = mm(ps[:, 6 + s, j * D:(j + 1) * D], hT[:, KH * s + h, j * P:(j + 1) * P],
                                  W2g[:, KH * s + h, :], start=(h == 0), stop=(h == KH - 1))
                last.then_inc(s_y_ps, 1)

            expert_T(0, 0, True)
            expert_up(0, 0, True)
            expert_T(0, 1, True)
            expert_down(0, 0, True)
            expert_up(0, 1, True)
            expert_T(1, 0, False)
            expert_down(0, 1, True)
            expert_up(1, 0, False)
            expert_T(1, 1, False)
            expert_down(1, 0, False)
            expert_up(1, 1, False)
            with pe.Fori(2, PAIRS_D) as i:
                expert_T(i, 0, False)
                expert_down(i - 1, 1, False)
                expert_up(i, 0, False)
                expert_T(i, 1, False)
                expert_down(i, 0, False)
                expert_up(i, 1, False)
            expert_down(PAIRS_D - 1, 1, False)


def _prod(shape):
    n = 1
    for s in shape:
        n *= s
    return n


def kernel(**inputs):
    import numpy as _np
    import concourse.bacc as _bacc
    from concourse import mybir as _mybir
    from concourse.bass_utils import run_bass_kernel_spmd as _run

    nc = _bacc.Bacc("TRN2", target_bir_lowering=False, num_devices=1)
    b1 = _np.asarray(inputs["L0_ffn_b1"])
    given = {
        "x": inputs["x"], "src": inputs["src"], "dst": inputs["dst"], "edge_weight": inputs["edge_weight"],
        "gnn_W": inputs["L0_gnn_W"], "gnn_b": inputs["L0_gnn_b"], "gamma": inputs["L0_ffn_gamma"],
        "beta": inputs["L0_ffn_beta"], "Wr": inputs["L0_ffn_Wr"], "br": inputs["L0_ffn_br"],
        "W1": inputs["L0_ffn_W1"], "b1_cols": b1.reshape(b1.shape[0], -1, 128).transpose(0, 2, 1),
        "W2": inputs["L0_ffn_W2"], "b2": inputs["L0_ffn_b2"],
    }
    arrays, args = {}, []
    for name, value in given.items():
        a = _np.ascontiguousarray(value)
        arrays[f"in_{name}"] = a
        args.append(nc.dram_tensor(f"in_{name}", a.shape, _mybir.dt.from_np(a.dtype), kind="ExternalInput").ap())
    out = nc.dram_tensor("out", arrays["in_x"].shape, f32, kind="ExternalOutput").ap()
    gnn_moe(nc, *args, out)
    r = _run(nc, [arrays], core_ids=[0])
    return r.results[0]["out"]
```

```python
import concourse.bass as bass
from concourse import mybir
from contextlib import ExitStack

f32 = mybir.dt.float32
bf16 = mybir.dt.bfloat16
i32 = mybir.dt.int32
ALU = mybir.AluOpType
ACT = mybir.ActivationFunctionType
AX = mybir.AxisListType


class Steps:

    def __init__(self, engine, semaphore):
        self.engine, self.semaphore = engine, semaphore
        self.before, self.base, self.n = 0, 0, 0

    def __call__(self, instruction, held=None):
        self.n += 1
        instruction.then_inc(self.semaphore, 1)
        self.engine.wait_ge(self.semaphore, self.base + self.n)
        if held is not None:
            self.engine.sem_inc(held, 1)

    def enter(self, i, first, per_round):
        self.before, self.base, self.n, self.per_round = self.before + self.n, 0, 0, per_round
        self.base = (i - first) * per_round + self.before

    def leave(self, rounds):
        assert self.n == self.per_round, (self.n, self.per_round)
        self.before, self.base, self.n = self.before + rounds * self.per_round, 0, 0
        self.base = self.before
        self.before = self.before

    def straight(self):
        self.base = self.before


def ceil_div(a, b):
    return -(-a // b)


def _prod(shape):
    n = 1
    for s in shape:
        n *= s
    return n


def carve(region, parts):
    at, views = 0, []
    for shape, dt in parts:
        words = ceil_div(int(mybir.dt.size(dt)) * _prod(shape), 4)
        v = region[:, at:at + words]
        if dt != f32:
            v = v.bitcast(dt)
        v = v[:, 0:_prod(shape)]
        if len(shape) == 2:
            v = v.rearrange("p (a b) -> p a b", a=shape[0])
        if len(shape) == 3:
            v = v.rearrange("p (a b c) -> p a b c", a=shape[0], b=shape[1])
        views.append(v)
        at += words
    assert at <= region.shape[1], (at, region.shape)
    return views


def gnn_moe(nc, x, src, dst, edge_weight, gnn_W, gnn_b, gamma, beta, Wr, br, W1, b1_cols, W2, b2, out):
    P = 128
    N, D = x.shape
    E_EDGES = src.shape[0]
    NE, _, H = W1.shape
    KD, KH = D // P, H // P
    EPS = 1e-5

    TILES = ceil_div(N, P)
    PAIRS = TILES // 2
    LAST = N - (TILES - 1) * P
    R0, T0 = 125, 4
    ROUNDS0 = N // (R0 * T0)
    COLS = E_EDGES // P
    TAIL = E_EDGES - COLS * P
    BC = 20
    BLOCKS = ceil_div(COLS + 1, BC)
    EC = (BLOCKS + 1) * BC
    assert BLOCKS % 2 == 0 and 0 < TAIL < P
    NOBUCKET = 127
    W_ = BC + 2
    SL = 64
    CPT = 19
    CAP = CPT * P
    PAGES = CAP // SL
    PACK = 1 << 14
    GT = 256
    PARTS = [(0, 14), (14, 34), (34, PAIRS)]

    def groups_of(a, b):
        real = 2 * (min(b * 2 * P, N) - a * 2 * P)
        return (real + NE * (GT - 1)) // GT

    LATER = 3
    FFN_STEPS = [(PARTS[0][1] + LATER, PARTS[1][1] + 1, 2), (PARTS[1][1] + LATER, PAIRS, 4)]
    NG = [(b - a) * m for a, b, m in FFN_STEPS] + [ceil_div(groups_of(*PARTS[2]), 2) * 2]
    for n, part in zip(NG, PARTS):
        assert n >= groups_of(*part), (n, groups_of(*part))
    assert FFN_STEPS[0][1] <= FFN_STEPS[1][0]
    G0 = [0, NG[0], NG[0] + NG[1]]
    GROUPS = sum(NG)
    SLOTS = GROUPS * GT
    MAXT = max(2 * (b - a) for a, b in PARTS)

    ctx = ExitStack()
    with ctx:
        def sb(name, shape, dt=f32):
            return ctx.enter_context(nc.sbuf_tensor(name, shape, dt))

        def sem(name):
            return ctx.enter_context(nc.semaphore(name))

        def sem2(name):
            return [sem(f"{name}{s}") for s in range(2)]

        features = nc.dram_tensor("features", [N + 1, D], f32, kind="Internal").ap()
        sums = nc.dram_tensor("sums", [(NOBUCKET + 1) * P, D], f32, kind="Internal").ap()
        pages = nc.dram_tensor("pages", [TILES * PAGES, SL * 2], f32, kind="Internal").ap()
        tokens = nc.dram_tensor("tokens", [TILES * P, D], f32, kind="Internal").ap()
        residual = nc.dram_tensor("residual", [TILES * P, D], f32, kind="Internal").ap()
        expert_in = nc.dram_tensor("expert_in", [SLOTS, D], f32, kind="Internal").ap()
        expert_out = nc.dram_tensor("expert_out", [SLOTS, D], f32, kind="Internal").ap()

        ident, lower, ones, iota_row = sb("ident", [P, P]), sb("lower", [P, P]), sb("ones", [P, P]), sb("iota_row", [P, P])
        lower_bf, ones_bf = sb("lower_bf", [P, P], bf16), sb("ones_bf", [P, P], bf16)
        zeros = sb("zeros", [P, D])
        Wg = sb("Wg", [P, KD, D])
        Wr_sb = sb("Wr_sb", [P, KD, NE])
        rows = sb("rows", [P, 3, D])
        br_row = sb("br_row", [P, NE])
        eps = sb("eps", [P, 1])
        real_row = sb("real_row", [P, 1])
        page_last = sb("page_last", [P, 1])
        group_ids = sb("group_ids", [1, GROUPS], i32)
        logits = sb("logits", [P, TILES, NE])
        slot = sb("slot", [P, TILES, 2], i32)
        gate = sb("gate", [P, 2, TILES])
        small0 = sb("small0", [P, 64])
        small = sb("small", [P, 64])

        ARENA = 42800
        U = sb("U", [P, ARENA])
        ps = ctx.enter_context(nc.psum_tensor("ps", [P, 8, 512], f32))

        (xin, xn0, xT0, hw_sb, src_raw, dst_raw, w_raw, fields, hi, bucket_no, oh_a, oh_b, reset, cum, prod,
         ohf_a, ohf_b, M_a, M_b, at_a, at_b) = carve(U, [
            ((T0, D), f32), ((T0, D), f32), ((T0 * KD, R0), f32), ((T0, D), f32),
            ((COLS + 1,), i32), ((COLS + 1,), i32), ((COLS + 1,), f32), ((EC, 2), f32), ((EC,), bf16),
            ((TILES, BC), bf16), ((TILES, W_), bf16), ((TILES, W_), bf16), ((TILES * W_,), bf16), ((TILES, W_), bf16),
            ((TILES, BC), bf16), ((TILES, BC), f32), ((TILES, BC), f32), ((BC, 2 * SL + 1), f32), ((BC, 2 * SL + 1), f32),
            ((BC, SL), f32), ((BC, SL), f32)])
        xin, xn0, hw_sb = xin[0:R0, :, :], xn0[0:R0, :, :], hw_sb[0:R0, :, :]
        oh, ohf, M, at_slot = (oh_a, oh_b), (ohf_a, ohf_b), (M_a, M_b), (at_a, at_b)
        seen = sb("seen", [P, TILES], i32)
        wrap = sb("wrap", [P, BC])
        slot_of = sb("slot_of", [P, BC])
        edge_f = [sb(f"edge_f{s}", [P, BC, 2]) for s in range(2)]
        lists = [sb(f"lists{s}", [P, 2 * SL + 1]) for s in range(2)]
        page = [sb(f"page{s}", [P, 2 * SL]) for s in range(2)]
        page_row = [sb(f"page_row{s}", [P, 1], i32) for s in range(2)]
        part_page, here, late, kept = (sb("part_page", [P, 2 * SL]), sb("here", [P, SL]), sb("late", [P, 2 * SL]),
                                       sb("kept", [P, 2 * SL]))
        st = sb("st", [P, 8])

        (c_src, c_dst, c_edge, c_wide, c_same, c_feat, c_sum, c_word) = carve(U[:, 9100:9100 + 1200], [
            ((1,), i32), ((1,), i32), ((2,), f32), ((P,), f32), ((P,), f32), ((D,), f32), ((D,), f32), ((TILES,), i32)])
        flag, over_sum = sb("flag", [1, 1], i32), sb("over_sum", [1, 1])

        (rec, row_word, src_row, row_f, gathered, onehot_w, xpair, norm, tok, tokT, W1g, W2g, b2g, b1g, xs, xT, hT, ysb,
         tok_ring, y_ring, out_ring) = carve(U, [
            ((TILES * CPT, 2), f32), ((TILES * CPT,), i32), ((TILES * CPT,), i32), ((TILES * CPT,), f32),
            ((2 * CPT, D), f32), ((2 * CPT, P), f32), ((4, D), f32), ((2, D), f32), ((4, D), f32), ((2 * KD, P), f32),
            ((2 * KD, H), f32), ((2 * KH, D), f32), ((2, D), f32), ((2, KH), f32), ((4, D), f32), ((KD, GT), f32),
            ((KH, GT), f32), ((4, D), f32), ((4, D), f32), ((8, D), f32), ((4, D), f32)])
        idx = [sb(f"idx{s}", [P, CPT], i32) for s in range(2)]
        row_w = [sb(f"row_w{s}", [P, CPT, 2]) for s in range(2)]
        slot_st = [sb(f"slot_st{s}", [P, 2, 2], i32) for s in range(2)]
        KM = 2 * MAXT
        (eq, score, oh12, rdata, rreset, rcum, rlog) = carve(
            sb("route", [P, 4640]),
            [((MAXT, NE), f32), ((MAXT, NE), f32), ((KM, NE), f32), ((NE, KM + 1), f32), ((NE * (KM + 1),), bf16),
             ((NE, KM + 1), f32), ((MAXT, NE), f32)])
        m1, m2, pick = sb("m1", [P, MAXT]), sb("m2", [P, MAXT]), sb("pick", [P, MAXT])
        falling = sb("falling", [P, NE])
        rsmall = sb("rsmall", [P, 3, NE])
        rcount = sb("rcount", [P, NE], i32)

        AGG, TOKT, LOGIT, XT, HB, YB = 0, 2, 3, 4, 5, 7

        (s_const_ld, s_edge_ld, s_pool_const, s_zero, s_cleared, s_held) = map(
            sem, "s_const_ld s_edge_ld s_pool_const s_zero s_cleared s_held".split())
        s_dve, s_pool = sem("s_dve"), sem("s_pool")
        s_oh, s_base, s_ohf, s_slot_of, s_m1, s_m2, s_main, s_lists = map(
            sem, "s_oh s_base s_ohf s_slot_of s_m1 s_m2 s_main s_lists".split())
        s_listed = sem("s_listed")
        s_page_st = sem2("s_page_st")
        s_over, s_over_ps, s_flag = map(sem, "s_over s_over_ps s_flag".split())
        (s_sums_zero, s_column, s_wide_T, s_same, s_column_ps, s_feat_ld, s_sum_ld, s_column_sum, s_column_st,
         s_sums_copied, s_sum_words, s_column_dve) = map(sem, (
             "s_sums_zero s_column s_wide_T s_same s_column_ps s_feat_ld s_sum_ld s_column_sum s_column_st "
             "s_sums_copied s_sum_words s_column_dve").split())
        s_xin, s_var0, s_std0, s_xn0, s_xT0_ps, s_xT0, s_hw_ps, s_hw, s_hw_st = map(
            sem, "s_xin s_var0 s_std0 s_xn0 s_xT0_ps s_xT0 s_hw_ps s_hw s_hw_st".split())
        s_rec_ld, s_split, s_staged, s_onehot, s_agg, s_x1, s_var, s_std, s_tok = map(
            sem, "s_rec_ld s_split s_staged s_onehot s_agg s_x1 s_var s_std s_tok".split())
        s_tokT_ps, s_tokT, s_logit_ps, s_logit = map(sem, "s_tokT_ps s_tokT s_logit_ps s_logit".split())
        s_gathered, s_x_ld, s_res_st, s_tok_st = map(sem2, "s_gathered s_x_ld s_res_st s_tok_st".split())
        s_rhist, s_rprefix, s_gap, s_exp, s_routed = map(sem, "s_rhist s_rprefix s_gap s_exp s_routed".split())
        s_exp_zero = sem("s_exp_zero")
        s_tok_ld, s_sent = sem2("s_tok_ld"), sem2("s_sent")
        s_xT_ps, s_xT, s_h_ps, s_h, s_y_ps, s_y = map(sem, "s_xT_ps s_xT s_h_ps s_h s_y_ps s_y".split())
        s_ld1, s_ld2, s_y_st = map(sem2, "s_ld1 s_ld2 s_y_st".split())
        s_fetch_ld, s_fetched, s_out_st = map(sem2, "s_fetch_ld s_fetched s_out_st".split())
        s_out = sem("s_out")

        def hold(engine, semaphore, value):
            engine.wait_ge(semaphore, value)
            engine.sem_inc(s_held, 1)

        x_rounds = x.rearrange("(t p) d -> p t d", p=R0)
        feat_rounds = features[1:N + 1, :].rearrange("(t p) d -> p t d", p=R0)
        page_words = pages.rearrange("r w -> (r w)").rearrange("(t p w) -> p t w", t=TILES, p=P)
        x_tiles = x[0:(TILES - 1) * P, :].rearrange("(t p) d -> p t d", p=P)
        out_tiles = out[0:(TILES - 1) * P, :].rearrange("(t p) d -> p t d", p=P)
        tok_tiles = tokens.rearrange("(t p) d -> p t d", p=P)
        res_tiles = residual.rearrange("(t p) d -> p t d", p=P)
        in_rows = expert_in.rearrange("(g p) d -> p g d", p=P)
        out_rows = expert_out.rearrange("(g p) d -> p g d", p=P)
        W1_e = W1.rearrange("e (k p) h -> p (e k) h", p=P)
        W2_e = W2.rearrange("e (k p) d -> p (e k) d", p=P)

        RUNS = [(0, 1, 0, 0, None), (1, PARTS[0][1] + 1, 0, 0, 0), (PARTS[0][1] + 1, FFN_STEPS[0][0], 0, 0, None),
                (FFN_STEPS[0][0], FFN_STEPS[0][0] + 1, 2, 0, None),
                (FFN_STEPS[0][0] + 1, FFN_STEPS[0][1], 2, 2, 1), (FFN_STEPS[0][1], FFN_STEPS[1][0], 0, 0, None),
                (FFN_STEPS[1][0], PAIRS - 1, 4, G0[1], None), (PAIRS - 1, PAIRS, 4, G0[1] + 4 * (PAIRS - 1 - FFN_STEPS[1][0]), None)]

        MIXED = PARTS[1][1] // 2

        def run_steps(engine, body, routed=None, own=None, per_step=None, begin=None):
            for a, b, m, g0, part in RUNS:
                if begin is not None:
                    begin(a)
                if b - a == 1:
                    body(a, [g0 + k for k in range(m)])
                elif b > a:
                    with engine.Fori(a, b) as p:
                        if own is not None:
                            own.enter(p, a, per_step)
                        body(p, [(p - a) * m + g0 + k for k in range(m)])
                    if own is not None:
                        own.leave(b - a)
                if part is not None and routed is not None:
                    routed(part)

        def is_first(p):
            return isinstance(p, int) and p == 0

        def is_last(p):
            return isinstance(p, int) and p == PAIRS - 1

        def overflowed(engine):
            engine.wait_ge(s_flag, 1)
            return engine.value_load(flag[0:1, 0:1], min_val=0, max_val=2 * P)

        block = ctx.enter_context(nc.Block())

        @block.sync
        def _(sp):
            sp.wait_ge(s_zero, 1)
            for raw, arr in ((src_raw, src), (dst_raw, dst), (w_raw, edge_weight)):
                sp.dma_start(raw[:, 0:COLS], arr[0:COLS * P].rearrange("(p c) -> p c", p=P)).then_inc(s_edge_ld, 16)
                sp.dma_start(raw[0:TAIL, COLS:COLS + 1],
                             arr[COLS * P:E_EDGES].rearrange("(p c) -> p c", c=1)).then_inc(s_edge_ld, 16)
            sp.dma_start(Wg[:, :, :], gnn_W.rearrange("(k p) n -> p k n", p=P)).then_inc(s_const_ld, 16)
            sp.dma_start(Wr_sb[:, :, :], Wr.rearrange("(k p) n -> p k n", p=P)).then_inc(s_const_ld, 16)
            for k, row in enumerate((gnn_b, gamma, beta)):
                sp.dma_start(rows[:, k, :], row.partition_broadcast(P)).then_inc(s_const_ld, 16)
            sp.dma_start(br_row[:, :], br.partition_broadcast(P)).then_inc(s_const_ld, 16)
            for q in range(PAGES // 2):
                rows_q = TILES * 2
                sp.dma_start(pages[q * rows_q:q * rows_q + 112, :], zeros[0:112, 0:2 * SL]).then_inc(s_cleared, 16)
                sp.dma_start(pages[q * rows_q + 112:(q + 1) * rows_q, :], zeros[0:rows_q - 112, 0:2 * SL]).then_inc(s_cleared, 16)
            sp.dma_start(features[0:1, :], zeros[0:1, :]).then_inc(s_cleared, 16)

            def load_round0(i, first):
                if not first:
                    sp.wait_ge(s_xn0, i)
                sp.dma_start(xin, x_rounds[:, bass.ds(i * T0, T0), :]).then_inc(s_xin, 16)
            load_round0(0, True)
            with sp.Fori(1, ROUNDS0) as i:
                load_round0(i, False)

            with sp.Fori(0, GROUPS // 2) as i:
                sp.dma_start(in_rows[:, bass.ds(i * 4, 4), :],
                             zeros[:, None, :].broadcast_to([P, 4, D])).then_inc(s_exp_zero, 16)

            for s in range(2):
                sp.wait_ge(s_page_st[s], 16 * (BLOCKS // 2 + (s == 0)))
            sp.wait_ge(s_hw_st, 16 * ROUNDS0)
            TQ = TILES // 2
            for q in range(2):
                sp.dma_start(rec.rearrange("p (t c) f -> p t (c f)", t=TILES)[:, q * TQ:(q + 1) * TQ, :],
                             page_words[:, q * TQ:(q + 1) * TQ, :]).then_inc(s_rec_ld, 16)

            with sp.If(overflowed(sp) > 0):
                for z in range(0, NOBUCKET + 1, 4):
                    sp.dma_start(sums.rearrange("(t p) d -> p t d", p=P)[:, z:z + 4, :],
                                 zeros[:, None, :].broadcast_to([P, 4, D])).then_inc(s_sums_zero, 16)
                sp.wait_ge(s_column_st, 16 * (COLS + 1))
                sp.dma_start(features[1:N + 1, :], sums[0:N, :]).then_inc(s_sums_copied, 16)

            def load_up(g, h):
                e = sp.value_load(group_ids[0:1, bass.ds(g, 1)], min_val=0, max_val=NE - 1)
                if not (isinstance(g, int) and g < 2):
                    hold(sp, s_h, (g - 1) * KH)
                sp.dma_start(xs[:, 2 * h:2 * h + 2, :], in_rows[:, bass.ds(g * 2, 2), :]).then_inc(s_ld1[h], 16)
                sp.dma_start(W1g[:, KD * h:KD * h + KD, :], W1_e[:, bass.ds(e * KD, KD), :]).then_inc(s_ld1[h], 16)
                sp.dma_start(b1g[:, h, :], b1_cols[bass.ds(e, 1), :, :].rearrange("a p k -> p (a k)")).then_inc(s_ld1[h], 16)

            def load_down(g, h):
                e = sp.value_load(group_ids[0:1, bass.ds(g, 1)], min_val=0, max_val=NE - 1)
                if not (isinstance(g, int) and g < 2):
                    hold(sp, s_y, g - 1)
                sp.dma_start(W2g[:, KH * h:KH * h + KH, :], W2_e[:, bass.ds(e * KH, KH), :]).then_inc(s_ld2[h], 16)
                sp.dma_start(b2g[:, h:h + 1, :], b2[bass.ds(e, 1), :].partition_broadcast(P)).then_inc(s_ld2[h], 16)

            def store_pair(p, first):
                sp.wait_ge(s_tok, p + 1)
                sp.dma_start(res_tiles[:, bass.ds(p * 2, 2), :], xpair[:, 0:2, :]).then_inc(s_res_st[0], 16)
                sp.dma_start(tok_tiles[:, bass.ds(p * 2, 2), :], tok[:, 0:2, :]).then_inc(s_tok_st[0], 16)

            def sp_step(p, groups):
                m = len(groups)
                for k, g in enumerate(groups[:m // 2]):
                    load_up(g, k % 2)
                    if k == 0:
                        load_down(g, 0)
                if m == 4:
                    load_down(groups[1], 1)
                for k, g in enumerate(groups[m // 2:]):
                    load_up(g, (m // 2 + k) % 2)
                    if not (m == 2):
                        load_down(g, (m // 2 + k) % 2)
                if m == 2:
                    load_down(groups[1], 1)

            def sp_step_all(p, groups):
                sp_step(p, groups)
                if not is_first(p):
                    store_pair(p - 1, False)
                if not is_first(p):
                    sp.wait_ge(s_res_st[0], p * 16)
                load_x_single(p)

            def load_x_single(p):
                if is_last(p):
                    sp.dma_start(xpair[:, 0, :], x[(TILES - 2) * P:(TILES - 1) * P, :]).then_inc(s_x_ld[0], 16)
                    sp.dma_start(xpair[0:LAST, 1, :], x[(TILES - 1) * P:N, :]).then_inc(s_x_ld[0], 16)
                else:
                    sp.dma_start(xpair[:, 0:2, :], x_tiles[:, bass.ds(p * 2, 2), :]).then_inc(s_x_ld[0], 16)

            def load_dispatch(j, h, first):
                if not first:
                    sp.wait_ge(s_sent[h], (j - h) * 32)
                sp.dma_start(tok_ring[:, 2 * h:2 * h + 2, :], tok_tiles[:, bass.ds(j * 2, 2), :]).then_inc(s_tok_ld[h], 16)
                sp.dma_start(slot_st[h][:, :, :], slot[:, bass.ds(j * 2, 2), :]).then_inc(s_tok_ld[h], 16)

            def dispatch(part):
                a, b = PARTS[part]
                sp.wait_ge(s_routed, part + 1)
                sp.wait_ge(s_tok_st[0], b * 16)
                n = (b - a) // 2
                if a == 0:
                    load_dispatch(0, 0, True)
                    load_dispatch(1, 1, True)
                with sp.Fori(1 if a == 0 else 0, n) as i:
                    load_dispatch(i * 2 + a, 0, False)
                    load_dispatch(i * 2 + (a + 1), 1, False)
                if (b - a) % 2:
                    load_dispatch(b - 1, 0, False)

            def tokens_sent(p):
                for part in range(2):
                    if p == FFN_STEPS[part][0]:
                        for s in range(2):
                            sp.wait_ge(s_sent[s], 64 * PARTS[part][1] // 2)

            run_steps(sp, sp_step_all, dispatch, begin=tokens_sent)
            store_pair(PAIRS - 1, False)
            dispatch(2)

            def load_final(j, h, first):
                if not first:
                    hold(sp, s_out, j - 1)
                    sp.wait_ge(s_out_st[h], (j - h) * 8)
                sp.dma_start(out_ring[:, 2 * h:2 * h + 2, :], res_tiles[:, bass.ds(j * 2, 2), :]).then_inc(s_fetch_ld[h], 16)
                sp.dma_start(slot_st[h][:, :, :], slot[:, bass.ds(j * 2, 2), :]).then_inc(s_fetch_ld[h], 16)

            def store_final(j, h):
                sp.wait_ge(s_out, j + 1)
                sp.dma_start(out_tiles[:, bass.ds(j * 2, 2), :], out_ring[:, 2 * h:2 * h + 2, :]).then_inc(s_out_st[h], 16)

            for s in range(2):
                sp.wait_ge(s_sent[s], 64 * (ceil_div(PAIRS, 2) if s == 0 else PAIRS // 2))
            g2 = G0[2]
            load_up(g2, 0)
            load_down(g2, 0)
            load_up(g2 + 1, 1)
            load_down(g2 + 1, 1)
            load_final(0, 0, True)
            load_final(1, 1, True)
            with sp.Fori(1, MIXED) as i:
                load_up(i * 2 + g2, 0)
                store_final(i * 2 - 2, 0)
                load_final(i * 2, 0, False)
                load_down(i * 2 + g2, 0)
                load_up(i * 2 + (g2 + 1), 1)
                store_final(i * 2 - 1, 1)
                load_final(i * 2 + 1, 1, False)
                load_down(i * 2 + (g2 + 1), 1)
            for i in range(MIXED, NG[2] // 2):
                for h in range(2):
                    load_up(g2 + 2 * i + h, h)
                    load_down(g2 + 2 * i + h, h)
            j = 2 * MIXED
            store_final(j - 2, 0)
            load_final(j, 0, False)
            store_final(j - 1, 1)
            load_final(j + 1, 1, False)
            with sp.Fori(MIXED + 1, PAIRS // 2) as i:
                store_final(i * 2 - 2, 0)
                load_final(i * 2, 0, False)
                store_final(i * 2 - 1, 1)
                load_final(i * 2 + 1, 1, False)
            store_final(PAIRS - 3, 0)
            load_final(PAIRS - 1, 0, False)
            store_final(PAIRS - 2, 1)
            sp.wait_ge(s_out, PAIRS)
            sp.dma_start(out[(TILES - 2) * P:(TILES - 1) * P, :], out_ring[:, 0, :]).then_inc(s_out_st[0], 16)
            sp.dma_start(out[(TILES - 1) * P:N, :], out_ring[0:LAST, 1, :]).then_inc(s_out_st[0], 16)
            sp.wait_ge(s_out_st[0], 16 * (PAIRS // 2 + 2))
            sp.wait_ge(s_out_st[1], 16 * (PAIRS // 2))

        @block.gpsimd
        def _(pool):
            q = nc.gpsimd
            own = Steps(pool, s_pool)
            q.memset(ident[:, :], 0.0)
            q.memset(ones[:, :], 1.0)
            q.iota(page_last[:, :], pattern=[[0, 1]], base=PAGES - 1, channel_multiplier=PAGES, allow_small_or_imprecise_dtypes=True)
            own(q.iota(iota_row[:, :], pattern=[[1, P]], base=0, channel_multiplier=0, allow_small_or_imprecise_dtypes=True))
            q.affine_select(out=ident[:, :], in_=ident[:, :], compare_op=ALU.not_equal, fill=1.0,
                            base=0, pattern=[[-1, P]], channel_multiplier=1)
            q.affine_select(out=real_row[:, :], in_=ones[:, 0:1], compare_op=ALU.is_gt, fill=0.0,
                            base=LAST, pattern=[[0, 1]], channel_multiplier=-1)
            q.memset(kept[:, :], 0.0)
            q.memset(st[:, 0:4], 0.0)
            q.memset(st[:, 5:8], 0.0)
            q.iota(st[:, 4:5], pattern=[[0, 1]], base=0, channel_multiplier=PAGES, allow_small_or_imprecise_dtypes=True)
            for s in range(2):
                q.memset(M[s][:, :, 2 * SL:2 * SL + 1], 1.0)
            own(q.affine_select(out=lower[:, :], in_=ones[:, :], compare_op=ALU.is_gt, fill=0.0,
                                base=0, pattern=[[1, P]], channel_multiplier=-1))
            pool.sem_inc(s_pool_const, 1)

            def weights(k, s, first):
                hold(pool, s_slot_of, k + 1)
                if not first:
                    hold(pool, s_main, k - 1)
                q.tensor_tensor(M[s][:, :, 1:2 * SL:2], at_slot[s], edge_f[s][:, :, 1:2].broadcast_to([P, BC, SL]),
                                ALU.mult).then_inc(s_m2, 1)

            T = TILES

            def list_pages(k, s, first):
                hold(pool, s_lists, k + 1)
                if not first:
                    hold(pool, s_page_st[s], (k - s) * 8)
                ls = lists[s][0:T, :]
                pairs = ls[:, 0:2 * SL].rearrange("p (a f) -> p a f", f=2)
                fill, filled, full, still, number, peak = (st[0:T, j:j + 1] for j in range(6))
                q.tensor_scalar(here[0:T, :], iota_row[0:T, 0:SL], fill, None, ALU.is_ge)
                own(q.tensor_tensor(filled, fill, ls[:, 2 * SL:2 * SL + 1], ALU.add), s_held)
                q.tensor_scalar(full, filled, float(SL), None, ALU.is_ge)
                q.tensor_scalar(still, filled, float(SL), None, ALU.is_lt)
                own(q.tensor_tensor(part_page[0:T, :].rearrange("p (a f) -> p a f", f=2), pairs,
                                    here[0:T, :, None].broadcast_to([T, SL, 2]), ALU.mult), s_held)
                q.tensor_scalar(page_row[s][0:T, :], number, page_last[0:T, :], None, ALU.min)
                q.tensor_scalar(peak, peak, ls[:, 2 * SL:2 * SL + 1], None, ALU.max)
                q.tensor_tensor(late[0:T, :], ls[:, 0:2 * SL], part_page[0:T, :], ALU.subtract)
                own(q.tensor_tensor(page[s][0:T, :], kept[0:T, :], part_page[0:T, :], ALU.add), s_held)
                if not (first and s == 0):
                    hold(pool, s_page_st[1 - s], (k + s) * 8 if s == 0 else (k + 1) * 8)
                q.indirect_dma_start(out=pages[:, :], out_offset=bass.IndirectOffsetOnAxis(ap=page_row[s][0:T, 0:1], axis=0),
                                     in_=page[s][0:T, :], in_offset=None, compute_op=ALU.bypass).then_inc(s_page_st[s], 16)
                q.tensor_tensor(number, number, full, ALU.add)
                own(q.tensor_scalar(kept[0:T, :], page[s][0:T, :], still, None, ALU.mult), s_held)
                q.tensor_scalar(full, full, -float(SL), None, ALU.mult)
                own(q.tensor_tensor(kept[0:T, :], kept[0:T, :], late[0:T, :], ALU.add), s_held)
                own(q.tensor_tensor(fill, filled, full, ALU.add), s_held)
                pool.sem_inc(s_listed, 1)

            SP_ = 6
            pool.wait_ge(s_cleared, 16 * (PAGES + 1))
            weights(0, 0, True)
            weights(1, 1, True)
            list_pages(0, 0, True)
            weights(2, 0, False)
            list_pages(1, 1, True)
            with pool.Fori(1, BLOCKS // 2 - 1) as i:
                own.enter(i, 1, 2 * SP_)
                weights(i * 2 + 1, 1, False)
                list_pages(i * 2, 0, False)
                weights(i * 2 + 2, 0, False)
                list_pages(i * 2 + 1, 1, False)
            own.leave(BLOCKS // 2 - 2)
            weights(BLOCKS - 1, 1, False)
            list_pages(BLOCKS - 2, 0, False)
            list_pages(BLOCKS - 1, 1, False)
            pool.wait_ge(s_page_st[0], 16 * (BLOCKS // 2))
            pool.wait_ge(s_page_st[1], 16 * (BLOCKS // 2))
            own(q.tensor_scalar(page_row[0][0:T, :], st[0:T, 4:5], page_last[0:T, :], None, ALU.min))
            q.indirect_dma_start(out=pages[:, :], out_offset=bass.IndirectOffsetOnAxis(ap=page_row[0][0:T, 0:1], axis=0),
                                 in_=kept[0:T, :], in_offset=None, compute_op=ALU.bypass).then_inc(s_page_st[0], 16)

            over = st[0:T, 6:8]
            q.tensor_scalar(over[:, 0:1], st[0:T, 5:6], float(SL), None, ALU.is_gt)
            q.tensor_scalar(over[:, 1:2], st[0:T, 4:5], page_last[0:T, :], None, ALU.is_gt).then_inc(s_over, 1)

            pool.wait_ge(s_hw_st, 16 * ROUNDS0)

            def column(c, first):
                hold(pool, s_column, c + 1)
                q.indirect_dma_start(out=c_feat[:, :], out_offset=None, in_=features[:, :],
                                     in_offset=bass.IndirectOffsetOnAxis(ap=c_dst[:, 0:1], axis=0),
                                     compute_op=ALU.bypass).then_inc(s_feat_ld, 16)
                q.indirect_dma_start(out=c_sum[:, :], out_offset=None, in_=sums[:, :],
                                     in_offset=bass.IndirectOffsetOnAxis(ap=c_src[:, 0:1], axis=0),
                                     compute_op=ALU.bypass).then_inc(s_sum_ld, 16)
                hold(pool, s_column_sum, c + 1)
                q.indirect_dma_start(out=sums[:, :], out_offset=bass.IndirectOffsetOnAxis(ap=c_src[:, 0:1], axis=0),
                                     in_=c_sum[:, :], in_offset=None, compute_op=ALU.bypass).then_inc(s_column_st, 16)

            with pool.If(overflowed(pool) > 0):
                q.iota(c_word[:, :], pattern=[[P, TILES]], base=1, channel_multiplier=PACK + 1).then_inc(s_sum_words, 1)
                pool.wait_ge(s_sums_zero, 16 * (NOBUCKET + 1) // 4)
                column(0, True)
                with pool.Fori(1, COLS + 1) as c:
                    column(c, False)
                pool.wait_ge(s_sums_copied, 16)

            def gather_tile(p, s):
                if not is_first(p):
                    hold(pool, s_agg, p * 2 + (s - 1))
                hold(pool, s_staged, p * 2 + (s + 1))
                for c in range(CPT):
                    q.indirect_dma_start(
                        out=gathered[:, s * CPT + c, :], out_offset=None, in_=features[:, :],
                        in_offset=bass.IndirectOffsetOnAxis(ap=idx[s][:, c:c + 1], axis=0),
                        compute_op=ALU.bypass).then_inc(s_gathered[s], 16)

            def gather_pair(p):
                gather_tile(p, 0)
                gather_tile(p, 1)

            def send(j, h, last):
                hold(pool, s_tok_ld[h], (j + (2 - h)) * 16)
                for t in range(2):
                    parts = LAST if last and t == 1 else P
                    for k in range(2):
                        q.indirect_dma_start(
                            out=expert_in[:, :],
                            out_offset=bass.IndirectOffsetOnAxis(ap=slot_st[h][0:parts, t, k:k + 1], axis=0),
                            in_=tok_ring[0:parts, 2 * h + t, :], in_offset=None,
                            compute_op=ALU.bypass).then_inc(s_sent[h], 16)

            def send_part(part):
                a, b = PARTS[part]
                with pool.Fori(0, (b - a) // 2) as i:
                    send(i * 2 + a, 0, False)
                    send(i * 2 + (a + 1), 1, False)
                if (b - a) % 2:
                    send(b - 1, 0, b == PAIRS)

            def gather_run(a, b):
                if a == 0:
                    gather_pair(0)
                    a = 1
                with pool.Fori(a, b) as p:
                    gather_pair(p)
            gather_run(0, PARTS[0][1] + 2)
            pool.wait_ge(s_exp_zero, 16 * (GROUPS // 2))
            send_part(0)
            gather_run(PARTS[0][1] + 2, PARTS[1][1] + 2)
            send_part(1)
            gather_run(PARTS[1][1] + 2, PAIRS)
            send_part(2)

            def fetch(j, h, first, last, answers):
                if not first:
                    hold(pool, s_out, j - 1)
                hold(pool, s_fetch_ld[h], (j + (2 - h)) * 16)
                for t in range(2):
                    parts = LAST if last and t == 1 else P
                    for k in range(2):
                        q.indirect_dma_start(
                            out=y_ring[0:parts, 4 * h + 2 * t + k, :], out_offset=None, in_=answers,
                            in_offset=bass.IndirectOffsetOnAxis(ap=slot_st[h][0:parts, t, k:k + 1], axis=0),
                            compute_op=ALU.bypass).then_inc(s_fetched[h], 16)
            for s in range(2):
                pool.wait_ge(s_y_st[s], 16 * (G0[2] // 2))
            earlier = expert_out[0:G0[2] * GT, :]
            fetch(0, 0, True, False, earlier)
            fetch(1, 1, True, False, earlier)
            with pool.Fori(1, MIXED) as i:
                fetch(i * 2, 0, False, False, earlier)
                fetch(i * 2 + 1, 1, False, False, earlier)
            for s in range(2):
                pool.wait_ge(s_y_st[s], 16 * (GROUPS // 2))
            with pool.Fori(MIXED, PAIRS // 2) as i:
                fetch(i * 2, 0, False, False, expert_out[:, :])
                fetch(i * 2 + 1, 1, False, False, expert_out[:, :])
            fetch(PAIRS - 1, 0, False, True, expert_out[:, :])

        @block.vector
        def _(dve):
            v = nc.vector
            step = Steps(dve, s_dve)
            v.memset(src_raw[:, COLS:COLS + 1], NOBUCKET * P)
            v.memset(dst_raw[:, COLS:COLS + 1], 0)
            v.memset(zeros[:, :], 0.0)
            v.memset(eps[:, :], EPS)
            v.memset(w_raw[:, COLS:COLS + 1], 0.0).then_inc(s_zero, 1)
            v.memset(small0[:, :], 0.0)
            v.memset(small[:, :], 0.0)
            v.memset(seen[:, :], 0)
            for s in range(2):
                v.memset(oh[s][:, :, 0:2], 0.0)
            v.memset(hi[:, COLS:EC], float(NOBUCKET))
            v.memset(fields[:, COLS:EC, :], 0.0)
            step(v.memset(reset[:, :], 1.0))
            step(v.memset(reset.rearrange("p (b c) -> p b c", c=W_)[:, :, 0:2], 0.0))

            dve.wait_ge(s_edge_ld, 16 * 6)
            src_hi = ohf_a.rearrange("p a b -> p (a b)").bitcast(i32)[:, 0:COLS + 1]
            src_lo = ohf_b.rearrange("p a b -> p (a b)").bitcast(i32)[:, 0:COLS + 1]
            v.tensor_single_scalar(src_hi, src_raw, 7, ALU.arith_shift_right)
            v.tensor_copy(fields[:, 0:COLS + 1, 1], w_raw)
            step(v.tensor_single_scalar(src_lo, src_raw, P - 1, ALU.bitwise_and))
            v.tensor_copy(hi[:, 0:COLS + 1], src_hi)
            step(v.scalar_tensor_tensor(fields[:, 0:COLS + 1, 0], src_lo, float(PACK), dst_raw, ALU.mult, ALU.add))
            step(v.tensor_scalar(fields[:, 0:COLS + 1, 0], fields[:, 0:COLS + 1, 0], 1.0, None, ALU.add))
            dve.wait_ge(s_pool_const, 1)
            v.tensor_copy(lower_bf[:, :], lower[:, :])
            v.tensor_copy(ones_bf[:, :], ones[:, :])
            step(v.tensor_copy(bucket_no, iota_row[:, 0:TILES, None].broadcast_to([P, TILES, BC])))
            step(v.tensor_scalar(falling[:, :], iota_row[:, 0:NE], -1.0, float(NE), ALU.mult, ALU.add))

            def buckets(k, s, first):
                if not first:
                    dve.wait_ge(s_ohf, k - 1)
                v.tensor_tensor(oh[s][:, :, 2:W_], hi[:, None, bass.ds(k * BC, BC)].broadcast_to([P, TILES, BC]),
                                bucket_no, ALU.is_equal).then_inc(s_oh, 1)

            def places(k, s, first):
                dve.wait_ge(s_base, k + 1)
                step(v.scalar_tensor_tensor(oh[s][:, :, 1], ps[:, 4 + s, 0:TILES], -1.0, seen[:, :], ALU.add, ALU.add))
                step(v.tensor_tensor(seen[:, :], ps[:, 4 + s, P:P + TILES], seen[:, :], ALU.add))
                v.tensor_single_scalar(seen[:, :], seen[:, :], SL - 1, ALU.bitwise_and)
                step(v.tensor_tensor_scan(cum.rearrange("p b c -> p (b c)"), reset,
                                          oh[s].rearrange("p b c -> p (b c)"), 0.0, ALU.mult, ALU.add))
                step(v.tensor_tensor(prod, cum[:, :, 2:W_], oh[s][:, :, 2:W_], ALU.mult))
                n = TILES
                while n > 1:
                    h = n // 2
                    step(v.tensor_tensor(prod[:, 0:h, :], prod[:, 0:h, :], prod[:, n - h:n, :], ALU.add))
                    n -= h
                step(v.tensor_scalar(wrap[:, :], prod[:, 0, :], float(SL), -float(SL), ALU.is_ge, ALU.mult))
                if not first:
                    dve.wait_ge(s_m2, k - 1)
                    dve.wait_ge(s_main, k - 1)
                v.tensor_copy(edge_f[s][:, :, :], fields[:, bass.ds(k * BC, BC), :])
                step(v.tensor_tensor(slot_of[:, :], prod[:, 0, :], wrap[:, :], ALU.add))
                step(v.tensor_tensor(at_slot[s], iota_row[:, None, 0:SL].broadcast_to([P, BC, SL]),
                                     slot_of[:, :, None].broadcast_to([P, BC, SL]), ALU.is_equal))
                dve.sem_inc(s_slot_of, 1)
                v.tensor_tensor(M[s][:, :, 0:2 * SL:2], at_slot[s], edge_f[s][:, :, 0:1].broadcast_to([P, BC, SL]),
                                ALU.mult).then_inc(s_m1, 1)

            def norm0(i, first):
                dve.wait_ge(s_xin, i * 16 + 16)
                if not first:
                    dve.wait_ge(s_xT0_ps, i)
                stt, mv, rs = small0[0:R0, 0:24], small0[0:R0, 24:32], small0[0:R0, 32:36]
                dve.sem_inc(s_held, 1)
                for t in range(T0):
                    last = v.bn_stats(stt[:, 6 * t:6 * t + 6], xin[:, t, :])
                step(last, s_held)
                for t in range(T0):
                    last = v.bn_aggr(mv[:, 2 * t:2 * t + 2], stt[:, 6 * t:6 * t + 6])
                last.then_inc(s_var0, 1)
                dve.wait_ge(s_std0, i + 1)
                step(v.reciprocal(rs, rs))
                for t in range(T0):
                    last = v.tensor_scalar(xn0[:, t, :], xin[:, t, :], mv[:, 2 * t:2 * t + 1], rs[:, t:t + 1],
                                           ALU.subtract, ALU.mult)
                last.then_inc(s_xn0, 1)

            SA, SN = 14, 2

            def two_blocks(i, first):
                buckets(i * 2 + 1, 1, first)
                places(i * 2, 0, first)
                buckets(i * 2 + 2, 0, False)
                places(i * 2 + 1, 1, first)
            buckets(0, 0, True)
            two_blocks(0, True)
            norm0(0, True)
            with dve.Fori(1, ROUNDS0) as i:
                step.enter(i, 1, 2 * SA + SN)
                two_blocks(i, False)
                norm0(i, False)
            step.leave(ROUNDS0 - 1)
            with dve.Fori(ROUNDS0, BLOCKS // 2) as i:
                step.enter(i, ROUNDS0, 2 * SA)
                two_blocks(i, False)
            step.leave(BLOCKS // 2 - ROUNDS0)

            dve.wait_ge(s_over_ps, 1)
            step(v.tensor_reduce(over_sum[0:1, :], ps[0:1, 5, 0:2], AX.X, ALU.add))
            step(v.tensor_copy(flag[0:1, :], over_sum[0:1, :]))
            dve.sem_inc(s_flag, 1)
            dve.wait_ge(s_rec_ld, 16 * 2)

            own = Steps(dve, s_column_dve)

            def column(c, first):
                if not first:
                    dve.wait_ge(s_column_st, c * 16)
                v.tensor_copy(c_src[:, :], src_raw[:, bass.ds(c, 1)])
                v.tensor_scalar(c_dst[:, :], dst_raw[:, bass.ds(c, 1)], 1.0, None, ALU.add)
                v.tensor_copy(c_edge[:, 1:2], w_raw[:, bass.ds(c, 1)])
                own(v.tensor_copy(c_edge[:, 0:1], src_raw[:, bass.ds(c, 1)]))
                own(v.tensor_copy(c_wide[:, :], c_edge[:, 0:1].broadcast_to([P, P])))
                dve.sem_inc(s_column, 1)
                dve.wait_ge(s_wide_T, c + 1)
                v.tensor_scalar(c_same[:, :], ps[:, 6, 0:P], c_edge[:, 0:1], c_edge[:, 1:2],
                                ALU.is_equal, ALU.mult).then_inc(s_same, 1)
                dve.wait_ge(s_column_ps, c + 1)
                dve.wait_ge(s_sum_ld, c * 16 + 16)
                v.tensor_tensor(c_sum[:, :], c_sum[:, :], ps[:, 7, 0:D], ALU.add).then_inc(s_column_sum, 1)

            with dve.If(overflowed(dve) > 0):
                column(0, True)
                with dve.Fori(1, COLS + 1) as c:
                    own.enter(c, 1, 2)
                    column(c, False)
                own.leave(COLS)
                dve.wait_ge(s_column_st, (COLS + 1) * 16)
                dve.wait_ge(s_sum_words, 1)
                own(v.memset(rec[:, :, :], 0.0))
                v.tensor_copy(rec[:, 0:TILES * CPT:CPT, 0], c_word[:, :])
                own(v.memset(rec[:, 0:TILES * CPT:CPT, 1], 1.0))

            step(v.tensor_copy(row_word, rec[:, :, 0]))
            step(v.tensor_single_scalar(src_row, row_word, PACK - 1, ALU.bitwise_and))
            v.tensor_scalar(src_row, src_row, float(N), None, ALU.min)
            step(v.tensor_single_scalar(row_word, row_word, 14, ALU.arith_shift_right))
            step(v.tensor_copy(row_f, row_word))
            dve.sem_inc(s_split, 1)

            def onehots(t, s, first):
                dve.wait_ge(s_staged, t + 1)
                if not first:
                    dve.wait_ge(s_agg, t - 1)
                for c in range(CPT):
                    last = v.tensor_scalar(onehot_w[:, s * CPT + c, :], iota_row[:, :], row_w[s][:, c, 0:1],
                                           row_w[s][:, c, 1:2], ALU.is_equal, ALU.mult)
                last.then_inc(s_onehot, 1)

            def residual_sum(p):
                dve.wait_ge(s_x_ld[0], p * 16 + (32 if is_last(p) else 16))
                for s in range(2):
                    dve.wait_ge(s_agg, p * 2 + (s + 1))
                    last = v.tensor_tensor(xpair[:, s, :], xpair[:, s, :], ps[:, AGG + s, 0:D], ALU.add)
                    last.then_inc(s_x1, 1)
                dve.wait_ge(s_x1, p * 2 + 2)

            def norms(p, first):
                a, n = xpair[:, 0:2, :], norm
                stt, mv, rs = small[:, 0:12], small[:, 12:16], small[:, 16:18]
                step(v.tensor_tensor(a, a, rows[:, 0:1, :].broadcast_to([P, 2, D]), ALU.add), s_held)
                for r in range(2):
                    inp = n if r else a
                    for t in range(2):
                        last = v.bn_stats(stt[:, 6 * t:6 * t + 6], inp[:, t, :])
                    step(last, s_held)
                    for t in range(2):
                        last = v.bn_aggr(mv[:, 2 * t:2 * t + 2], stt[:, 6 * t:6 * t + 6])
                    last.then_inc(s_var, 1)
                    dve.wait_ge(s_std, p * 2 + (r + 1))
                    step(v.reciprocal(rs, rs))
                    for t in range(2):
                        last = v.tensor_scalar(n[:, t, :], inp[:, t, :], mv[:, 2 * t:2 * t + 1], rs[:, t:t + 1],
                                               ALU.subtract, ALU.mult)
                    step(last, s_held)
                step(v.tensor_tensor(n, n, rows[:, 1:2, :].broadcast_to([P, 2, D]), ALU.mult))
                if not first:
                    dve.wait_ge(s_tokT_ps, p)
                    dve.wait_ge(s_tok_st[0], p * 16)
                v.tensor_tensor(tok[:, 0:2, :], n, rows[:, 2:3, :].broadcast_to([P, 2, D]), ALU.add).then_inc(s_tok, 1)

            def scores(p):
                dve.wait_ge(s_logit_ps, p + 1)
                v.tensor_tensor(logits[:, bass.ds(p * 2, 2), :], ps[:, LOGIT, 0:2 * NE].rearrange("p (t e) -> p t e", t=2),
                                br_row[:, None, :].broadcast_to([P, 2, NE]), ALU.add).then_inc(s_logit, 1)

            def move_xT(g):
                dve.wait_ge(s_xT_ps, g + 1)
                if not (isinstance(g, int) and g == 0):
                    dve.wait_ge(s_h_ps, g * KH)
                v.tensor_copy(xT[:, :, :], ps[:, XT, :].rearrange("p (k t) -> p k t", k=KD)).then_inc(s_xT, 1)

            def add_b2(g, h):
                dve.wait_ge(s_y_ps, g + 1)
                if not (isinstance(g, int) and g < 2):
                    dve.wait_ge(s_y_st[h], (g - h) * 8)
                v.tensor_tensor(ysb[:, 2 * h:2 * h + 2, :], ps[:, YB, :].rearrange("p (j d) -> p j d", j=2),
                                b2g[:, h:h + 1, :].broadcast_to([P, 2, D]), ALU.add).then_inc(s_y, 1)

            def experts(groups, k0):
                for k, g in enumerate(groups):
                    move_xT(g)
                    if not (isinstance(g, int) and g == 0):
                        add_b2(g - 1, (k0 + k + 1) % 2)

            SD = 8

            def dve_step(p, groups):
                m = len(groups) // 2
                if not is_first(p):
                    residual_sum(p - 1)
                onehots(p * 2 + 1, 1, is_first(p))
                if not is_first(p):
                    norms(p - 1, isinstance(p, int) and p == 1)
                experts(groups[:m], 0)
                if not is_last(p):
                    onehots(p * 2 + 2, 0, False)
                experts(groups[m:], m)
                if not is_first(p):
                    scores(p - 1)

            def route(part):
                a, b = PARTS[part]
                t0, nt = 2 * a, 2 * (b - a)
                kt = 2 * nt
                dve.wait_ge(s_logit, b)
                L = logits[:, t0:t0 + nt, :]

                def wide(z):
                    return z[:, 0:nt, None].broadcast_to([P, nt, NE])
                fall = falling[:, None, :].broadcast_to([P, nt, NE])
                eq_, sc_, rl_ = eq[:, 0:nt, :], score[:, 0:nt, :], rlog[:, 0:nt, :]
                cur = L
                for k, mx in enumerate((m1, m2)):
                    pickd = oh12[:, k * nt:(k + 1) * nt, :]
                    step(v.tensor_reduce(mx[:, 0:nt], cur, AX.X, ALU.max))
                    step(v.tensor_tensor(eq_, cur, wide(mx), ALU.is_equal))
                    step(v.tensor_tensor(sc_, eq_, fall, ALU.mult))
                    step(v.tensor_reduce(pick[:, 0:nt], sc_, AX.X, ALU.max))
                    step(v.tensor_tensor(pickd, fall, wide(pick), ALU.is_equal))
                    if k == 0:
                        step(v.scalar_tensor_tensor(rl_.rearrange("p a b -> p (a b)"), pickd.rearrange("p a b -> p (a b)"),
                                                    -3.0e38, L.rearrange("p a b -> p (a b)"), ALU.mult, ALU.add))
                        cur = rl_
                v.tensor_tensor(pick[:, 0:nt], m2[:, 0:nt], m1[:, 0:nt], ALU.subtract).then_inc(s_gap, 1)
                if b == PAIRS:
                    for k in range(2):
                        z = oh12[:, (k + 1) * nt - 1, :]
                        step(v.tensor_scalar(z, z, real_row[:, 0:1], None, ALU.mult))
                dve.wait_ge(s_exp, part + 1)
                g1, g2 = gate[:, 0, t0:t0 + nt], gate[:, 1, t0:t0 + nt]
                step(v.tensor_scalar(m1[:, 0:nt], m2[:, 0:nt], 1.0, None, ALU.add))
                step(v.reciprocal(g1, m1[:, 0:nt]))
                step(v.tensor_tensor(g2, m2[:, 0:nt], g1, ALU.mult))

                ww = kt + 1
                rd = rdata.rearrange("p e t -> p (e t)")[:, 0:NE * ww]
                rr, rc_ = rreset[:, 0:NE * ww], rcum.rearrange("p e t -> p (e t)")[:, 0:NE * ww]
                rd3, rr3, rc3 = (z.rearrange("p (e t) -> p e t", e=NE) for z in (rd, rr, rc_))
                step(v.tensor_copy(rd3[:, :, 1:ww], oh12[:, 0:kt, :].rearrange("p t e -> p e t")))
                step(v.memset(rr, 1.0))
                step(v.memset(rr3[:, :, 0:1], 0.0))
                step(v.tensor_reduce(rsmall[:, 0, :], rd3[:, :, 1:ww], AX.X, ALU.add))
                dve.sem_inc(s_rhist, 1)
                dve.wait_ge(s_rprefix, part + 1)
                first_, end_ = rsmall[:, 1, :], rsmall[:, 2, :]
                step(v.tensor_scalar(rcount[:, :], ps[:, LOGIT, 2 * P:2 * P + NE], float(GT - 1), None, ALU.add))
                step(v.tensor_single_scalar(rcount[:, :], rcount[:, :], 8, ALU.arith_shift_right))
                step(v.tensor_copy(first_, rcount[:, :]))
                step(v.tensor_tensor_scan(end_, ones[:, 0:NE], first_, 0.0, ALU.mult, ALU.add))
                step(v.tensor_tensor(first_, end_, first_, ALU.subtract))
                step(v.tensor_scalar(first_, first_, float(GT), float(G0[part] * GT - 1), ALU.mult, ALU.add))
                step(v.tensor_tensor(rd3[:, :, 0], ps[:, LOGIT, P:P + NE], first_, ALU.add))
                step(v.tensor_tensor_scan(rc_, rr, rd, 0.0, ALU.mult, ALU.add))
                step(v.tensor_tensor(rc3[:, :, 1:ww], rc3[:, :, 1:ww], rd3[:, :, 1:ww], ALU.mult))
                rank_f = eq.rearrange("p a b -> p (a b)")[:, 0:kt]
                step(v.tensor_reduce(rank_f, rc3[:, :, 1:ww].rearrange("p e t -> p t e"), AX.X, ALU.add))
                step(v.tensor_copy(slot[:, t0:t0 + nt, :].rearrange("p t k -> p k t"), rank_f.rearrange("p (k t) -> p k t", k=2)))
                ng = NG[part]
                ge = rcum.rearrange("p e t -> p (e t)")[0:1, 0:NE * ng].rearrange("p (e g) -> p e g", e=NE)
                gf = score.rearrange("p a b -> p (a b)")[0:1, 0:ng]
                step(v.tensor_tensor(ge, iota_row[0:1, None, 0:ng].broadcast_to([1, NE, ng]),
                                     end_[0:1, :, None].broadcast_to([1, NE, ng]), ALU.is_ge))
                step(v.tensor_reduce(gf, ge.rearrange("p e g -> p g e"), AX.X, ALU.add))
                step(v.tensor_scalar(group_ids[0:1, G0[part]:G0[part] + ng], gf, float(NE - 1), None, ALU.min))
                dve.sem_inc(s_routed, 1)

            onehots(0, 0, True)
            run_steps(dve, dve_step, route, step, SD)
            residual_sum(PAIRS - 1)
            norms(PAIRS - 1, False)
            add_b2(G0[2] - 1, 1)
            scores(PAIRS - 1)
            route(2)

            def final(j, h, last):
                hold(dve, s_fetched[h], (j + (2 - h)) * 32)
                for k in range(2):
                    for t in range(2):
                        n = LAST if last and t == 1 else P
                        o = out_ring[0:n, 2 * h + t, :]
                        ins = v.scalar_tensor_tensor(o, y_ring[0:n, 4 * h + 2 * t + k, :],
                                                     gate[0:n, k, bass.ds(j * 2 + t, 1)], o, ALU.mult, ALU.add)
                    if k == 0:
                        step(ins)
                ins.then_inc(s_out, 1)
            g2 = G0[2]
            move_xT(g2)
            move_xT(g2 + 1)
            add_b2(g2, 0)
            final(0, 0, False)
            final(1, 1, False)
            with dve.Fori(1, MIXED) as i:
                step.enter(i, 1, 2)
                move_xT(i * 2 + g2)
                add_b2(i * 2 + (g2 - 1), 1)
                final(i * 2, 0, False)
                move_xT(i * 2 + (g2 + 1))
                add_b2(i * 2 + g2, 0)
                final(i * 2 + 1, 1, False)
            step.leave(MIXED - 1)
            for g in range(g2 + 2 * MIXED, GROUPS):
                move_xT(g)
                add_b2(g - 1, (g - 1) % 2)
            add_b2(GROUPS - 1, 1)
            with dve.Fori(MIXED, PAIRS // 2) as i:
                step.enter(i, MIXED, 2)
                final(i * 2, 0, False)
                final(i * 2 + 1, 1, False)
            step.leave(PAIRS // 2 - MIXED)
            final(PAIRS - 1, 0, True)

        @block.scalar
        def _(act):
            a = nc.scalar
            act.wait_ge(s_zero, 1)

            def convert(k, s, first):
                act.wait_ge(s_oh, k + 1)
                if not first:
                    act.wait_ge(s_main, k - 1)
                a.activation(ohf[s], oh[s][:, :, 2:W_], ACT.Copy).then_inc(s_ohf, 1)

            def lists_out(k, s, first):
                act.wait_ge(s_main, k + 1)
                if not first:
                    act.wait_ge(s_listed, k - 1)
                a.activation(lists[s][0:TILES, :], ps[0:TILES, 6 + s, 0:2 * SL + 1], ACT.Copy).then_inc(s_lists, 1)

            def round0(i, first):
                act.wait_ge(s_var0, i + 1)
                a.activation(small0[0:R0, 32:36], small0[0:R0, 25:32:2], ACT.Sqrt, bias=eps[0:R0, :]).then_inc(s_std0, 1)
                act.wait_ge(s_xT0_ps, i + 1)
                a.activation(xT0.rearrange("p a b -> p (a b)").rearrange("p (q c) -> p q c", q=2),
                             ps[:, 0:2, 0:T0 * KD * R0 // 2], ACT.Copy).then_inc(s_xT0, 1)
                act.wait_ge(s_hw_ps, i + 1)
                if not first:
                    act.wait_ge(s_hw_st, i * 16)
                a.activation(hw_sb.rearrange("p t d -> p (t d)").rearrange("p (q c) -> p q c", q=2),
                             ps[0:R0, 2:4, :], ACT.Copy).then_inc(s_hw, 1)
                act.wait_ge(s_hw, i + 1)
                act.dma_start(feat_rounds[:, bass.ds(i * T0, T0), :], hw_sb).then_inc(s_hw_st, 16)

            act.wait_ge(s_oh, 1)
            convert(0, 0, True)
            convert(1, 1, True)
            lists_out(0, 0, True)
            convert(2, 0, False)
            lists_out(1, 1, True)
            round0(0, True)
            with act.Fori(1, ROUNDS0) as i:
                convert(i * 2 + 1, 1, False)
                lists_out(i * 2, 0, False)
                convert(i * 2 + 2, 0, False)
                lists_out(i * 2 + 1, 1, False)
                round0(i, False)
            with act.Fori(ROUNDS0, BLOCKS // 2 - 1) as i:
                convert(i * 2 + 1, 1, False)
                lists_out(i * 2, 0, False)
                convert(i * 2 + 2, 0, False)
                lists_out(i * 2 + 1, 1, False)
            convert(BLOCKS - 1, 1, False)
            lists_out(BLOCKS - 2, 0, False)
            lists_out(BLOCKS - 1, 1, False)

            def stage(t, s, first):
                if not first:
                    act.wait_ge(s_gathered[s], (t - s) * (CPT * 8))
                    act.wait_ge(s_onehot, t - 1)
                a.activation(row_w[s][:, :, 0], row_f[:, bass.ds(t * CPT, CPT)], ACT.Copy)
                a.activation(row_w[s][:, :, 1], rec[:, bass.ds(t * CPT, CPT), 1], ACT.Copy)
                a.activation(idx[s][:, :], src_row[:, bass.ds(t * CPT, CPT)], ACT.Copy).then_inc(s_staged, 1)

            def stds(p):
                for r in range(2):
                    act.wait_ge(s_var, p * 2 + (r + 1))
                    a.activation(small[:, 16:18], small[:, 13:16:2], ACT.Sqrt, bias=eps[:, :]).then_inc(s_std, 1)

            def move_tokT(p, first):
                act.wait_ge(s_tokT_ps, p + 1)
                if not first:
                    act.wait_ge(s_logit_ps, p)
                a.activation(tokT[:, :, :], ps[:, TOKT, :].rearrange("p (k t) -> p k t", k=2 * KD), ACT.Copy).then_inc(s_tokT, 1)

            def gelu(g, h):
                for k in range(KH):
                    if k % 2 == 0:
                        act.wait_ge(s_h_ps, g * KH + (k + 2))
                    if k == 0 and not (isinstance(g, int) and g == 0):
                        act.wait_ge(s_y_ps, g)
                    a.activation(hT[:, k, :], ps[:, HB + k // 2, GT * (k % 2):GT * (k % 2) + GT],
                                 ACT.Gelu, bias=b1g[:, h, k:k + 1]).then_inc(s_h, 1)

            def store_y(g, h):
                act.wait_ge(s_y, g + 1)
                act.dma_start(out_rows[:, bass.ds(g * 2, 2), :], ysb[:, 2 * h:2 * h + 2, :]).then_inc(s_y_st[h], 16)

            def experts(groups, k0):
                for k, g in enumerate(groups):
                    gelu(g, (k0 + k) % 2)
                    if not (isinstance(g, int) and g == 0):
                        store_y(g - 1, (k0 + k + 1) % 2)

            def act_step(p, groups):
                m = len(groups) // 2
                if not is_first(p):
                    stds(p - 1)
                if not is_last(p):
                    stage(p * 2 + 2, 0, False)
                experts(groups[:m], 0)
                if not is_last(p):
                    stage(p * 2 + 3, 1, False)
                if not is_first(p):
                    move_tokT(p - 1, isinstance(p, int) and p == 1)
                experts(groups[m:], m)

            def weigh(part):
                nt = 2 * (PARTS[part][1] - PARTS[part][0])
                act.wait_ge(s_gap, part + 1)
                a.activation(m2[:, 0:nt], pick[:, 0:nt], ACT.Exp).then_inc(s_exp, 1)

            act.wait_ge(s_split, 1)
            stage(0, 0, True)
            stage(1, 1, True)
            run_steps(act, act_step, weigh)
            stds(PAIRS - 1)
            move_tokT(PAIRS - 1, False)
            store_y(G0[2] - 1, 1)
            weigh(2)
            g2 = G0[2]
            gelu(g2, 0)
            gelu(g2 + 1, 1)
            store_y(g2, 0)
            with act.Fori(1, NG[2] // 2) as i:
                gelu(i * 2 + g2, 0)
                store_y(i * 2 + (g2 - 1), 1)
                gelu(i * 2 + (g2 + 1), 1)
                store_y(i * 2 + g2, 0)
            store_y(GROUPS - 1, 1)

        @block.tensor
        def _(pe):
            mm = nc.tensor.matmul

            def T(out_, in_, n):
                return nc.tensor.transpose(out_, in_, ident[0:n, 0:n])

            pe.wait_ge(s_const_ld, 16 * 6)
            pe.wait_ge(s_pool_const, 1)

            def bases(k, s):
                pe.wait_ge(s_oh, k + 1)
                for c in range(BC):
                    mm(ps[:, 4 + s, 0:TILES], lower_bf[:, :], oh[s][:, :, 2 + c], start=(c == 0), stop=(c == BC - 1))
                for c in range(BC):
                    last = mm(ps[:, 4 + s, P:P + TILES], ones_bf[:, :], oh[s][:, :, 2 + c], start=(c == 0), stop=(c == BC - 1))
                last.then_inc(s_base, 1)

            def place(k, s, first):
                pe.wait_ge(s_ohf, k + 1)
                pe.wait_ge(s_m1, k + 1)
                pe.wait_ge(s_m2, k + 1)
                if not first:
                    pe.wait_ge(s_lists, k - 1)
                for c in range(BC):
                    last = mm(ps[0:TILES, 6 + s, 0:2 * SL + 1], ohf[s][:, :, c], M[s][:, c, :], start=(c == 0), stop=(c == BC - 1))
                last.then_inc(s_main, 1)

            def round0(i, first):
                pe.wait_ge(s_xn0, i + 1)
                for t in range(T0):
                    for k in range(KD):
                        j = t * KD + k
                        last = T(ps[:, j // 4, R0 * (j % 4):R0 * (j % 4) + R0], xn0[:, t, k * P:(k + 1) * P], R0)
                last.then_inc(s_xT0_ps, 1)
                pe.wait_ge(s_xT0, i + 1)
                if not first:
                    pe.wait_ge(s_hw, i)
                for t in range(T0):
                    for k in range(KD):
                        last = mm(ps[0:R0, 2 + t // 2, D * (t % 2):D * (t % 2) + D], xT0[:, t * KD + k, :],
                                  Wg[:, k, :], start=(k == 0), stop=(k == KD - 1))
                last.then_inc(s_hw_ps, 1)

            bases(0, 0)
            bases(1, 1)
            place(0, 0, True)
            bases(2, 0)
            place(1, 1, True)
            round0(0, True)
            with pe.Fori(1, ROUNDS0) as i:
                bases(i * 2 + 1, 1)
                place(i * 2, 0, False)
                bases(i * 2 + 2, 0)
                place(i * 2 + 1, 1, False)
                round0(i, False)
            with pe.Fori(ROUNDS0, BLOCKS // 2 - 1) as i:
                bases(i * 2 + 1, 1)
                place(i * 2, 0, False)
                bases(i * 2 + 2, 0)
                place(i * 2 + 1, 1, False)
            bases(BLOCKS - 1, 1)
            place(BLOCKS - 2, 0, False)
            place(BLOCKS - 1, 1, False)
            pe.wait_ge(s_hw, ROUNDS0)
            pe.wait_ge(s_lists, BLOCKS)
            pe.wait_ge(s_over, 1)
            mm(ps[0:1, 5, 0:2], ones[0:TILES, 0:1], st[0:TILES, 6:8], start=True, stop=True).then_inc(s_over_ps, 1)

            def column(c, first):
                pe.wait_ge(s_column, c + 1)
                T(ps[:, 6, 0:P], c_wide[:, :], P).then_inc(s_wide_T, 1)
                pe.wait_ge(s_same, c + 1)
                pe.wait_ge(s_feat_ld, c * 16 + 16)
                mm(ps[:, 7, 0:D], c_same[:, :], c_feat[:, :], start=True, stop=True).then_inc(s_column_ps, 1)

            with pe.If(overflowed(pe) > 0):
                column(0, True)
                with pe.Fori(1, COLS + 1) as c:
                    column(c, False)
            pe.wait_ge(s_split, 1)

            def sum_tile(p, s):
                pe.wait_ge(s_gathered[s], p * (CPT * 16) + CPT * 16)
                pe.wait_ge(s_onehot, p * 2 + (s + 1))
                if not is_first(p):
                    pe.wait_ge(s_x1, p * 2 + (s - 1))
                for c in range(CPT):
                    last = mm(ps[:, AGG + s, 0:D], onehot_w[:, s * CPT + c, :], gathered[:, s * CPT + c, :],
                              start=(c == 0), stop=(c == CPT - 1))
                last.then_inc(s_agg, 1)

            def transpose_tokens(p, first):
                pe.wait_ge(s_tok, p + 1)
                for t in range(2):
                    for k in range(KD):
                        j = t * KD + k
                        last = T(ps[:, TOKT, j * P:(j + 1) * P], tok[:, t, k * P:(k + 1) * P], P)
                last.then_inc(s_tokT_ps, 1)

            def router(p, first):
                pe.wait_ge(s_tokT, p + 1)
                if not first:
                    pe.wait_ge(s_logit, p)
                for t in range(2):
                    for k in range(KD):
                        last = mm(ps[:, LOGIT, t * NE:(t + 1) * NE], tokT[:, t * KD + k, :], Wr_sb[:, k, :],
                                  start=(k == 0), stop=(k == KD - 1))
                last.then_inc(s_logit_ps, 1)

            def expert_T(g, h):
                pe.wait_ge(s_ld1[h], (g - h) * 24 + 48)
                for j in range(2):
                    for k in range(KD):
                        last = T(ps[:, XT, k * GT + j * P:k * GT + (j + 1) * P], xs[:, 2 * h + j, k * P:(k + 1) * P], P)
                last.then_inc(s_xT_ps, 1)

            def expert_up(g, h):
                pe.wait_ge(s_xT, g + 1)
                if not (isinstance(g, int) and g == 0):
                    pe.wait_ge(s_h, g * KH)
                for k in range(KH):
                    for j in range(KD):
                        last = mm(ps[:, HB + k // 2, GT * (k % 2):GT * (k % 2) + GT],
                                  W1g[:, KD * h + j, k * P:(k + 1) * P], xT[:, j, :], start=(j == 0), stop=(j == KD - 1))
                    last.then_inc(s_h_ps, 1)

            def expert_down(g, h):
                pe.wait_ge(s_h, g * KH + KH)
                pe.wait_ge(s_ld2[h], (g - h) * 16 + 32)
                if not (isinstance(g, int) and g == 0):
                    pe.wait_ge(s_y, g)
                for j in range(2):
                    for k in range(KH):
                        last = mm(ps[:, YB, j * D:(j + 1) * D], hT[:, k, j * P:(j + 1) * P],
                                  W2g[:, KH * h + k, :], start=(k == 0), stop=(k == KH - 1))
                last.then_inc(s_y_ps, 1)

            def experts_before(g, h):
                expert_T(g, h)

            def experts_after(g, h):
                if not (isinstance(g, int) and g == 0):
                    expert_down(g - 1, 1 - h)
                expert_up(g, h)

            def pe_step(p, groups):
                m = len(groups) // 2
                if m:
                    expert_T(groups[0], 0)
                sum_tile(p, 0)
                for k, g in enumerate(groups[:m]):
                    if k:
                        expert_T(g, k % 2)
                    experts_after(g, k % 2)
                if m:
                    expert_T(groups[m], m % 2)
                if not is_first(p):
                    transpose_tokens(p - 1, isinstance(p, int) and p == 1)
                sum_tile(p, 1)
                for k, g in enumerate(groups[m:]):
                    if k:
                        expert_T(g, (m + k) % 2)
                    experts_after(g, (m + k) % 2)
                if not is_first(p):
                    router(p - 1, isinstance(p, int) and p == 1)

            def count(part):
                pe.wait_ge(s_rhist, part + 1)
                mm(ps[:, LOGIT, P:P + NE], lower[:, :], rsmall[:, 0, :], start=True, stop=True)
                mm(ps[:, LOGIT, 2 * P:2 * P + NE], ones[:, :], rsmall[:, 0, :], start=True, stop=True).then_inc(s_rprefix, 1)

            run_steps(pe, pe_step, count)
            transpose_tokens(PAIRS - 1, False)
            expert_down(G0[2] - 1, 1)
            router(PAIRS - 1, False)
            count(2)
            g2 = G0[2]
            expert_T(g2, 0)
            expert_up(g2, 0)
            expert_T(g2 + 1, 1)
            expert_down(g2, 0)
            expert_up(g2 + 1, 1)
            with pe.Fori(1, NG[2] // 2) as i:
                expert_T(i * 2 + g2, 0)
                expert_down(i * 2 + (g2 - 1), 1)
                expert_up(i * 2 + g2, 0)
                expert_T(i * 2 + (g2 + 1), 1)
                expert_down(i * 2 + g2, 0)
                expert_up(i * 2 + (g2 + 1), 1)
            expert_down(GROUPS - 1, 1)


def kernel(**inputs):
    import numpy as _np
    import concourse.bacc as _bacc
    from concourse import mybir as _mybir
    from concourse.bass_utils import run_bass_kernel_spmd as _run

    nc = _bacc.Bacc("TRN2", target_bir_lowering=False, num_devices=1)
    b1 = _np.asarray(inputs["L0_ffn_b1"])
    given = {
        "x": inputs["x"], "src": inputs["src"], "dst": inputs["dst"], "edge_weight": inputs["edge_weight"],
        "gnn_W": inputs["L0_gnn_W"], "gnn_b": inputs["L0_gnn_b"], "gamma": inputs["L0_ffn_gamma"],
        "beta": inputs["L0_ffn_beta"], "Wr": inputs["L0_ffn_Wr"], "br": inputs["L0_ffn_br"],
        "W1": inputs["L0_ffn_W1"], "b1_cols": b1.reshape(b1.shape[0], -1, 128).transpose(0, 2, 1),
        "W2": inputs["L0_ffn_W2"], "b2": inputs["L0_ffn_b2"],
    }
    arrays, args = {}, []
    for name, value in given.items():
        a = _np.ascontiguousarray(value)
        arrays[f"in_{name}"] = a
        args.append(nc.dram_tensor(f"in_{name}", a.shape, _mybir.dt.from_np(a.dtype), kind="ExternalInput").ap())
    out = nc.dram_tensor("out", arrays["in_x"].shape, f32, kind="ExternalOutput").ap()
    gnn_moe(nc, *args, out)
    r = _run(nc, [arrays], core_ids=[0])
    return r.results[0]["out"]
```

```python
import itertools

import concourse.bass as bass
from concourse import mybir
from contextlib import ExitStack

f32 = mybir.dt.float32
bf16 = mybir.dt.bfloat16
i32 = mybir.dt.int32
ALU = mybir.AluOpType
ACT = mybir.ActivationFunctionType
AX = mybir.AxisListType


class Steps:

    def __init__(self, engine, semaphore):
        self.engine, self.semaphore = engine, semaphore
        self.before, self.base, self.n = 0, 0, 0

    def __call__(self, instruction, held=None):
        self.n += 1
        instruction.then_inc(self.semaphore, 1)
        self.engine.wait_ge(self.semaphore, self.base + self.n)
        if held is not None:
            self.engine.sem_inc(held, 1)

    def enter(self, i, first, per_round):
        self.before, self.base, self.n, self.per_round = self.before + self.n, 0, 0, per_round
        self.base = (i - first) * per_round + self.before

    def leave(self, rounds):
        assert self.n == self.per_round, (self.n, self.per_round)
        self.before, self.base, self.n = self.before + rounds * self.per_round, 0, 0
        self.base = self.before
        self.before = self.before

    def straight(self):
        self.base = self.before


def ceil_div(a, b):
    return -(-a // b)


def _prod(shape):
    n = 1
    for s in shape:
        n *= s
    return n


def carve(region, parts):
    at, views = 0, []
    for shape, dt in parts:
        words = ceil_div(int(mybir.dt.size(dt)) * _prod(shape), 4)
        v = region[:, at:at + words]
        if dt != f32:
            v = v.bitcast(dt)
        v = v[:, 0:_prod(shape)]
        if len(shape) == 2:
            v = v.rearrange("p (a b) -> p a b", a=shape[0])
        if len(shape) == 3:
            v = v.rearrange("p (a b c) -> p a b c", a=shape[0], b=shape[1])
        views.append(v)
        at += words
    assert at <= region.shape[1], (at, region.shape)
    return views


def gnn_moe(nc, x, src, dst, edge_weight, gnn_W, gnn_b, gamma, beta, Wr, br, W1, b1_cols, W2, b2, out):
    P = 128
    N, D = x.shape
    E_EDGES = src.shape[0]
    NE, _, H = W1.shape
    KD, KH = D // P, H // P
    EPS = 1e-5

    TILES = ceil_div(N, P)
    PAIRS = TILES // 2
    LAST = N - (TILES - 1) * P
    R0, T0 = 125, 4
    ROUNDS0 = N // (R0 * T0)
    COLS = E_EDGES // P
    TAIL = E_EDGES - COLS * P
    BC = 20
    BLOCKS = ceil_div(COLS + 1, BC)
    EC = (BLOCKS + 1) * BC
    assert BLOCKS % 2 == 0 and 0 < TAIL < P
    NOBUCKET = 127
    W_ = BC + 2
    SL = 64
    CPT = 19
    CAP = CPT * P
    PAGES = CAP // SL
    PACK = 1 << 14
    GT = 256
    PARTS = [(0, 18), (18, 38), (38, PAIRS)]

    def groups_of(a, b):
        real = 2 * (min(b * 2 * P, N) - a * 2 * P)
        return (real + NE * (GT - 1)) // GT

    LATER = 3
    FFN_STEPS = [(PARTS[0][1] + LATER, PARTS[1][1] + 1, 2), (PARTS[1][1] + LATER, PAIRS, 4)]
    LEFT = 20
    SLOW = 2
    NG = [(b - a) * m for a, b, m in FFN_STEPS] + [ceil_div(groups_of(*PARTS[2]), 2) * 2]
    NG[0] += 4 * (FFN_STEPS[1][0] - FFN_STEPS[0][1])
    NG[1] += LEFT - 2 * SLOW
    for n, part in zip(NG, PARTS):
        assert n >= groups_of(*part), (n, groups_of(*part))
    assert FFN_STEPS[0][1] <= FFN_STEPS[1][0]
    G0 = [0, NG[0], NG[0] + NG[1]]
    GROUPS = sum(NG)
    SLOTS = GROUPS * GT
    MAXT = max(2 * (b - a) for a, b in PARTS)

    ctx = ExitStack()
    with ctx:
        def sb(name, shape, dt=f32):
            return ctx.enter_context(nc.sbuf_tensor(name, shape, dt))

        def sem(name):
            return ctx.enter_context(nc.semaphore(name))

        def sem2(name):
            return [sem(f"{name}{s}") for s in range(2)]

        features = nc.dram_tensor("features", [N + 1, D], f32, kind="Internal").ap()
        sums = nc.dram_tensor("sums", [(NOBUCKET + 1) * P, D], f32, kind="Internal").ap()
        pages = nc.dram_tensor("pages", [TILES * PAGES, SL * 2], f32, kind="Internal").ap()
        tokens = nc.dram_tensor("tokens", [TILES * P, D], f32, kind="Internal").ap()
        residual = nc.dram_tensor("residual", [TILES * P, D], f32, kind="Internal").ap()
        expert_in = nc.dram_tensor("expert_in", [SLOTS, D], f32, kind="Internal").ap()
        expert_out = nc.dram_tensor("expert_out", [SLOTS, D], f32, kind="Internal").ap()

        ident, lower, ones, iota_row = sb("ident", [P, P]), sb("lower", [P, P]), sb("ones", [P, P]), sb("iota_row", [P, P])
        lower_bf, ones_bf = sb("lower_bf", [P, P], bf16), sb("ones_bf", [P, P], bf16)
        zeros = sb("zeros", [P, D])
        Wg = sb("Wg", [P, KD, D])
        Wr_sb = sb("Wr_sb", [P, KD, NE])
        rows = sb("rows", [P, 3, D])
        br_row = sb("br_row", [P, NE])
        eps = sb("eps", [P, 1])
        real_row = sb("real_row", [P, 1])
        page_last = sb("page_last", [P, 1])
        group_ids, group_new = sb("group_ids", [1, GROUPS], i32), sb("group_new", [1, GROUPS], i32)
        logits = sb("logits", [P, TILES, NE])
        slot = sb("slot", [P, TILES, 2], i32)
        gate = sb("gate", [P, 2, TILES])
        small0 = sb("small0", [P, 64])
        small = sb("small", [P, 64])

        ARENA = 42800
        U = sb("U", [P, ARENA])
        ps = ctx.enter_context(nc.psum_tensor("ps", [P, 8, 512], f32))

        (xin, xn0, xT0, hw_sb, src_raw, dst_raw, w_raw, fields, hi, bucket_no, oh_a, oh_b, reset, cum, prod,
         ohf_a, ohf_b, M_a, M_b, at_a, at_b, slot_no) = carve(U, [
            ((T0, D), f32), ((T0, D), f32), ((T0 * KD, R0), f32), ((T0, D), f32),
            ((COLS + 1,), i32), ((COLS + 1,), i32), ((COLS + 1,), f32), ((EC, 2), f32), ((EC,), bf16),
            ((TILES, BC), bf16), ((TILES, W_), bf16), ((TILES, W_), bf16), ((TILES * W_,), bf16), ((TILES, W_), bf16),
            ((TILES, BC), bf16), ((TILES, BC), f32), ((TILES, BC), f32), ((BC, 2 * SL + 1), f32), ((BC, 2 * SL + 1), f32),
            ((SL, BC), bf16), ((SL, BC), bf16),
            ((SL, BC), bf16)])
        xin, xn0, hw_sb = xin[0:R0, :, :], xn0[0:R0, :, :], hw_sb[0:R0, :, :]
        oh, ohf, M, at_slot = (oh_a, oh_b), (ohf_a, ohf_b), (M_a, M_b), (at_a, at_b)
        seen = sb("seen", [P, TILES], i32)
        wrap = sb("wrap", [P, BC])
        slot_of, place_sum = sb("slot_of", [P, BC], bf16), sb("place_sum", [P, BC])
        edge_f = [sb(f"edge_f{s}", [P, BC, 2]) for s in range(2)]
        lists = [sb(f"lists{s}", [P, 2 * SL + 1]) for s in range(2)]
        page = [sb(f"page{s}", [P, 2 * SL]) for s in range(2)]
        page_row = [sb(f"page_row{s}", [P, 1], i32) for s in range(2)]
        part_page, here, late, kept = (sb("part_page", [P, 2 * SL]), sb("here", [P, SL]), sb("late", [P, 2 * SL]),
                                       sb("kept", [P, 2 * SL]))
        st = sb("st", [P, 8])

        (c_src, c_dst, c_edge, c_wide, c_same, c_feat, c_sum, c_word) = carve(U[:, 9100:9100 + 1200], [
            ((1,), i32), ((1,), i32), ((2,), f32), ((P,), f32), ((P,), f32), ((D,), f32), ((D,), f32), ((TILES,), i32)])
        flag, over_sum = sb("flag", [1, 1], i32), sb("over_sum", [1, 1])

        (rec, row_word, src_row, row_f, gathered, onehot_w, xpair, norm, tok, tokT, W1g, W2g, b2g, b1g, xs, xT, hT, ysb,
         tok_ring, y_ring, out_ring) = carve(U, [
            ((TILES * CPT, 2), f32), ((TILES * CPT,), i32), ((TILES * CPT,), i32), ((TILES * CPT,), f32),
            ((2 * CPT, D), f32), ((2 * CPT, P), f32), ((4, D), f32), ((2, D), f32), ((4, D), f32), ((2 * KD, P), f32),
            ((2 * KD, H), f32), ((2 * KH, D), f32), ((2, D), f32), ((2, KH), f32), ((4, D), f32), ((KD, GT), f32),
            ((KH, GT), f32), ((4, D), f32), ((4, D), f32), ((8, D), f32), ((4, D), f32)])
        idx = [sb(f"idx{s}", [P, CPT], i32) for s in range(2)]
        row_w = [sb(f"row_w{s}", [P, CPT, 2]) for s in range(2)]
        slot_st = [sb(f"slot_st{s}", [P, 2, 2], i32) for s in range(2)]
        slot_ft = [sb(f"slot_ft{s}", [P, 2, 2], i32) for s in range(2)]
        KM = 2 * MAXT
        (eq, score, oh12, rdata, rreset, rcum, rlog) = carve(
            sb("route", [P, 4640]),
            [((MAXT, NE), f32), ((MAXT, NE), f32), ((KM, NE), f32), ((NE, KM + 1), f32), ((NE * (KM + 1),), bf16),
             ((NE, KM + 1), f32), ((MAXT, NE), f32)])
        m1, m2, pick = sb("m1", [P, MAXT]), sb("m2", [P, MAXT]), sb("pick", [P, MAXT])
        falling = sb("falling", [P, NE])
        rsmall = sb("rsmall", [P, 3, NE])
        rcount = sb("rcount", [P, NE], i32)

        AGG, TOKT, LOGIT, XT, HB, YB = 0, 2, 3, 4, 5, 7

        (s_const_ld, s_edge_ld, s_pool_const, s_zero, s_cleared, s_held) = map(
            sem, "s_const_ld s_edge_ld s_pool_const s_zero s_cleared s_held".split())
        s_dve, s_pool = sem("s_dve"), sem("s_pool")
        s_oh, s_base, s_ohf, s_slot_of, s_m1, s_m2, s_main, s_lists = map(
            sem, "s_oh s_base s_ohf s_slot_of s_m1 s_m2 s_main s_lists".split())
        s_listed = sem("s_listed")
        s_page_st = sem2("s_page_st")
        s_over, s_over_ps, s_flag = map(sem, "s_over s_over_ps s_flag".split())
        (s_sums_zero, s_column, s_wide_T, s_same, s_column_ps, s_feat_ld, s_sum_ld, s_column_sum, s_column_st,
         s_sums_copied, s_sum_words, s_column_dve) = map(sem, (
             "s_sums_zero s_column s_wide_T s_same s_column_ps s_feat_ld s_sum_ld s_column_sum s_column_st "
             "s_sums_copied s_sum_words s_column_dve").split())
        s_xin, s_var0, s_std0, s_xn0, s_xT0_ps, s_xT0, s_hw_ps, s_hw, s_hw_st = map(
            sem, "s_xin s_var0 s_std0 s_xn0 s_xT0_ps s_xT0 s_hw_ps s_hw s_hw_st".split())
        s_rec_ld, s_split, s_staged, s_onehot, s_agg, s_x1, s_var, s_std, s_tok = map(
            sem, "s_rec_ld s_split s_staged s_onehot s_agg s_x1 s_var s_std s_tok".split())
        s_tokT_ps, s_tokT, s_logit_ps, s_logit = map(sem, "s_tokT_ps s_tokT s_logit_ps s_logit".split())
        s_gathered, s_x_ld, s_res_st, s_tok_st = map(sem2, "s_gathered s_x_ld s_res_st s_tok_st".split())
        s_rhist, s_rprefix, s_gap, s_exp, s_routed = map(sem, "s_rhist s_rprefix s_gap s_exp s_routed".split())
        s_exp_zero = sem("s_exp_zero")
        s_tok_ld, s_sent = sem2("s_tok_ld"), sem2("s_sent")
        s_xT_ps, s_xT, s_h_ps, s_h, s_y_ps, s_y = map(sem, "s_xT_ps s_xT s_h_ps s_h s_y_ps s_y".split())
        s_ld1, s_ld2, s_y_st = map(sem2, "s_ld1 s_ld2 s_y_st".split())
        s_fetch_ld, s_fetched, s_out_st = map(sem2, "s_fetch_ld s_fetched s_out_st".split())
        s_out = sem("s_out")

        def hold(engine, semaphore, value):
            engine.wait_ge(semaphore, value)
            engine.sem_inc(s_held, 1)

        x_rounds = x.rearrange("(t p) d -> p t d", p=R0)
        feat_rounds = features[1:N + 1, :].rearrange("(t p) d -> p t d", p=R0)
        page_words = pages.rearrange("r w -> (r w)").rearrange("(t p w) -> p t w", t=TILES, p=P)
        x_tiles = x[0:(TILES - 1) * P, :].rearrange("(t p) d -> p t d", p=P)
        out_tiles = out[0:(TILES - 1) * P, :].rearrange("(t p) d -> p t d", p=P)
        tok_tiles = tokens.rearrange("(t p) d -> p t d", p=P)
        res_tiles = residual.rearrange("(t p) d -> p t d", p=P)
        in_rows = expert_in.rearrange("(g p) d -> p g d", p=P)
        out_rows = expert_out.rearrange("(g p) d -> p g d", p=P)
        W1_e = W1.rearrange("e (k p) h -> p (e k) h", p=P)
        W2_e = W2.rearrange("e (k p) d -> p (e k) d", p=P)

        RUNS = [(0, 1, 0, 0, None), (1, PARTS[0][1] + 1, 0, 0, 0), (PARTS[0][1] + 1, FFN_STEPS[0][0], 0, 0, None),
                (FFN_STEPS[0][0], FFN_STEPS[0][0] + 1, 2, 0, None),
                (FFN_STEPS[0][0] + 1, FFN_STEPS[0][1], 2, 2, 1), 
                *((p, p + 1, 4, 2 * (FFN_STEPS[0][1] - FFN_STEPS[0][0]) + 4 * (p - FFN_STEPS[0][1]), None)
                  for p in range(FFN_STEPS[0][1], FFN_STEPS[1][0])),
                (FFN_STEPS[1][0], PAIRS - SLOW, 4, G0[1], None),
                *((p, p + 1, 2, G0[2] - LEFT - 2 * (PAIRS - p), None) for p in range(PAIRS - SLOW, PAIRS))]

        MIXED = NG[2] // 2
        LEFT0 = G0[2] - LEFT
        EARLY, COUNT_AT, ROUTED_AT = 3, 6, 7
        DONE = PARTS[1][1] - 2 * MIXED
        assert 2 < DONE <= PARTS[0][1] and DONE % 2 == 0

        def run_steps(engine, body, routed=None, own=None, per_step=None, begin=None):
            for a, b, m, g0, part in RUNS:
                if begin is not None:
                    begin(a)
                if b - a == 1:
                    body(a, [g0 + k for k in range(m)])
                elif b > a:
                    with engine.Fori(a, b) as p:
                        if own is not None:
                            own.enter(p, a, per_step)
                        body(p, [(p - a) * m + g0 + k for k in range(m)])
                    if own is not None:
                        own.leave(b - a)
                if part is not None and routed is not None:
                    routed(part)

        def is_first(p):
            return isinstance(p, int) and p == 0

        def is_last(p):
            return isinstance(p, int) and p == PAIRS - 1

        def overflowed(engine):
            engine.wait_ge(s_flag, 1)
            return engine.value_load(flag[0:1, 0:1], min_val=0, max_val=2 * P)

        block = ctx.enter_context(nc.Block())

        @block.sync
        def _(sp):
            sp.wait_ge(s_zero, 1)
            for raw, arr in ((src_raw, src), (dst_raw, dst), (w_raw, edge_weight)):
                sp.dma_start(raw[:, 0:COLS], arr[0:COLS * P].rearrange("(p c) -> p c", p=P)).then_inc(s_edge_ld, 16)
                sp.dma_start(raw[0:TAIL, COLS:COLS + 1],
                             arr[COLS * P:E_EDGES].rearrange("(p c) -> p c", c=1)).then_inc(s_edge_ld, 16)
            sp.dma_start(Wg[:, :, :], gnn_W.rearrange("(k p) n -> p k n", p=P)).then_inc(s_const_ld, 16)
            sp.dma_start(Wr_sb[:, :, :], Wr.rearrange("(k p) n -> p k n", p=P)).then_inc(s_const_ld, 16)
            for k, row in enumerate((gnn_b, gamma, beta)):
                sp.dma_start(rows[:, k, :], row.partition_broadcast(P)).then_inc(s_const_ld, 16)
            sp.dma_start(br_row[:, :], br.partition_broadcast(P)).then_inc(s_const_ld, 16)
            for q in range(PAGES // 2):
                rows_q = TILES * 2
                sp.dma_start(pages[q * rows_q:q * rows_q + 112, :], zeros[0:112, 0:2 * SL]).then_inc(s_cleared, 16)
                sp.dma_start(pages[q * rows_q + 112:(q + 1) * rows_q, :], zeros[0:rows_q - 112, 0:2 * SL]).then_inc(s_cleared, 16)
            sp.dma_start(features[0:1, :], zeros[0:1, :]).then_inc(s_cleared, 16)

            def load_round0(i, first):
                if not first:
                    sp.wait_ge(s_xn0, i)
                sp.dma_start(xin, x_rounds[:, bass.ds(i * T0, T0), :]).then_inc(s_xin, 16)
            load_round0(0, True)
            with sp.Fori(1, ROUNDS0) as i:
                load_round0(i, False)

            def zero_slots(i):
                sp.dma_start(in_rows[:, bass.ds(i * 4, 4), :],
                             zeros[:, None, :].broadcast_to([P, 4, D])).then_inc(s_exp_zero, 16)
            assert GROUPS % 4 == 2 and 2 * ROUNDS0 + GROUPS // 4 <= BLOCKS
            zero_slots(0)
            with sp.Fori(0, GROUPS // 4) as i:
                sp.wait_ge(s_listed, i + 2 * ROUNDS0)
                zero_slots(i * 2 + 1)
                zero_slots(i * 2 + 2)

            for s in range(2):
                sp.wait_ge(s_page_st[s], 16 * (BLOCKS // 2 + (s == 0)))
            sp.wait_ge(s_hw_st, 16 * ROUNDS0)
            TQ = TILES // 2
            for q in range(2):
                sp.dma_start(rec.rearrange("p (t c) f -> p t (c f)", t=TILES)[:, q * TQ:(q + 1) * TQ, :],
                             page_words[:, q * TQ:(q + 1) * TQ, :]).then_inc(s_rec_ld, 16)

            with sp.If(overflowed(sp) > 0):
                for z in range(0, NOBUCKET + 1, 4):
                    sp.dma_start(sums.rearrange("(t p) d -> p t d", p=P)[:, z:z + 4, :],
                                 zeros[:, None, :].broadcast_to([P, 4, D])).then_inc(s_sums_zero, 16)
                sp.wait_ge(s_column_st, 16 * (COLS + 1))
                sp.dma_start(features[1:N + 1, :], sums[0:N, :]).then_inc(s_sums_copied, 16)

            def load_up(g, h):
                new = sp.value_load(group_new[0:1, bass.ds(g, 1)], min_val=0, max_val=1)
                if not (isinstance(g, int) and g < 2):
                    hold(sp, s_h, (g - 1) * KH)
                sp.dma_start(xs[:, 2 * h:2 * h + 2, :], in_rows[:, bass.ds(g * 2, 2), :]).then_inc(s_ld1[h], 16)
                with sp.If(new > 0):
                    e = sp.value_load(group_ids[0:1, bass.ds(g, 1)], min_val=0, max_val=NE - 1)
                    sp.dma_start(W1g[:, KD * h:KD * h + KD, :], W1_e[:, bass.ds(e * KD, KD), :]).then_inc(s_ld1[h], 16)
                    sp.dma_start(b1g[:, h, :], b1_cols[bass.ds(e, 1), :, :].rearrange("a p k -> p (a k)")).then_inc(s_ld1[h], 16)
                with sp.Else():
                    sp.sem_inc(s_ld1[h], 32)

            def load_down(g, h):
                new = sp.value_load(group_new[0:1, bass.ds(g, 1)], min_val=0, max_val=1)
                if not (isinstance(g, int) and g < 2):
                    hold(sp, s_y, g - 1)
                with sp.If(new > 0):
                    e = sp.value_load(group_ids[0:1, bass.ds(g, 1)], min_val=0, max_val=NE - 1)
                    sp.dma_start(W2g[:, KH * h:KH * h + KH, :], W2_e[:, bass.ds(e * KH, KH), :]).then_inc(s_ld2[h], 16)
                    sp.dma_start(b2g[:, h:h + 1, :], b2[bass.ds(e, 1), :].partition_broadcast(P)).then_inc(s_ld2[h], 16)
                with sp.Else():
                    sp.sem_inc(s_ld2[h], 32)

            def store_pair(p, first):
                sp.wait_ge(s_tok, p + 1)
                sp.dma_start(res_tiles[:, bass.ds(p * 2, 2), :], xpair[:, 0:2, :]).then_inc(s_res_st[0], 16)
                sp.dma_start(tok_tiles[:, bass.ds(p * 2, 2), :], tok[:, 0:2, :]).then_inc(s_tok_st[0], 16)

            def sp_step(p, groups):
                m = len(groups)
                for k, g in enumerate(groups[:m // 2]):
                    load_up(g, k % 2)
                    if k == 0:
                        load_down(g, 0)
                if m == 4:
                    load_down(groups[1], 1)
                for k, g in enumerate(groups[m // 2:]):
                    load_up(g, (m // 2 + k) % 2)
                    if not (m == 2):
                        load_down(g, (m // 2 + k) % 2)
                if m == 2:
                    load_down(groups[1], 1)

            def sp_step_all(p, groups):
                sp_step(p, groups)
                if not is_first(p):
                    store_pair(p - 1, False)
                if not is_first(p):
                    sp.wait_ge(s_res_st[0], p * 16)
                load_x_single(p)

            def load_x_single(p):
                if is_last(p):
                    sp.dma_start(xpair[:, 0, :], x[(TILES - 2) * P:(TILES - 1) * P, :]).then_inc(s_x_ld[0], 16)
                    sp.dma_start(xpair[0:LAST, 1, :], x[(TILES - 1) * P:N, :]).then_inc(s_x_ld[0], 16)
                else:
                    sp.dma_start(xpair[:, 0:2, :], x_tiles[:, bass.ds(p * 2, 2), :]).then_inc(s_x_ld[0], 16)

            def load_dispatch(j, h, first):
                if not first:
                    sp.wait_ge(s_sent[h], (j - h) * 32)
                sp.dma_start(tok_ring[:, 2 * h:2 * h + 2, :], tok_tiles[:, bass.ds(j * 2, 2), :]).then_inc(s_tok_ld[h], 16)
                sp.dma_start(slot_st[h][:, :, :], slot[:, bass.ds(j * 2, 2), :]).then_inc(s_tok_ld[h], 16)

            def dispatch(part):
                a, b = PARTS[part]
                sp.wait_ge(s_routed, part + 1)
                sp.wait_ge(s_tok_st[0], b * 16)
                load_dispatch(a, 0, part == 0)
                load_dispatch(a + 1, 1, part == 0)
                if part == 0:
                    with sp.Fori(a // 2 + 1, b // 2) as i:
                        load_dispatch(i * 2, 0, False)
                        load_dispatch(i * 2 + 1, 1, False)

            def sp_step_sending(p, groups):
                a, b = PARTS[1]
                pairs = list(range(a + 2, b))
                for k, g in enumerate(groups):
                    load_up(g, k % 2)
                    load_down(g, k % 2)
                    for j in pairs[4 * k:(4 * k + 4 if k < 3 else None)]:
                        load_dispatch(j, j % 2, False)
                store_pair(p - 1, False)
                sp.wait_ge(s_res_st[0], p * 16)
                load_x_single(p)

            def sp_any_step(p, groups):
                if isinstance(p, int) and p == FFN_STEPS[1][0] - 1:
                    sp_step_sending(p, groups)
                else:
                    sp_step_all(p, groups)

            def tokens_sent(p):
                for part in range(2):
                    if p == FFN_STEPS[part][0]:
                        for s in range(2):
                            sp.wait_ge(s_sent[s], 64 * PARTS[part][1] // 2)

            run_steps(sp, sp_any_step, dispatch, begin=tokens_sent)
            def load_final(j, h, first):
                if not first:
                    hold(sp, s_out, j - 1)
                    sp.wait_ge(s_out_st[h], (j - h) * 8)
                sp.dma_start(out_ring[:, 2 * h:2 * h + 2, :], res_tiles[:, bass.ds(j * 2, 2), :]).then_inc(s_fetch_ld[h], 16)
                sp.dma_start(slot_ft[h][:, :, :], slot[:, bass.ds(j * 2, 2), :]).then_inc(s_fetch_ld[h], 16)

            def store_final(j, h):
                sp.wait_ge(s_out, j + 1)
                sp.dma_start(out_tiles[:, bass.ds(j * 2, 2), :], out_ring[:, 2 * h:2 * h + 2, :]).then_inc(s_out_st[h], 16)

            def load_left(n):
                load_up(LEFT0 + n, n % 2)
                load_down(LEFT0 + n, n % 2)
            load_left(0)
            load_left(1)
            store_pair(PAIRS - 1, False)
            a, b = PARTS[2]
            pairs = iter(range(a, b))
            load_final(0, 0, True)
            load_final(1, 1, True)
            for n in range(2, LEFT):
                load_left(n)
                if n - 2 < DONE:
                    store_final(n - 2, n % 2)
                if n < DONE:
                    load_final(n, n % 2, False)
                if n >= ROUTED_AT:
                    if n == ROUTED_AT:
                        sp.wait_ge(s_routed, 3)
                        sp.wait_ge(s_tok_st[0], b * 16)
                    for j in itertools.islice(pairs, 1):
                        load_dispatch(j, (j - a) % 2, False)
            assert next(pairs, None) is None

            for s in range(2):
                sp.wait_ge(s_sent[s], 64 * (ceil_div(PAIRS, 2) if s == 0 else PAIRS // 2))
            g2 = G0[2]
            def load_group(g, h):
                load_up(g, h)
                load_down(g, h)

            def sp_round(i, last):
                for h in range(2):
                    store_final(i * 2 + (DONE + h - 2), h)
                    if not last:
                        load_up(i * 2 + (g2 + 2 + h), h)
                    load_final(i * 2 + (DONE + h), h, False)
                    if not last:
                        load_down(i * 2 + (g2 + 2 + h), h)
            load_group(g2, 0)
            load_group(g2 + 1, 1)
            load_final(DONE, 0, False)
            load_final(DONE + 1, 1, False)
            load_group(g2 + 2, 0)
            load_group(g2 + 3, 1)
            with sp.Fori(1, MIXED - 1) as i:
                sp_round(i, False)
            sp_round(MIXED - 1, True)
            for j in range(PARTS[1][1], PAIRS):
                h = j % 2
                store_final(j - 2, h)
                sp.wait_ge(s_out_st[h], (j - h) * 8)
                sp.dma_start(out_ring[:, 2 * h:2 * h + 2, :], res_tiles[:, j * 2:j * 2 + 2, :]).then_inc(s_fetch_ld[h], 16)
            store_final(PAIRS - 2, 1)
            sp.wait_ge(s_out, PAIRS)
            sp.dma_start(out[(TILES - 2) * P:(TILES - 1) * P, :], out_ring[:, 0, :]).then_inc(s_out_st[0], 16)
            sp.dma_start(out[(TILES - 1) * P:N, :], out_ring[0:LAST, 1, :]).then_inc(s_out_st[0], 16)
            sp.wait_ge(s_out_st[0], 16 * (PAIRS // 2 + 2))
            sp.wait_ge(s_out_st[1], 16 * (PAIRS // 2))

        @block.gpsimd
        def _(pool):
            q = nc.gpsimd
            own = Steps(pool, s_pool)
            q.memset(ident[:, :], 0.0)
            q.memset(ones[:, :], 1.0)
            q.iota(page_last[:, :], pattern=[[0, 1]], base=PAGES - 1, channel_multiplier=PAGES, allow_small_or_imprecise_dtypes=True)
            own(q.iota(iota_row[:, :], pattern=[[1, P]], base=0, channel_multiplier=0, allow_small_or_imprecise_dtypes=True))
            q.affine_select(out=ident[:, :], in_=ident[:, :], compare_op=ALU.not_equal, fill=1.0,
                            base=0, pattern=[[-1, P]], channel_multiplier=1)
            q.affine_select(out=real_row[:, :], in_=ones[:, 0:1], compare_op=ALU.is_gt, fill=0.0,
                            base=LAST, pattern=[[0, 1]], channel_multiplier=-1)
            q.memset(kept[:, :], 0.0)
            q.memset(st[:, 0:4], 0.0)
            q.memset(st[:, 5:8], 0.0)
            q.iota(st[:, 4:5], pattern=[[0, 1]], base=0, channel_multiplier=PAGES, allow_small_or_imprecise_dtypes=True)
            for s in range(2):
                q.memset(M[s][:, :, 2 * SL:2 * SL + 1], 1.0)
            own(q.affine_select(out=lower[:, :], in_=ones[:, :], compare_op=ALU.is_gt, fill=0.0,
                                base=0, pattern=[[1, P]], channel_multiplier=-1))
            pool.sem_inc(s_pool_const, 1)

            def weights(k, s, first):
                hold(pool, s_slot_of, k + 1)
                if not first:
                    hold(pool, s_main, k - 1)
                q.tensor_tensor(M[s][:, :, 1:2 * SL:2], at_slot[s].rearrange("p a c -> p c a"), edge_f[s][:, :, 1:2].broadcast_to([P, BC, SL]),
                                ALU.mult).then_inc(s_m2, 1)

            T = TILES

            def list_pages(k, s, first):
                hold(pool, s_lists, k + 1)
                if not first:
                    hold(pool, s_page_st[s], (k - s) * 8)
                ls = lists[s][0:T, :]
                pairs = ls[:, 0:2 * SL].rearrange("p (a f) -> p a f", f=2)
                fill, filled, full, still, number, peak = (st[0:T, j:j + 1] for j in range(6))
                q.tensor_scalar(here[0:T, :], iota_row[0:T, 0:SL], fill, None, ALU.is_ge)
                own(q.tensor_tensor(filled, fill, ls[:, 2 * SL:2 * SL + 1], ALU.add), s_held)
                q.tensor_scalar(full, filled, float(SL), None, ALU.is_ge)
                q.tensor_scalar(still, filled, float(SL), None, ALU.is_lt)
                own(q.tensor_tensor(part_page[0:T, :].rearrange("p (a f) -> p a f", f=2), pairs,
                                    here[0:T, :, None].broadcast_to([T, SL, 2]), ALU.mult), s_held)
                q.tensor_scalar(page_row[s][0:T, :], number, page_last[0:T, :], None, ALU.min)
                q.tensor_scalar(peak, peak, ls[:, 2 * SL:2 * SL + 1], None, ALU.max)
                q.tensor_tensor(late[0:T, :], ls[:, 0:2 * SL], part_page[0:T, :], ALU.subtract)
                own(q.tensor_tensor(page[s][0:T, :], kept[0:T, :], part_page[0:T, :], ALU.add), s_held)
                if not (first and s == 0):
                    hold(pool, s_page_st[1 - s], (k + s) * 8 if s == 0 else (k + 1) * 8)
                q.indirect_dma_start(out=pages[:, :], out_offset=bass.IndirectOffsetOnAxis(ap=page_row[s][0:T, 0:1], axis=0),
                                     in_=page[s][0:T, :], in_offset=None, compute_op=ALU.bypass).then_inc(s_page_st[s], 16)
                q.tensor_tensor(number, number, full, ALU.add)
                own(q.tensor_scalar(kept[0:T, :], page[s][0:T, :], still, None, ALU.mult), s_held)
                q.tensor_scalar(full, full, -float(SL), None, ALU.mult)
                own(q.tensor_tensor(kept[0:T, :], kept[0:T, :], late[0:T, :], ALU.add), s_held)
                own(q.tensor_tensor(fill, filled, full, ALU.add), s_held)
                pool.sem_inc(s_listed, 1)

            SP_ = 6
            pool.wait_ge(s_cleared, 16 * (PAGES + 1))
            weights(0, 0, True)
            weights(1, 1, True)
            list_pages(0, 0, True)
            weights(2, 0, False)
            list_pages(1, 1, True)
            with pool.Fori(1, BLOCKS // 2 - 1) as i:
                own.enter(i, 1, 2 * SP_)
                weights(i * 2 + 1, 1, False)
                list_pages(i * 2, 0, False)
                weights(i * 2 + 2, 0, False)
                list_pages(i * 2 + 1, 1, False)
            own.leave(BLOCKS // 2 - 2)
            weights(BLOCKS - 1, 1, False)
            list_pages(BLOCKS - 2, 0, False)
            list_pages(BLOCKS - 1, 1, False)
            pool.wait_ge(s_page_st[0], 16 * (BLOCKS // 2))
            pool.wait_ge(s_page_st[1], 16 * (BLOCKS // 2))
            own(q.tensor_scalar(page_row[0][0:T, :], st[0:T, 4:5], page_last[0:T, :], None, ALU.min))
            q.indirect_dma_start(out=pages[:, :], out_offset=bass.IndirectOffsetOnAxis(ap=page_row[0][0:T, 0:1], axis=0),
                                 in_=kept[0:T, :], in_offset=None, compute_op=ALU.bypass).then_inc(s_page_st[0], 16)

            over = st[0:T, 6:8]
            q.tensor_scalar(over[:, 0:1], st[0:T, 5:6], float(SL), None, ALU.is_gt)
            q.tensor_scalar(over[:, 1:2], st[0:T, 4:5], page_last[0:T, :], None, ALU.is_gt).then_inc(s_over, 1)

            pool.wait_ge(s_hw_st, 16 * ROUNDS0)

            def column(c, first):
                hold(pool, s_column, c + 1)
                q.indirect_dma_start(out=c_feat[:, :], out_offset=None, in_=features[:, :],
                                     in_offset=bass.IndirectOffsetOnAxis(ap=c_dst[:, 0:1], axis=0),
                                     compute_op=ALU.bypass).then_inc(s_feat_ld, 16)
                q.indirect_dma_start(out=c_sum[:, :], out_offset=None, in_=sums[:, :],
                                     in_offset=bass.IndirectOffsetOnAxis(ap=c_src[:, 0:1], axis=0),
                                     compute_op=ALU.bypass).then_inc(s_sum_ld, 16)
                hold(pool, s_column_sum, c + 1)
                q.indirect_dma_start(out=sums[:, :], out_offset=bass.IndirectOffsetOnAxis(ap=c_src[:, 0:1], axis=0),
                                     in_=c_sum[:, :], in_offset=None, compute_op=ALU.bypass).then_inc(s_column_st, 16)

            with pool.If(overflowed(pool) > 0):
                q.iota(c_word[:, :], pattern=[[P, TILES]], base=1, channel_multiplier=PACK + 1).then_inc(s_sum_words, 1)
                pool.wait_ge(s_sums_zero, 16 * (NOBUCKET + 1) // 4)
                column(0, True)
                with pool.Fori(1, COLS + 1) as c:
                    column(c, False)
                pool.wait_ge(s_sums_copied, 16)

            def gather_tile(p, s):
                if not is_first(p):
                    hold(pool, s_agg, p * 2 + (s - 1))
                hold(pool, s_staged, p * 2 + (s + 1))
                for c in range(CPT):
                    q.indirect_dma_start(
                        out=gathered[:, s * CPT + c, :], out_offset=None, in_=features[:, :],
                        in_offset=bass.IndirectOffsetOnAxis(ap=idx[s][:, c:c + 1], axis=0),
                        compute_op=ALU.bypass).then_inc(s_gathered[s], 16)

            def gather_pair(p):
                gather_tile(p, 0)
                gather_tile(p, 1)

            def send(j, h, last):
                hold(pool, s_tok_ld[h], (j + (2 - h)) * 16)
                for t in range(2):
                    parts = LAST if last and t == 1 else P
                    for k in range(2):
                        q.indirect_dma_start(
                            out=expert_in[:, :],
                            out_offset=bass.IndirectOffsetOnAxis(ap=slot_st[h][0:parts, t, k:k + 1], axis=0),
                            in_=tok_ring[0:parts, 2 * h + t, :], in_offset=None,
                            compute_op=ALU.bypass).then_inc(s_sent[h], 16)

            def send_part(part):
                a, b = PARTS[part]
                with pool.Fori(0, (b - a) // 2) as i:
                    send(i * 2 + a, 0, False)
                    send(i * 2 + (a + 1), 1, False)
                if (b - a) % 2:
                    send(b - 1, 0, b == PAIRS)

            def gather_run(a, b):
                if a == 0:
                    gather_pair(0)
                    a = 1
                with pool.Fori(a, b) as p:
                    gather_pair(p)
            gather_run(0, PARTS[0][1] + 2)
            pool.wait_ge(s_exp_zero, 16 * (GROUPS // 2))
            send_part(0)
            gather_run(PARTS[0][1] + 2, FFN_STEPS[1][0])
            send_part(1)
            gather_run(FFN_STEPS[1][0], PAIRS)

            def take(h, slots, last, answers):
                for t in range(2):
                    parts = LAST if last and t == 1 else P
                    for k in range(2):
                        q.indirect_dma_start(
                            out=y_ring[0:parts, 4 * h + 2 * t + k, :], out_offset=None, in_=answers,
                            in_offset=bass.IndirectOffsetOnAxis(ap=slots[0:parts, t, k:k + 1], axis=0),
                            compute_op=ALU.bypass).then_inc(s_fetched[h], 16)

            def fetch(j, h, first, last, answers):
                if not first:
                    hold(pool, s_out, j - 1)
                hold(pool, s_fetch_ld[h], (j + (2 - h)) * 16)
                take(h, slot_ft[h], last, answers)
            for s in range(2):
                pool.wait_ge(s_y_st[s], 16 * (G0[1] // 2))
            for j in range(DONE):
                fetch(j, j % 2, j < 2, False, expert_out[0:G0[1] * GT, :])
            send_part(2)

            for s in range(2):
                pool.wait_ge(s_y_st[s], 16 * (G0[2] // 2))
            earlier = expert_out[0:G0[2] * GT, :]
            with pool.Fori(DONE // 2, PARTS[1][1] // 2) as i:
                fetch(i * 2, 0, False, False, earlier)
                fetch(i * 2 + 1, 1, False, False, earlier)
            for s in range(2):
                pool.wait_ge(s_y_st[s], 16 * (GROUPS // 2))
            pool.wait_ge(s_routed, 3)
            for j in range(PARTS[1][1], PAIRS):
                pool.wait_ge(s_out, j - 1)
                take(j % 2, slot[:, j * 2:j * 2 + 2, :], j == PAIRS - 1, expert_out[:, :])

        @block.vector
        def _(dve):
            v = nc.vector
            step = Steps(dve, s_dve)
            v.memset(src_raw[:, COLS:COLS + 1], NOBUCKET * P)
            v.memset(dst_raw[:, COLS:COLS + 1], 0)
            v.memset(zeros[:, :], 0.0)
            v.memset(eps[:, :], EPS)
            v.memset(w_raw[:, COLS:COLS + 1], 0.0).then_inc(s_zero, 1)
            v.memset(small0[:, :], 0.0)
            v.memset(small[:, :], 0.0)
            v.memset(seen[:, :], 0)
            for s in range(2):
                v.memset(oh[s][:, :, 0:2], 0.0)
            v.memset(hi[:, COLS:EC], float(NOBUCKET))
            v.memset(fields[:, COLS:EC, :], 0.0)
            step(v.memset(reset[:, :], 1.0))
            step(v.memset(reset.rearrange("p (b c) -> p b c", c=W_)[:, :, 0:2], 0.0))

            dve.wait_ge(s_edge_ld, 16 * 6)
            src_hi = ohf_a.rearrange("p a b -> p (a b)").bitcast(i32)[:, 0:COLS + 1]
            src_lo = ohf_b.rearrange("p a b -> p (a b)").bitcast(i32)[:, 0:COLS + 1]
            v.tensor_single_scalar(src_hi, src_raw, 7, ALU.arith_shift_right)
            v.tensor_copy(fields[:, 0:COLS + 1, 1], w_raw)
            step(v.tensor_single_scalar(src_lo, src_raw, P - 1, ALU.bitwise_and))
            v.tensor_copy(hi[:, 0:COLS + 1], src_hi)
            step(v.scalar_tensor_tensor(fields[:, 0:COLS + 1, 0], src_lo, float(PACK), dst_raw, ALU.mult, ALU.add))
            step(v.tensor_scalar(fields[:, 0:COLS + 1, 0], fields[:, 0:COLS + 1, 0], 1.0, None, ALU.add))
            dve.wait_ge(s_pool_const, 1)
            v.tensor_copy(lower_bf[:, :], lower[:, :])
            v.tensor_copy(ones_bf[:, :], ones[:, :])
            v.tensor_copy(slot_no, iota_row[:, 0:SL, None].broadcast_to([P, SL, BC]))
            step(v.tensor_copy(bucket_no, iota_row[:, 0:TILES, None].broadcast_to([P, TILES, BC])))
            step(v.tensor_scalar(falling[:, :], iota_row[:, 0:NE], -1.0, float(NE), ALU.mult, ALU.add))

            def buckets(k, s, first):
                if not first:
                    dve.wait_ge(s_ohf, k - 1)
                v.tensor_tensor(oh[s][:, :, 2:W_], hi[:, None, bass.ds(k * BC, BC)].broadcast_to([P, TILES, BC]),
                                bucket_no, ALU.is_equal).then_inc(s_oh, 1)

            def places(k, s, first):
                dve.wait_ge(s_base, k + 1)
                step(v.scalar_tensor_tensor(oh[s][:, :, 1], ps[:, 4 + s, 0:TILES], -1.0, seen[:, :], ALU.add, ALU.add))
                step(v.tensor_tensor(seen[:, :], ps[:, 4 + s, P:P + TILES], seen[:, :], ALU.add))
                v.tensor_single_scalar(seen[:, :], seen[:, :], SL - 1, ALU.bitwise_and)
                step(v.tensor_tensor_scan(cum.rearrange("p b c -> p (b c)"), reset,
                                          oh[s].rearrange("p b c -> p (b c)"), 0.0, ALU.mult, ALU.add))
                step(v.tensor_tensor(prod, cum[:, :, 2:W_], oh[s][:, :, 2:W_], ALU.mult))
                n = TILES
                while n > 13:
                    h = n // 2
                    step(v.tensor_tensor(prod[:, 0:h, :], prod[:, 0:h, :], prod[:, n - h:n, :], ALU.add))
                    n -= h
                step(v.tensor_reduce(place_sum[:, :], prod[:, 0:n, :].rearrange("p b c -> p c b"), AX.X, ALU.add))
                step(v.tensor_scalar(wrap[:, :], place_sum[:, :], float(SL), -float(SL), ALU.is_ge, ALU.mult))
                if not first:
                    dve.wait_ge(s_m2, k - 1)
                    dve.wait_ge(s_main, k - 1)
                v.tensor_copy(edge_f[s][:, :, :], fields[:, bass.ds(k * BC, BC), :])
                step(v.tensor_tensor(slot_of[:, :], place_sum[:, :], wrap[:, :], ALU.add))
                step(v.tensor_tensor(at_slot[s], slot_no, slot_of[:, None, :].broadcast_to([P, SL, BC]), ALU.is_equal))
                dve.sem_inc(s_slot_of, 1)
                v.tensor_tensor(M[s][:, :, 0:2 * SL:2], at_slot[s].rearrange("p a c -> p c a"),
                                edge_f[s][:, :, 0:1].broadcast_to([P, BC, SL]), ALU.mult).then_inc(s_m1, 1)

            stt0, mv0, rs0 = small0[0:R0, 0:24], small0[0:R0, 24:32], small0[0:R0, 32:36]

            def stats0(i):
                dve.wait_ge(s_xin, i * 16 + 16)
                stt, mv = stt0, mv0
                dve.sem_inc(s_held, 1)
                for t in range(T0):
                    last = v.bn_stats(stt[:, 6 * t:6 * t + 6], xin[:, t, :])
                step(last, s_held)
                for t in range(T0):
                    last = v.bn_aggr(mv[:, 2 * t:2 * t + 2], stt[:, 6 * t:6 * t + 6])
                last.then_inc(s_var0, 1)

            def norm0(i, first):
                mv, rs = mv0, rs0
                dve.wait_ge(s_std0, i + 1)
                step(v.reciprocal(rs, rs))
                if not first:
                    dve.wait_ge(s_xT0_ps, i)
                for t in range(T0):
                    last = v.tensor_scalar(xn0[:, t, :], xin[:, t, :], mv[:, 2 * t:2 * t + 1], rs[:, t:t + 1],
                                           ALU.subtract, ALU.mult)
                last.then_inc(s_xn0, 1)

            SA, SN = 11, 2

            def two_blocks(i, first, features):
                buckets(i * 2 + 1, 1, first)
                places(i * 2, 0, first)
                if features:
                    stats0(i)
                buckets(i * 2 + 2, 0, False)
                places(i * 2 + 1, 1, first)
                if features:
                    norm0(i, first)
            buckets(0, 0, True)
            two_blocks(0, True, True)
            with dve.Fori(1, ROUNDS0) as i:
                step.enter(i, 1, 2 * SA + SN)
                two_blocks(i, False, True)
            step.leave(ROUNDS0 - 1)
            with dve.Fori(ROUNDS0, BLOCKS // 2) as i:
                step.enter(i, ROUNDS0, 2 * SA)
                two_blocks(i, False, False)
            step.leave(BLOCKS // 2 - ROUNDS0)

            dve.wait_ge(s_over_ps, 1)
            step(v.tensor_reduce(over_sum[0:1, :], ps[0:1, 5, 0:2], AX.X, ALU.add))
            step(v.tensor_copy(flag[0:1, :], over_sum[0:1, :]))
            dve.sem_inc(s_flag, 1)
            dve.wait_ge(s_rec_ld, 16 * 2)

            own = Steps(dve, s_column_dve)

            def column(c, first):
                if not first:
                    dve.wait_ge(s_column_st, c * 16)
                v.tensor_copy(c_src[:, :], src_raw[:, bass.ds(c, 1)])
                v.tensor_scalar(c_dst[:, :], dst_raw[:, bass.ds(c, 1)], 1.0, None, ALU.add)
                v.tensor_copy(c_edge[:, 1:2], w_raw[:, bass.ds(c, 1)])
                own(v.tensor_copy(c_edge[:, 0:1], src_raw[:, bass.ds(c, 1)]))
                own(v.tensor_copy(c_wide[:, :], c_edge[:, 0:1].broadcast_to([P, P])))
                dve.sem_inc(s_column, 1)
                dve.wait_ge(s_wide_T, c + 1)
                v.tensor_scalar(c_same[:, :], ps[:, 6, 0:P], c_edge[:, 0:1], c_edge[:, 1:2],
                                ALU.is_equal, ALU.mult).then_inc(s_same, 1)
                dve.wait_ge(s_column_ps, c + 1)
                dve.wait_ge(s_sum_ld, c * 16 + 16)
                v.tensor_tensor(c_sum[:, :], c_sum[:, :], ps[:, 7, 0:D], ALU.add).then_inc(s_column_sum, 1)

            with dve.If(overflowed(dve) > 0):
                column(0, True)
                with dve.Fori(1, COLS + 1) as c:
                    own.enter(c, 1, 2)
                    column(c, False)
                own.leave(COLS)
                dve.wait_ge(s_column_st, (COLS + 1) * 16)
                dve.wait_ge(s_sum_words, 1)
                own(v.memset(rec[:, :, :], 0.0))
                v.tensor_copy(rec[:, 0:TILES * CPT:CPT, 0], c_word[:, :])
                own(v.memset(rec[:, 0:TILES * CPT:CPT, 1], 1.0))

            step(v.tensor_copy(row_word, rec[:, :, 0]))
            step(v.tensor_single_scalar(src_row, row_word, PACK - 1, ALU.bitwise_and))
            v.tensor_scalar(src_row, src_row, float(N), None, ALU.min)
            step(v.tensor_single_scalar(row_word, row_word, 14, ALU.arith_shift_right))
            step(v.tensor_copy(row_f, row_word))
            dve.sem_inc(s_split, 1)

            def onehots(t, s, first):
                dve.wait_ge(s_staged, t + 1)
                if not first:
                    dve.wait_ge(s_agg, t - 1)
                for c in range(CPT):
                    last = v.tensor_scalar(onehot_w[:, s * CPT + c, :], iota_row[:, :], row_w[s][:, c, 0:1],
                                           row_w[s][:, c, 1:2], ALU.is_equal, ALU.mult)
                last.then_inc(s_onehot, 1)

            def residual_sum(p):
                dve.wait_ge(s_x_ld[0], p * 16 + (32 if is_last(p) else 16))
                for s in range(2):
                    dve.wait_ge(s_agg, p * 2 + (s + 1))
                    last = v.tensor_tensor(xpair[:, s, :], xpair[:, s, :], ps[:, AGG + s, 0:D], ALU.add)
                    last.then_inc(s_x1, 1)
                dve.wait_ge(s_x1, p * 2 + 2)

            def norms(p, first):
                a, n = xpair[:, 0:2, :], norm
                stt, mv, rs = small[:, 0:12], small[:, 12:16], small[:, 16:18]
                step(v.tensor_tensor(a, a, rows[:, 0:1, :].broadcast_to([P, 2, D]), ALU.add), s_held)
                for r in range(2):
                    inp = n if r else a
                    for t in range(2):
                        last = v.bn_stats(stt[:, 6 * t:6 * t + 6], inp[:, t, :])
                    step(last, s_held)
                    for t in range(2):
                        last = v.bn_aggr(mv[:, 2 * t:2 * t + 2], stt[:, 6 * t:6 * t + 6])
                    last.then_inc(s_var, 1)
                    dve.wait_ge(s_std, p * 2 + (r + 1))
                    step(v.reciprocal(rs, rs))
                    for t in range(2):
                        last = v.tensor_scalar(n[:, t, :], inp[:, t, :], mv[:, 2 * t:2 * t + 1], rs[:, t:t + 1],
                                               ALU.subtract, ALU.mult)
                    step(last, s_held)
                step(v.tensor_tensor(n, n, rows[:, 1:2, :].broadcast_to([P, 2, D]), ALU.mult))
                if not first:
                    dve.wait_ge(s_tokT_ps, p)
                    dve.wait_ge(s_tok_st[0], p * 16)
                v.tensor_tensor(tok[:, 0:2, :], n, rows[:, 2:3, :].broadcast_to([P, 2, D]), ALU.add).then_inc(s_tok, 1)

            def scores(p):
                dve.wait_ge(s_logit_ps, p + 1)
                v.tensor_tensor(logits[:, bass.ds(p * 2, 2), :], ps[:, LOGIT, 0:2 * NE].rearrange("p (t e) -> p t e", t=2),
                                br_row[:, None, :].broadcast_to([P, 2, NE]), ALU.add).then_inc(s_logit, 1)

            def move_xT(g):
                dve.wait_ge(s_xT_ps, g + 1)
                if not (isinstance(g, int) and g == 0):
                    dve.wait_ge(s_h_ps, g * KH)
                v.tensor_copy(xT[:, :, :], ps[:, XT, :].rearrange("p (k t) -> p k t", k=KD)).then_inc(s_xT, 1)

            def add_b2(g, h):
                dve.wait_ge(s_y_ps, g + 1)
                if not (isinstance(g, int) and g < 2):
                    dve.wait_ge(s_y_st[h], (g - h) * 8)
                v.tensor_tensor(ysb[:, 2 * h:2 * h + 2, :], ps[:, YB, :].rearrange("p (j d) -> p j d", j=2),
                                b2g[:, h:h + 1, :].broadcast_to([P, 2, D]), ALU.add).then_inc(s_y, 1)

            def experts(groups, k0):
                for k, g in enumerate(groups):
                    move_xT(g)
                    if not (isinstance(g, int) and g == 0):
                        add_b2(g - 1, (k0 + k + 1) % 2)

            SD = 8

            def dve_step(p, groups):
                m = len(groups) // 2
                if not is_first(p):
                    residual_sum(p - 1)
                onehots(p * 2 + 1, 1, is_first(p))
                if not is_first(p):
                    norms(p - 1, isinstance(p, int) and p == 1)
                experts(groups[:m], 0)
                if not is_last(p):
                    onehots(p * 2 + 2, 0, False)
                experts(groups[m:], m)
                if not is_first(p):
                    scores(p - 1)

            def route(part, beside=lambda: None):
                a, b = PARTS[part]
                t0, nt = 2 * a, 2 * (b - a)
                kt = 2 * nt
                dve.wait_ge(s_logit, b)
                L = logits[:, t0:t0 + nt, :]

                def wide(z):
                    return z[:, 0:nt, None].broadcast_to([P, nt, NE])
                fall = falling[:, None, :].broadcast_to([P, nt, NE])
                eq_, sc_, rl_ = eq[:, 0:nt, :], score[:, 0:nt, :], rlog[:, 0:nt, :]
                cur = L
                for k, mx in enumerate((m1, m2)):
                    beside()
                    pickd = oh12[:, k * nt:(k + 1) * nt, :]
                    step(v.tensor_reduce(mx[:, 0:nt], cur, AX.X, ALU.max))
                    step(v.tensor_tensor(eq_, cur, wide(mx), ALU.is_equal))
                    step(v.tensor_tensor(sc_, eq_, fall, ALU.mult))
                    step(v.tensor_reduce(pick[:, 0:nt], sc_, AX.X, ALU.max))
                    step(v.tensor_tensor(pickd, fall, wide(pick), ALU.is_equal))
                    if k == 0:
                        step(v.scalar_tensor_tensor(rl_.rearrange("p a b -> p (a b)"), pickd.rearrange("p a b -> p (a b)"),
                                                    -3.0e38, L.rearrange("p a b -> p (a b)"), ALU.mult, ALU.add))
                        cur = rl_
                v.tensor_tensor(pick[:, 0:nt], m2[:, 0:nt], m1[:, 0:nt], ALU.subtract).then_inc(s_gap, 1)
                beside()
                if b == PAIRS:
                    for k in range(2):
                        z = oh12[:, (k + 1) * nt - 1, :]
                        step(v.tensor_scalar(z, z, real_row[:, 0:1], None, ALU.mult))
                dve.wait_ge(s_exp, part + 1)
                g1, g2 = gate[:, 0, t0:t0 + nt], gate[:, 1, t0:t0 + nt]
                step(v.tensor_scalar(m1[:, 0:nt], m2[:, 0:nt], 1.0, None, ALU.add))
                step(v.reciprocal(g1, m1[:, 0:nt]))
                step(v.tensor_tensor(g2, m2[:, 0:nt], g1, ALU.mult))

                ww = kt + 1
                rd = rdata.rearrange("p e t -> p (e t)")[:, 0:NE * ww]
                rr, rc_ = rreset[:, 0:NE * ww], rcum.rearrange("p e t -> p (e t)")[:, 0:NE * ww]
                rd3, rr3, rc3 = (z.rearrange("p (e t) -> p e t", e=NE) for z in (rd, rr, rc_))
                step(v.tensor_copy(rd3[:, :, 1:ww], oh12[:, 0:kt, :].rearrange("p t e -> p e t")))
                step(v.memset(rr, 1.0))
                step(v.memset(rr3[:, :, 0:1], 0.0))
                step(v.tensor_reduce(rsmall[:, 0, :], rd3[:, :, 1:ww], AX.X, ALU.add))
                dve.sem_inc(s_rhist, 1)
                dve.wait_ge(s_rprefix, part + 1)
                first_, end_ = rsmall[:, 1, :], rsmall[:, 2, :]
                step(v.tensor_scalar(rcount[:, :], ps[:, LOGIT, 2 * P:2 * P + NE], float(GT - 1), None, ALU.add))
                step(v.tensor_single_scalar(rcount[:, :], rcount[:, :], 8, ALU.arith_shift_right))
                step(v.tensor_copy(first_, rcount[:, :]))
                step(v.tensor_tensor_scan(end_, ones[:, 0:NE], first_, 0.0, ALU.mult, ALU.add))
                step(v.tensor_tensor(first_, end_, first_, ALU.subtract))
                step(v.tensor_scalar(first_, first_, float(GT), float(G0[part] * GT - 1), ALU.mult, ALU.add))
                step(v.tensor_tensor(rd3[:, :, 0], ps[:, LOGIT, P:P + NE], first_, ALU.add))
                step(v.tensor_tensor_scan(rc_, rr, rd, 0.0, ALU.mult, ALU.add))
                step(v.tensor_tensor(rc3[:, :, 1:ww], rc3[:, :, 1:ww], rd3[:, :, 1:ww], ALU.mult))
                beside()
                rank_f = eq.rearrange("p a b -> p (a b)")[:, 0:kt]
                step(v.tensor_reduce(rank_f, rc3[:, :, 1:ww].rearrange("p e t -> p t e"), AX.X, ALU.add))
                step(v.tensor_copy(slot[:, t0:t0 + nt, :].rearrange("p t k -> p k t"), rank_f.rearrange("p (k t) -> p k t", k=2)))
                ng = NG[part]
                ge = rcum.rearrange("p e t -> p (e t)")[0:1, 0:NE * ng].rearrange("p (e g) -> p e g", e=NE)
                gf = score.rearrange("p a b -> p (a b)")[0:1, 0:ng]
                step(v.tensor_tensor(ge, iota_row[0:1, None, 0:ng].broadcast_to([1, NE, ng]),
                                     end_[0:1, :, None].broadcast_to([1, NE, ng]), ALU.is_ge))
                step(v.tensor_reduce(gf, ge.rearrange("p e g -> p g e"), AX.X, ALU.add))
                step(v.tensor_scalar(gf, gf, float(NE - 1), None, ALU.min))
                v.tensor_copy(group_ids[0:1, G0[part]:G0[part] + ng], gf)
                step(v.memset(group_new[0:1, G0[part]:G0[part] + 2], 1))
                step(v.tensor_tensor(group_new[0:1, G0[part] + 2:G0[part] + ng], gf[:, 2:ng], gf[:, 0:ng - 2], ALU.not_equal))
                dve.sem_inc(s_routed, 1)

            onehots(0, 0, True)
            run_steps(dve, dve_step, route, step, SD)
            def final(j, h, last):
                if isinstance(j, int) and j >= PARTS[1][1]:
                    dve.wait_ge(s_fetch_ld[h], 32 * (PARTS[1][1] // 2) + 16 * ((j - PARTS[1][1]) // 2 + 1))
                hold(dve, s_fetched[h], (j + (2 - h)) * 32)
                for k in range(2):
                    for t in range(2):
                        n = LAST if last and t == 1 else P
                        o = out_ring[0:n, 2 * h + t, :]
                        ins = v.scalar_tensor_tensor(o, y_ring[0:n, 4 * h + 2 * t + k, :],
                                                     gate[0:n, k, bass.ds(j * 2 + t, 1)], o, ALU.mult, ALU.add)
                    if k == 0:
                        step(ins)
                ins.then_inc(s_out, 1)
            left = iter(range(LEFT))

            def beside():
                n = next(left)
                move_xT(LEFT0 + n)
                add_b2(LEFT0 + n - 1, (n + 1) % 2)
                if 1 <= n <= DONE:
                    final(n - 1, (n - 1) % 2, False)

            residual_sum(PAIRS - 1)
            beside()
            norms(PAIRS - 1, False)
            for _ in range(1, EARLY):
                beside()
            scores(PAIRS - 1)
            route(2, beside)
            for _ in range(LEFT - ROUTED_AT):
                beside()
            add_b2(G0[2] - 1, 1)

            g2 = G0[2]
            move_xT(g2)
            move_xT(g2 + 1)
            add_b2(g2, 0)
            with dve.Fori(1, MIXED) as i:
                step.enter(i, 1, 2)
                move_xT(i * 2 + g2)
                add_b2(i * 2 + (g2 - 1), 1)
                final(i * 2 + (DONE - 2), 0, False)
                move_xT(i * 2 + (g2 + 1))
                add_b2(i * 2 + g2, 0)
                final(i * 2 + (DONE - 1), 1, False)
            step.leave(MIXED - 1)
            add_b2(GROUPS - 1, 1)
            for j in range(PARTS[1][1] - 2, PAIRS - 1):
                final(j, j % 2, False)
            final(PAIRS - 1, 0, True)

        @block.scalar
        def _(act):
            a = nc.scalar
            act.wait_ge(s_zero, 1)

            def convert(k, s, first):
                act.wait_ge(s_oh, k + 1)
                if not first:
                    act.wait_ge(s_main, k - 1)
                a.activation(ohf[s], oh[s][:, :, 2:W_], ACT.Copy).then_inc(s_ohf, 1)

            def lists_out(k, s, first):
                act.wait_ge(s_main, k + 1)
                if not first:
                    act.wait_ge(s_listed, k - 1)
                a.activation(lists[s][0:TILES, :], ps[0:TILES, 6 + s, 0:2 * SL + 1], ACT.Copy).then_inc(s_lists, 1)

            def std0(i):
                act.wait_ge(s_var0, i + 1)
                a.activation(small0[0:R0, 32:36], small0[0:R0, 25:32:2], ACT.Sqrt, bias=eps[0:R0, :]).then_inc(s_std0, 1)

            def xT0_out(i):
                act.wait_ge(s_xT0_ps, i + 1)
                a.activation(xT0.rearrange("p a b -> p (a b)").rearrange("p (q c) -> p q c", q=2),
                             ps[:, 0:2, 0:T0 * KD * R0 // 2], ACT.Copy).then_inc(s_xT0, 1)

            def features_out(i, first):
                act.wait_ge(s_hw_ps, i + 1)
                if not first:
                    act.wait_ge(s_hw_st, i * 16)
                a.activation(hw_sb.rearrange("p t d -> p (t d)").rearrange("p (q c) -> p q c", q=2),
                             ps[0:R0, 2:4, :], ACT.Copy).then_inc(s_hw, 1)
                act.wait_ge(s_hw, i + 1)
                act.dma_start(feat_rounds[:, bass.ds(i * T0, T0), :], hw_sb).then_inc(s_hw_st, 16)

            def act_round(i, first, second):
                convert(i * 2 + 1, 1, first)
                if not first:
                    xT0_out(i - 1)
                lists_out(i * 2, 0, first)
                std0(i)
                convert(i * 2 + 2, 0, False)
                if not first:
                    features_out(i - 1, second)
                lists_out(i * 2 + 1, 1, first)

            act.wait_ge(s_oh, 1)
            convert(0, 0, True)
            act_round(0, True, False)
            act_round(1, False, True)
            with act.Fori(2, ROUNDS0) as i:
                act_round(i, False, False)
            xT0_out(ROUNDS0 - 1)
            features_out(ROUNDS0 - 1, False)
            with act.Fori(ROUNDS0, BLOCKS // 2 - 1) as i:
                convert(i * 2 + 1, 1, False)
                lists_out(i * 2, 0, False)
                convert(i * 2 + 2, 0, False)
                lists_out(i * 2 + 1, 1, False)
            convert(BLOCKS - 1, 1, False)
            lists_out(BLOCKS - 2, 0, False)
            lists_out(BLOCKS - 1, 1, False)

            def stage(t, s, first):
                if not first:
                    act.wait_ge(s_gathered[s], (t - s) * (CPT * 8))
                    act.wait_ge(s_onehot, t - 1)
                a.activation(row_w[s][:, :, 0], row_f[:, bass.ds(t * CPT, CPT)], ACT.Copy)
                a.activation(row_w[s][:, :, 1], rec[:, bass.ds(t * CPT, CPT), 1], ACT.Copy)
                a.activation(idx[s][:, :], src_row[:, bass.ds(t * CPT, CPT)], ACT.Copy).then_inc(s_staged, 1)

            def stds(p):
                for r in range(2):
                    act.wait_ge(s_var, p * 2 + (r + 1))
                    a.activation(small[:, 16:18], small[:, 13:16:2], ACT.Sqrt, bias=eps[:, :]).then_inc(s_std, 1)

            def move_tokT(p, first):
                act.wait_ge(s_tokT_ps, p + 1)
                if not first:
                    act.wait_ge(s_logit_ps, p)
                a.activation(tokT[:, :, :], ps[:, TOKT, :].rearrange("p (k t) -> p k t", k=2 * KD), ACT.Copy).then_inc(s_tokT, 1)

            def gelu(g, h):
                for k in range(KH):
                    if k % 2 == 0:
                        act.wait_ge(s_h_ps, g * KH + (k + 2))
                    if k == 0 and not (isinstance(g, int) and g == 0):
                        act.wait_ge(s_y_ps, g)
                    a.activation(hT[:, k, :], ps[:, HB + k // 2, GT * (k % 2):GT * (k % 2) + GT],
                                 ACT.Gelu, bias=b1g[:, h, k:k + 1]).then_inc(s_h, 1)

            def store_y(g, h):
                act.wait_ge(s_y, g + 1)
                act.dma_start(out_rows[:, bass.ds(g * 2, 2), :], ysb[:, 2 * h:2 * h + 2, :]).then_inc(s_y_st[h], 16)

            def experts(groups, k0):
                for k, g in enumerate(groups):
                    gelu(g, (k0 + k) % 2)
                    if not (isinstance(g, int) and g == 0):
                        store_y(g - 1, (k0 + k + 1) % 2)

            def act_step(p, groups):
                m = len(groups) // 2
                if not is_first(p):
                    stds(p - 1)
                if not is_last(p):
                    stage(p * 2 + 2, 0, False)
                experts(groups[:m], 0)
                if not is_last(p):
                    stage(p * 2 + 3, 1, False)
                if not is_first(p):
                    move_tokT(p - 1, isinstance(p, int) and p == 1)
                experts(groups[m:], m)

            def weigh(part):
                nt = 2 * (PARTS[part][1] - PARTS[part][0])
                act.wait_ge(s_gap, part + 1)
                a.activation(m2[:, 0:nt], pick[:, 0:nt], ACT.Exp).then_inc(s_exp, 1)

            act.wait_ge(s_split, 1)
            stage(0, 0, True)
            stage(1, 1, True)
            run_steps(act, act_step, weigh)
            def left(n):
                gelu(LEFT0 + n, n % 2)
                store_y(LEFT0 + n - 1, (n + 1) % 2)
            stds(PAIRS - 1)
            for n in range(EARLY - 1):
                left(n)
            move_tokT(PAIRS - 1, False)
            for n in range(EARLY - 1, EARLY + 2):
                left(n)
            weigh(2)
            for n in range(EARLY + 2, LEFT):
                left(n)
            store_y(G0[2] - 1, 1)
            g2 = G0[2]
            gelu(g2, 0)
            gelu(g2 + 1, 1)
            store_y(g2, 0)
            with act.Fori(1, NG[2] // 2) as i:
                gelu(i * 2 + g2, 0)
                store_y(i * 2 + (g2 - 1), 1)
                gelu(i * 2 + (g2 + 1), 1)
                store_y(i * 2 + g2, 0)
            store_y(GROUPS - 1, 1)

        @block.tensor
        def _(pe):
            mm = nc.tensor.matmul

            def T(out_, in_, n):
                return nc.tensor.transpose(out_, in_, ident[0:n, 0:n])

            pe.wait_ge(s_const_ld, 16 * 6)
            pe.wait_ge(s_pool_const, 1)

            def bases(k, s):
                pe.wait_ge(s_oh, k + 1)
                for c in range(BC):
                    mm(ps[:, 4 + s, 0:TILES], lower_bf[:, :], oh[s][:, :, 2 + c], start=(c == 0), stop=(c == BC - 1))
                for c in range(BC):
                    last = mm(ps[:, 4 + s, P:P + TILES], ones_bf[:, :], oh[s][:, :, 2 + c], start=(c == 0), stop=(c == BC - 1))
                last.then_inc(s_base, 1)

            def place(k, s, first):
                pe.wait_ge(s_ohf, k + 1)
                pe.wait_ge(s_m1, k + 1)
                pe.wait_ge(s_m2, k + 1)
                if not first:
                    pe.wait_ge(s_lists, k - 1)
                for c in range(BC):
                    last = mm(ps[0:TILES, 6 + s, 0:2 * SL + 1], ohf[s][:, :, c], M[s][:, c, :], start=(c == 0), stop=(c == BC - 1))
                last.then_inc(s_main, 1)

            def transpose_x(i):
                pe.wait_ge(s_xn0, i + 1)
                for t in range(T0):
                    for k in range(KD):
                        j = t * KD + k
                        last = T(ps[:, j // 4, R0 * (j % 4):R0 * (j % 4) + R0], xn0[:, t, k * P:(k + 1) * P], R0)
                last.then_inc(s_xT0_ps, 1)

            def feature_product(i, first):
                pe.wait_ge(s_xT0, i + 1)
                if not first:
                    pe.wait_ge(s_hw, i)
                for t in range(T0):
                    for k in range(KD):
                        last = mm(ps[0:R0, 2 + t // 2, D * (t % 2):D * (t % 2) + D], xT0[:, t * KD + k, :],
                                  Wg[:, k, :], start=(k == 0), stop=(k == KD - 1))
                last.then_inc(s_hw_ps, 1)

            def pe_round(i, first, second):
                bases(i * 2 + 1, 1)
                if not first:
                    transpose_x(i - 1)
                place(i * 2, 0, first)
                bases(i * 2 + 2, 0)
                if not first:
                    feature_product(i - 1, second)
                place(i * 2 + 1, 1, first)

            bases(0, 0)
            pe_round(0, True, False)
            pe_round(1, False, True)
            with pe.Fori(2, ROUNDS0) as i:
                pe_round(i, False, False)
            transpose_x(ROUNDS0 - 1)
            feature_product(ROUNDS0 - 1, False)
            with pe.Fori(ROUNDS0, BLOCKS // 2 - 1) as i:
                bases(i * 2 + 1, 1)
                place(i * 2, 0, False)
                bases(i * 2 + 2, 0)
                place(i * 2 + 1, 1, False)
            bases(BLOCKS - 1, 1)
            place(BLOCKS - 2, 0, False)
            place(BLOCKS - 1, 1, False)
            pe.wait_ge(s_hw, ROUNDS0)
            pe.wait_ge(s_lists, BLOCKS)
            pe.wait_ge(s_over, 1)
            mm(ps[0:1, 5, 0:2], ones[0:TILES, 0:1], st[0:TILES, 6:8], start=True, stop=True).then_inc(s_over_ps, 1)

            def column(c, first):
                pe.wait_ge(s_column, c + 1)
                T(ps[:, 6, 0:P], c_wide[:, :], P).then_inc(s_wide_T, 1)
                pe.wait_ge(s_same, c + 1)
                pe.wait_ge(s_feat_ld, c * 16 + 16)
                mm(ps[:, 7, 0:D], c_same[:, :], c_feat[:, :], start=True, stop=True).then_inc(s_column_ps, 1)

            with pe.If(overflowed(pe) > 0):
                column(0, True)
                with pe.Fori(1, COLS + 1) as c:
                    column(c, False)
            pe.wait_ge(s_split, 1)

            def sum_tile(p, s):
                pe.wait_ge(s_gathered[s], p * (CPT * 16) + CPT * 16)
                pe.wait_ge(s_onehot, p * 2 + (s + 1))
                if not is_first(p):
                    pe.wait_ge(s_x1, p * 2 + (s - 1))
                for c in range(CPT):
                    last = mm(ps[:, AGG + s, 0:D], onehot_w[:, s * CPT + c, :], gathered[:, s * CPT + c, :],
                              start=(c == 0), stop=(c == CPT - 1))
                last.then_inc(s_agg, 1)

            def transpose_tokens(p, first):
                pe.wait_ge(s_tok, p + 1)
                for t in range(2):
                    for k in range(KD):
                        j = t * KD + k
                        last = T(ps[:, TOKT, j * P:(j + 1) * P], tok[:, t, k * P:(k + 1) * P], P)
                last.then_inc(s_tokT_ps, 1)

            def router(p, first):
                pe.wait_ge(s_tokT, p + 1)
                if not first:
                    pe.wait_ge(s_logit, p)
                for t in range(2):
                    for k in range(KD):
                        last = mm(ps[:, LOGIT, t * NE:(t + 1) * NE], tokT[:, t * KD + k, :], Wr_sb[:, k, :],
                                  start=(k == 0), stop=(k == KD - 1))
                last.then_inc(s_logit_ps, 1)

            def expert_T(g, h):
                pe.wait_ge(s_ld1[h], (g - h) * 24 + 48)
                for j in range(2):
                    for k in range(KD):
                        last = T(ps[:, XT, k * GT + j * P:k * GT + (j + 1) * P], xs[:, 2 * h + j, k * P:(k + 1) * P], P)
                last.then_inc(s_xT_ps, 1)

            def expert_up(g, h):
                pe.wait_ge(s_xT, g + 1)
                if not (isinstance(g, int) and g == 0):
                    pe.wait_ge(s_h, g * KH)
                for k in range(KH):
                    for j in range(KD):
                        last = mm(ps[:, HB + k // 2, GT * (k % 2):GT * (k % 2) + GT],
                                  W1g[:, KD * h + j, k * P:(k + 1) * P], xT[:, j, :], start=(j == 0), stop=(j == KD - 1))
                    last.then_inc(s_h_ps, 1)

            def expert_down(g, h):
                pe.wait_ge(s_h, g * KH + KH)
                pe.wait_ge(s_ld2[h], (g - h) * 16 + 32)
                if not (isinstance(g, int) and g == 0):
                    pe.wait_ge(s_y, g)
                for j in range(2):
                    for k in range(KH):
                        last = mm(ps[:, YB, j * D:(j + 1) * D], hT[:, k, j * P:(j + 1) * P],
                                  W2g[:, KH * h + k, :], start=(k == 0), stop=(k == KH - 1))
                last.then_inc(s_y_ps, 1)

            def experts_after(g, h):
                if not (isinstance(g, int) and g == 0):
                    expert_down(g - 1, 1 - h)
                expert_up(g, h)

            def pe_step(p, groups):
                m = len(groups) // 2
                if m:
                    expert_T(groups[0], 0)
                sum_tile(p, 0)
                for k, g in enumerate(groups[:m]):
                    if k:
                        expert_T(g, k % 2)
                    experts_after(g, k % 2)
                if m:
                    expert_T(groups[m], m % 2)
                if not is_first(p):
                    transpose_tokens(p - 1, isinstance(p, int) and p == 1)
                sum_tile(p, 1)
                for k, g in enumerate(groups[m:]):
                    if k:
                        expert_T(g, (m + k) % 2)
                    experts_after(g, (m + k) % 2)
                if not is_first(p):
                    router(p - 1, isinstance(p, int) and p == 1)

            def count(part):
                pe.wait_ge(s_rhist, part + 1)
                mm(ps[:, LOGIT, P:P + NE], lower[:, :], rsmall[:, 0, :], start=True, stop=True)
                mm(ps[:, LOGIT, 2 * P:2 * P + NE], ones[:, :], rsmall[:, 0, :], start=True, stop=True).then_inc(s_rprefix, 1)

            run_steps(pe, pe_step, count)
            for n in range(LEFT):
                expert_T(LEFT0 + n, n % 2)
                experts_after(LEFT0 + n, n % 2)
                if n == EARLY - 2:
                    transpose_tokens(PAIRS - 1, False)
                if n == EARLY - 1:
                    router(PAIRS - 1, False)
                if n == COUNT_AT - 1:
                    count(2)
            expert_down(G0[2] - 1, 1)
            g2 = G0[2]
            expert_T(g2, 0)
            expert_up(g2, 0)
            expert_T(g2 + 1, 1)
            expert_down(g2, 0)
            expert_up(g2 + 1, 1)
            with pe.Fori(1, NG[2] // 2) as i:
                expert_T(i * 2 + g2, 0)
                expert_down(i * 2 + (g2 - 1), 1)
                expert_up(i * 2 + g2, 0)
                expert_T(i * 2 + (g2 + 1), 1)
                expert_down(i * 2 + g2, 0)
                expert_up(i * 2 + (g2 + 1), 1)
            expert_down(GROUPS - 1, 1)


def kernel(**inputs):
    import numpy as _np
    import concourse.bacc as _bacc
    from concourse import mybir as _mybir
    from concourse.bass_utils import run_bass_kernel_spmd as _run

    nc = _bacc.Bacc("TRN2", target_bir_lowering=False, num_devices=1)
    b1 = _np.asarray(inputs["L0_ffn_b1"])
    given = {
        "x": inputs["x"], "src": inputs["src"], "dst": inputs["dst"], "edge_weight": inputs["edge_weight"],
        "gnn_W": inputs["L0_gnn_W"], "gnn_b": inputs["L0_gnn_b"], "gamma": inputs["L0_ffn_gamma"],
        "beta": inputs["L0_ffn_beta"], "Wr": inputs["L0_ffn_Wr"], "br": inputs["L0_ffn_br"],
        "W1": inputs["L0_ffn_W1"], "b1_cols": b1.reshape(b1.shape[0], -1, 128).transpose(0, 2, 1),
        "W2": inputs["L0_ffn_W2"], "b2": inputs["L0_ffn_b2"],
    }
    arrays, args = {}, []
    for name, value in given.items():
        a = _np.ascontiguousarray(value)
        arrays[f"in_{name}"] = a
        args.append(nc.dram_tensor(f"in_{name}", a.shape, _mybir.dt.from_np(a.dtype), kind="ExternalInput").ap())
    out = nc.dram_tensor("out", arrays["in_x"].shape, f32, kind="ExternalOutput").ap()
    gnn_moe(nc, *args, out)
    r = _run(nc, [arrays], core_ids=[0])
    return r.results[0]["out"]
```
